# Optimizing a Trainium2 kernel written in Bass

```python
import numpy as np
import jax
import jax.numpy as jnp

def _softmax(x, axis=-1):
    return jax.nn.softmax(x, axis=axis)

def _gelu(x):
    return jax.nn.gelu(x, approximate=True)

def _silu(x):
    return jax.nn.silu(x)

def _sigmoid(x):
    return jax.nn.sigmoid(x)

def _layernorm(x, axis=-1, eps=1e-05):
    m = jnp.mean(x, axis=axis, keepdims=True)
    v = jnp.var(x, axis=axis, keepdims=True)
    return (x - m) / jnp.sqrt(v + eps)

def _scatter_add(tgt, idx, src, axis=0):
    return tgt.at[idx].add(src)

def _segment_sum(src, seg, n):
    return jax.ops.segment_sum(src, seg, n)
kernel_name = 'mk_gps_d1_gnn_r16_ce721b'

def setup_inputs(seed: int=0):
    np.random.seed(seed)
    _w = jnp.asarray

    def _rec_inputs():
        import jax
        import jax.numpy as jnp
        _gk = jax.random.key(seed)
        x = -0.0001126 + 1 * jax.random.normal(jax.random.fold_in(_gk, 1), (3125, 768), jnp.float32)
        _s = jax.random.randint(jax.random.fold_in(_gk, 2), (25000,), 0, 3125, jnp.int32)
        _d = jax.random.randint(jax.random.fold_in(_gk, 3), (25000,), 0, 3125, jnp.int32)
        _loop = jnp.arange(3125, dtype=jnp.int32)
        src = jnp.concatenate([_s, _d, _loop])
        dst = jnp.concatenate([_d, _s, _loop])
        _o = jnp.argsort(dst, stable=True)
        src = src[_o]
        dst = dst[_o]
        return (x, src, dst)
    x, src, dst = _rec_inputs()

    def _L0_gnn_setup():
        import jax, jax.numpy as jnp
        import numpy as np
        N_NODES = 625
        N_EDGES = 10000
        NEG_SLOPE = 0.2

        def _gat_layer(x, src, dst, W, a_src, a_dst, bias, concat):
            N = x.shape[0]
            H, C = a_src.shape
            h = (x @ W).reshape(N, H, C)
            al_s = jnp.einsum('nhc,hc->nh', h, a_src)
            al_d = jnp.einsum('nhc,hc->nh', h, a_dst)
            e = jax.nn.leaky_relu(al_s[src] + al_d[dst], NEG_SLOPE)
            m = jax.ops.segment_max(e, dst, num_segments=N)
            ex = jnp.exp(e - m[dst])
            denom = jax.ops.segment_sum(ex, dst, num_segments=N)
            alpha = ex / (denom[dst] + 1e-16)
            msg = h[src] * alpha[:, :, None]
            out = jax.ops.segment_sum(msg, dst, num_segments=N)
            out = out.reshape(N, H * C) if concat else out.mean(axis=1)
            return out + bias
        key = jax.random.key(seed)
        ks = jax.random.split(key, 10)
        in_dim, hid, out_dim, heads = (768, 512, 768, 4)
        x = jax.random.normal(ks[0], (N_NODES, in_dim), dtype=jnp.float32)
        edge_index = jax.random.randint(ks[1], (2, N_EDGES), 0, N_NODES, dtype=jnp.int64)
        g = lambda k, shape, fan: jax.random.normal(k, shape, jnp.float32) / np.sqrt(fan)
        return {'x': x, 'edge_index': edge_index, 'W1': g(ks[2], (in_dim, heads * hid), in_dim), 'att_src1': g(ks[3], (heads, hid), hid), 'att_dst1': g(ks[4], (heads, hid), hid), 'b1': jnp.zeros((heads * hid,), jnp.float32), 'W2': g(ks[5], (heads * hid, out_dim), heads * hid), 'att_src2': g(ks[6], (1, out_dim), out_dim), 'att_dst2': g(ks[7], (1, out_dim), out_dim), 'b2': jnp.zeros((out_dim,), jnp.float32)}
    _L0_gnn_all = _L0_gnn_setup()
    _L0_gnn_in = {k: v for k, v in _L0_gnn_all.items() if k in ('W1', 'att_src1', 'att_dst1', 'b1', 'W2', 'att_src2', 'att_dst2', 'b2')}
    del _L0_gnn_all

    def _L0_mix_setup():
        import jax, jax.numpy as jnp
        import numpy as np
        NUM_HEADS = 12
        EPS = 0.0001

        def softmax_kernel(data, proj, is_query):
            d = data.shape[-1]
            data_normalizer = d ** (-0.25)
            ratio = proj.shape[0] ** (-0.5)
            data_dash = jnp.einsum('bhnd,md->bhnm', data_normalizer * data, proj)
            diag = jnp.sum(data * data, axis=-1, keepdims=True) * 0.5 * data_normalizer ** 2
            if is_query:
                m = jnp.max(data_dash, axis=-1, keepdims=True)
            else:
                m = jnp.max(data_dash, axis=(-3, -2, -1), keepdims=True)
            return ratio * (jnp.exp(data_dash - diag - m) + EPS)
        key = jax.random.key(seed)
        ks = jax.random.split(key, 5)
        B, N, C = (8, 256, 768)
        x = jax.random.normal(ks[0], (B, N, C), dtype=jnp.float32)
        w_qkv = jax.random.normal(ks[1], (3 * C, C), dtype=jnp.float32) * 0.02
        w_proj = jax.random.normal(ks[2], (C, C), dtype=jnp.float32) * 0.02
        b_proj = jnp.zeros((C,), dtype=jnp.float32)
        proj_mat = jax.random.normal(ks[3], (256, C // NUM_HEADS), dtype=jnp.float32)
        return {'x': x, 'w_qkv': w_qkv, 'w_proj': w_proj, 'b_proj': b_proj, 'proj_mat': proj_mat}
    _L0_mix_all = _L0_mix_setup()
    _L0_mix_in = {k: v for k, v in _L0_mix_all.items() if k in ('w_qkv', 'w_proj', 'b_proj', 'proj_mat')}
    del _L0_mix_all

    def _L0_ffn_setup():
        import jax, jax.numpy as jnp
        import numpy as np
        D_MODEL = 768
        D_HID = 192
        D_OUT = 768
        N_EXP = 8
        TOP_K = 2
        B, S = (2, 128)
        LN_EPS = 1e-05
        key = jax.random.key(seed)
        ks = jax.random.split(key, 10)
        sc_in = 1.0 / np.sqrt(D_MODEL)
        sc_hid = 1.0 / np.sqrt(D_HID)
        return {'x': jax.random.normal(ks[0], (B, S, D_MODEL), dtype=jnp.float32), 'Wr': jax.random.normal(ks[1], (D_MODEL, N_EXP), dtype=jnp.float32) * sc_in, 'br': jnp.zeros((N_EXP,), dtype=jnp.float32), 'W1': jax.random.normal(ks[2], (N_EXP, D_MODEL, D_HID), dtype=jnp.float32) * sc_in, 'b1': jnp.zeros((N_EXP, D_HID), dtype=jnp.float32), 'W2': jax.random.normal(ks[3], (N_EXP, D_HID, D_OUT), dtype=jnp.float32) * sc_hid, 'b2': jnp.zeros((N_EXP, D_OUT), dtype=jnp.float32), 'ln_g': jnp.ones((D_OUT,), dtype=jnp.float32), 'ln_b': jnp.zeros((D_OUT,), dtype=jnp.float32)}
    _L0_ffn_all = _L0_ffn_setup()
    _L0_ffn_in = {k: v for k, v in _L0_ffn_all.items() if k in ('Wr', 'br', 'W1', 'b1', 'W2', 'b2', 'ln_g', 'ln_b')}
    del _L0_ffn_all
    return {'x': x, 'src': src, 'dst': dst, 'L0_gnn_W1': _L0_gnn_in['W1'], 'L0_gnn_att_src1': _L0_gnn_in['att_src1'], 'L0_gnn_att_dst1': _L0_gnn_in['att_dst1'], 'L0_gnn_b1': _L0_gnn_in['b1'], 'L0_gnn_W2': _L0_gnn_in['W2'], 'L0_gnn_att_src2': _L0_gnn_in['att_src2'], 'L0_gnn_att_dst2': _L0_gnn_in['att_dst2'], 'L0_gnn_b2': _L0_gnn_in['b2'], 'L0_mix_w_qkv': _L0_mix_in['w_qkv'], 'L0_mix_w_proj': _L0_mix_in['w_proj'], 'L0_mix_b_proj': _L0_mix_in['b_proj'], 'L0_mix_proj_mat': _L0_mix_in['proj_mat'], 'L0_ffn_Wr': _L0_ffn_in['Wr'], 'L0_ffn_br': _L0_ffn_in['br'], 'L0_ffn_W1': _L0_ffn_in['W1'], 'L0_ffn_b1': _L0_ffn_in['b1'], 'L0_ffn_W2': _L0_ffn_in['W2'], 'L0_ffn_b2': _L0_ffn_in['b2'], 'L0_ffn_ln_g': _L0_ffn_in['ln_g'], 'L0_ffn_ln_b': _L0_ffn_in['ln_b']}

def reference(x, src, dst, L0_gnn_W1, L0_gnn_att_src1, L0_gnn_att_dst1, L0_gnn_b1, L0_gnn_W2, L0_gnn_att_src2, L0_gnn_att_dst2, L0_gnn_b2, L0_mix_w_qkv, L0_mix_w_proj, L0_mix_b_proj, L0_mix_proj_mat, L0_ffn_Wr, L0_ffn_br, L0_ffn_W1, L0_ffn_b1, L0_ffn_W2, L0_ffn_b2, L0_ffn_ln_g, L0_ffn_ln_b):
    import jax
    import jax.numpy as jnp

    def _L0_gnn_ref(x, edge_index, W1, att_src1, att_dst1, b1, W2, att_src2, att_dst2, b2):
        import jax, jax.numpy as jnp
        import numpy as np
        N_NODES = 625
        N_EDGES = 10000
        NEG_SLOPE = 0.2

        def _gat_layer(x, src, dst, W, a_src, a_dst, bias, concat):
            N = x.shape[0]
            H, C = a_src.shape
            h = (x @ W).reshape(N, H, C)
            al_s = jnp.einsum('nhc,hc->nh', h, a_src)
            al_d = jnp.einsum('nhc,hc->nh', h, a_dst)
            e = jax.nn.leaky_relu(al_s[src] + al_d[dst], NEG_SLOPE)
            m = jax.ops.segment_max(e, dst, num_segments=N)
            ex = jnp.exp(e - m[dst])
            denom = jax.ops.segment_sum(ex, dst, num_segments=N)
            alpha = ex / (denom[dst] + 1e-16)
            msg = h[src] * alpha[:, :, None]
            out = jax.ops.segment_sum(msg, dst, num_segments=N)
            out = out.reshape(N, H * C) if concat else out.mean(axis=1)
            return out + bias
        N = x.shape[0]
        loops = jnp.arange(N, dtype=edge_index.dtype)
        src = jnp.concatenate([edge_index[0], loops])
        dst = jnp.concatenate([edge_index[1], loops])
        h = jax.nn.elu(_gat_layer(x, src, dst, W1, att_src1, att_dst1, b1, concat=True))
        out = _gat_layer(h, src, dst, W2, att_src2, att_dst2, b2, concat=False)
        return out

    def _L0_mix_ref(x, w_qkv, w_proj, b_proj, proj_mat):
        import jax, jax.numpy as jnp
        import numpy as np
        NUM_HEADS = 12
        EPS = 0.0001

        def softmax_kernel(data, proj, is_query):
            d = data.shape[-1]
            data_normalizer = d ** (-0.25)
            ratio = proj.shape[0] ** (-0.5)
            data_dash = jnp.einsum('bhnd,md->bhnm', data_normalizer * data, proj)
            diag = jnp.sum(data * data, axis=-1, keepdims=True) * 0.5 * data_normalizer ** 2
            if is_query:
                m = jnp.max(data_dash, axis=-1, keepdims=True)
            else:
                m = jnp.max(data_dash, axis=(-3, -2, -1), keepdims=True)
            return ratio * (jnp.exp(data_dash - diag - m) + EPS)
        B, N, C = x.shape
        H = NUM_HEADS
        d = C // H
        qkv = (x @ w_qkv.T).reshape(B, N, 3, H, d).transpose(2, 0, 3, 1, 4)
        q, k, v = (qkv[0], qkv[1], qkv[2])
        q_prime = softmax_kernel(q, proj_mat, is_query=True)
        k_prime = softmax_kernel(k, proj_mat, is_query=False)
        k_sum = jnp.sum(k_prime, axis=-2)
        d_inv = 1.0 / jnp.einsum('bhnm,bhm->bhn', q_prime, k_sum)
        context = jnp.einsum('bhnm,bhnd->bhmd', k_prime, v)
        out = jnp.einsum('bhnm,bhmd,bhn->bhnd', q_prime, context, d_inv)
        out = out.transpose(0, 2, 1, 3).reshape(B, N, C)
        return out @ w_proj.T + b_proj

    def _L0_ffn_ref(x, Wr, br, W1, b1, W2, b2, ln_g, ln_b):
        import jax, jax.numpy as jnp
        import numpy as np
        D_MODEL = 768
        D_HID = 192
        D_OUT = 768
        N_EXP = 8
        TOP_K = 2
        B, S = (2, 128)
        LN_EPS = 1e-05
        logits = jnp.einsum('bsd,de->bse', x, Wr) + br
        probs = jax.nn.softmax(logits, axis=-1)
        top_vals, top_idx = jax.lax.top_k(probs, TOP_K)
        routing_weights = top_vals / jnp.sum(top_vals, axis=-1, keepdims=True)
        onehot = jax.nn.one_hot(top_idx, N_EXP, dtype=x.dtype)
        expert_weights = jnp.einsum('bsk,bske->bse', routing_weights, onehot)
        h = jax.nn.gelu(jnp.einsum('bsd,edh->besh', x, W1) + b1[None, :, None, :])
        y = jnp.einsum('besh,eho->beso', h, W2) + b2[None, :, None, :]
        out = jnp.einsum('beso,bse->bso', y, expert_weights)
        mu = jnp.mean(out, axis=-1, keepdims=True)
        var = jnp.mean(jnp.square(out - mu), axis=-1, keepdims=True)
        out = (out - mu) * jax.lax.rsqrt(var + LN_EPS) * ln_g + ln_b
        return out
    edge_index = jnp.stack([src, dst])
    xn = _layernorm(x, axis=-1)
    x = x + _L0_gnn_ref(xn, edge_index, L0_gnn_W1, L0_gnn_att_src1, L0_gnn_att_dst1, L0_gnn_b1, L0_gnn_W2, L0_gnn_att_src2, L0_gnn_att_dst2, L0_gnn_b2) + _L0_mix_ref(xn[None], L0_mix_w_qkv, L0_mix_w_proj, L0_mix_b_proj, L0_mix_proj_mat)[0]
    x = x + _L0_ffn_ref(_layernorm(x, axis=-1)[None], L0_ffn_Wr, L0_ffn_br, L0_ffn_W1, L0_ffn_b1, L0_ffn_W2, L0_ffn_b2, L0_ffn_ln_g, L0_ffn_ln_b)[0]
    return x

_drawn_inputs = setup_inputs


def setup_inputs(seed=0):
    import zlib

    import numpy as np

    out = dict(_drawn_inputs(seed))
    spreads = {'L0_gnn_b1': (0.0, 0.1),
     'L0_gnn_b2': (0.0, 0.1),
     'L0_mix_b_proj': (0.0, 0.1),
     'L0_ffn_br': (0.0, 0.1),
     'L0_ffn_b1': (0.0, 0.1),
     'L0_ffn_b2': (0.0, 0.1),
     'L0_ffn_ln_g': (1.0, 0.2),
     'L0_ffn_ln_b': (0.0, 0.1)}
    factors = {}
    for name, (base, spread) in spreads.items():
        noise = np.random.default_rng([zlib.crc32(name.encode()), seed]).standard_normal(out[name].shape)
        drawn = base * np.exp(spread * noise) if base else spread * noise
        out[name] = jnp.asarray(drawn.astype(out[name].dtype))
    for name, factor in factors.items():
        out[name] = (out[name] * factor).astype(out[name].dtype)
    return out
```

```python
from contextlib import ExitStack

import concourse.bass as bass
from concourse import mybir

F32 = mybir.dt.float32
F32R = mybir.dt.float32r
I32 = mybir.dt.int32
ALU = mybir.AluOpType
ACT = mybir.ActivationFunctionType
AX = mybir.AxisListType
P = 128

N = 3125
NT = (N + P - 1) // P
NP = NT * P
LAST = N - (NT - 1) * P
D = 768
KC = D // P
HEADS = 12
DH = D // HEADS
M = 256
VW = DH + 1
MIX_EPS = 1e-4
LN_EPS = 1e-5
GH = 4
GC = 512
HID = GH * GC
SLOPE = 0.2
TW = 32
TROW1 = D + 1 + 2 * GH
TROW2 = D + 3
NSTEP = (N + TW - 1) // TW
SLOTS = 5
CAP = SLOTS * P
BIG = 1.0e30
NEXP = 8
EP = 53760
EROOM = EP + CAP
DHID = 192


def tile_pairs(eng, step, tiles=NT):
    pairs = tiles // 2
    step(0, 0, True, False)
    step(0, 1, True, False)
    with eng.Fori(1, pairs) as p:
        step(p, 0, False, False)
        step(p, 1, False, False)
    step(pairs, 0, False, True)


def loads_ahead(eng, load, store):
    pairs = NT // 2
    load(0, 0, True, False)
    load(0, 1, True, False)
    store(0, 0, True, False)
    load(1, 0, False, False)
    store(0, 1, True, False)
    load(1, 1, False, False)
    with eng.Fori(1, pairs - 1) as p:
        store(p, 0, False, False)
        load(p + 1, 0, False, False)
        store(p, 1, False, False)
        load(p + 1, 1, False, False)
    store(pairs - 1, 0, False, False)
    load(pairs, 0, False, True)
    store(pairs - 1, 1, False, False)
    store(pairs, 0, False, True)


class Pool:

    def __init__(self, nc, tag):
        self.nc, self.tag, self.stack, self.sems, self.blk = nc, tag, ExitStack(), [], None

    def __enter__(self):
        return self

    def __exit__(self, *exc):
        if exc[0]:
            return
        if self.blk is not None:
            self.blk.close()
        if self.sems:
            nums = sorted(self.sems)
            starts = [n for n in nums if n - 1 not in nums]
            for first in starts:
                end = next(n for n in range(first, nums[-1] + 2) if n not in nums)
                self.nc.all_engine_barrier(sems_to_clear=range(first, end))
        self.stack.close()

    def sb(self, name, shape, dt=F32):
        return self.stack.enter_context(self.nc.sbuf_tensor(f"{self.tag}_{name}", shape, dt))

    def sb2(self, name, shape, dt=F32):
        return [self.sb(f"{name}{b}", shape, dt) for b in range(2)]

    def bank(self, name):
        return self.stack.enter_context(self.nc.psum_tensor(f"{self.tag}_{name}", [P, 512], F32))

    def sem(self, name):
        s = self.stack.enter_context(self.nc.semaphore(f"{self.tag}_{name}"))
        self.sems.append(s.num)
        return s

    def sem2(self, name):
        return [self.sem(f"{name}{b}") for b in range(2)]

    def block(self):
        self.blk = ExitStack()
        return self.blk.enter_context(self.nc.Block())


def product3(pe, out, x_hi, x_lo, w_hi, w_lo, last=True):
    n = len(x_hi)
    for k in range(n):
        pe.matmul(out, x_hi[k], w_hi[k], start=(k == 0), stop=False)
        pe.matmul(out, x_hi[k], w_lo[k], start=False, stop=False)
        mm = pe.matmul(out, x_lo[k], w_hi[k], start=False, stop=(last and k == n - 1))
    return mm


def group_heads(g):
    return 4 * (g // 2) + g % 2, 4 * (g // 2) + g % 2 + 2


def dash_pair(pe, banks, k_hi, k_lo, j, pj_h, pj_l, full):
    for i in range(2):
        for a, (x, w) in enumerate(((k_hi, pj_h), (k_hi, pj_l), (k_lo, pj_h))):
            for e in range(2):
                r = slice(e * DH, e * DH + DH)
                mm = pe.matmul(banks[e][:, M * i:M * i + M], x[r, j + i, :], w[r, :], start=(a == 0), stop=(a == 2))
                if i == 1 and a == 2:
                    mm.then_inc(full, 1)


def split_weights(nc, tag, jobs, width):
    with Pool(nc, tag) as s:
        stage = [s.sb(f"stage{b}", [P, width]) for b in range(3)]
        staged = [s.sem(f"staged{b}") for b in range(3)]
        hi_done, lo_done = s.sem("hi_done"), s.sem("lo_done")
        blk = s.block()

        @blk.sync
        def _(sp):
            for n, (src, hi, lo) in enumerate(jobs):
                if n >= 3:
                    sp.wait_ge(lo_done, n - 2)
                sp.dma_start(stage[n % 3][:, :src.shape[1]], src).then_inc(staged[n % 3], 16)

        @blk.scalar
        def _(act):
            for n, (src, hi, lo) in enumerate(jobs):
                act.wait_ge(staged[n % 3], 16 * (n // 3 + 1))
                act.activation(hi, stage[n % 3][:, :src.shape[1]], ACT.Copy).then_inc(hi_done, 1)

        @blk.vector
        def _(dve):
            for n, (src, hi, lo) in enumerate(jobs):
                dve.wait_ge(hi_done, n + 1)
                dve.tensor_tensor(lo, stage[n % 3][:, :src.shape[1]], hi.bitcast(F32),
                                  ALU.subtract).then_inc(lo_done, 1)


def layernorm_stats(dve, x, st, mv, stats_done, stats_seen, mean_done, t):
    for i in range(2):
        dve.bn_stats(st[:, i, :], x[:, i * (D // 2):(i + 1) * (D // 2)]).then_inc(stats_done, 1)
    dve.wait_ge(stats_done, t * 2 + 2)
    dve.sem_inc(stats_seen, 1)
    dve.bn_aggr(mv[:, :], st[:, :, :]).then_inc(mean_done, 1)


def layernorm_rstd(pool, mv, vps, rstd, ln_eps, minus_half, mean_done, vps_done, rstd_done, t):
    pool.wait_ge(mean_done, t + 1)
    pool.tensor_tensor(vps[:, :], mv[:, 1:2], ln_eps[:, :], ALU.add).then_inc(vps_done, 1)
    pool.wait_ge(vps_done, t + 1)
    pool.tensor_tensor(rstd[:, :], vps[:, :], minus_half[:, :], ALU.pow).then_inc(rstd_done, 1)


def logit_weights(nc, io, keep, w_hi, w_lo):
    with Pool(nc, "lw") as s:
        w1 = [s.sb(f"w1{b}", [P, HID]) for b in range(2)]
        att = s.sb("att", [P, 2, HID])
        junk = s.sb("junk", [P, GC])
        dots = s.sb("dots", [P, KC, 2 * GH])
        att_in, w1_in = s.sem("att_in"), s.sem2("w1_in")
        dot_done, split_done = s.sem("dot_done"), s.sem("split_done")
        blk = s.block()

        @blk.sync
        def _(sp):
            sp.dma_start(att[:, 0, :], io["asrc1"].partition_broadcast(P)).then_inc(att_in, 16)
            sp.dma_start(att[:, 1, :], io["adst1"].partition_broadcast(P)).then_inc(att_in, 16)
            for k in range(KC):
                if k >= 2:
                    sp.wait_ge(dot_done, (k - 1) * 2 * GH)
                sp.dma_start(w1[k % 2][:, :], io["W1"][k * P:(k + 1) * P, :]).then_inc(w1_in[k % 2], 16)

        @blk.vector
        def _(dve):
            dve.wait_ge(att_in, 32)
            n = 0
            for k in range(KC):
                dve.wait_ge(w1_in[k % 2], 16 * (k // 2 + 1))
                for side in range(2):
                    for h in range(GH):
                        if n:
                            dve.wait_ge(dot_done, n)
                        j = side * GH + h
                        dve.tensor_tensor_reduce(
                            junk[:, :], w1[k % 2][:, h * GC:(h + 1) * GC],
                            att[:, side, h * GC:(h + 1) * GC], 1.0, 0.0, ALU.mult, ALU.add,
                            dots[:, k, j:j + 1]).then_inc(dot_done, 1)
                        n += 1
            dve.wait_ge(dot_done, n)
            a = 3 * D
            dve.tensor_copy(w_hi[:, :, a:a + 2 * GH], dots[:, :, :]).then_inc(split_done, 1)
            dve.wait_ge(split_done, 1)
            dve.tensor_tensor(w_lo[:, :, a:a + 2 * GH], dots[:, :, :],
                              w_hi[:, :, a:a + 2 * GH].bitcast(F32), ALU.subtract).then_inc(split_done, 1)


def phase_a(nc, io, dram, keep):
    WA = 3 * D + 2 * GH
    with Pool(nc, "a") as s:
        w_hi, w_lo = s.sb("w_hi", [P, KC, WA], F32R), s.sb("w_lo", [P, KC, WA], F32R)
        logit_weights(nc, io, keep, w_hi, w_lo)
        split_weights(nc, "as", [(io["wqkvT"][k * P:(k + 1) * P, :], w_hi[:, k, 0:3 * D], w_lo[:, k, 0:3 * D])
                                 for k in range(KC)], 3 * D)
        ident = keep["ident"]
        x = s.sb2("x", [P, D])
        xn = s.sb2("xn", [P, D])
        xt_h, xt_l = s.sb2("xt_h", [P, KC, P], F32R), s.sb2("xt_l", [P, KC, P], F32R)
        qk = s.sb2("qk", [P, 2 * D])
        sq = s.sb("sq", [P, 2 * D])
        dsum = s.sb("dsum", [P, 2 * HEADS])
        v = s.sb2("v", [P, HEADS * VW])
        al = s.sb2("al", [P, 1 + 2 * GH])
        qt_h, qt_l = s.sb2("qt_h", [P, 2 * KC, P], F32R), s.sb2("qt_l", [P, 2 * KC, P], F32R)
        st, mv = s.sb("st", [P, 2, 6]), s.sb("mv", [P, 2])
        vps, rstd = s.sb("vps", [P, 1]), s.sb("rstd", [P, 1])
        bank = [s.bank(f"bank{i}") for i in range(8)]

        x_in = s.sem2("x_in")
        stats_done, stats_seen, mean_done = s.sem("stats_done"), s.sem("stats_seen"), s.sem("mean_done")
        vps_done, rstd_done, xn_done = s.sem("vps_done"), s.sem("rstd_done"), s.sem("xn_done")
        xt_full, hi_done, lo_done = s.sem("xt_full"), s.sem("xt_hi_done"), s.sem("xt_lo_done")
        gemm_full = s.sem("gemm_full")
        qk_done, v_done = s.sem("qk_done"), s.sem("v_done")
        qt_full, qhi_done, qlo_done = s.sem("qt_full"), s.sem("qt_hi_done"), s.sem("qt_lo_done")
        dash_full, kmax_done = s.sem("dash_full"), s.sem("kmax_done")
        sq_done, dsum_done, diag_done = s.sem("sq_done"), s.sem("dsum_done"), s.sem("diag_done")
        ones_set, kmax_set = s.sem("ones_set"), s.sem("kmax_set")
        xn_out, v_out, q_out = s.sem2("xn_out"), s.sem2("v_out"), s.sem2("q_out")
        blk = s.block()
        CH = [(0, 512), (512, 512), (1024, 512), (1536, 512), (2048, WA - 2048)]
        pj_h, pj_l = keep["pj_h"], keep["pj_l"]

        @blk.sync
        def _(sp):
            def load(p, b, first, last):
                r = sp.snap((p * 2 + b) * P) if not first else b * P
                if not first:
                    sp.wait_ge(xn_done, p * 2 + b - 1)
                sp.dma_start(x[b][:, :], io["x"][bass.ds(r, P), :]).then_inc(x_in[b], 16)

            def store(p, b, first, last):
                t = p * 2 + b
                r = sp.snap(t * P) if not first else t * P
                t4 = sp.snap(t * 4) if not first else t * 4
                tt = sp.snap(t) if not first else t
                sp.wait_ge(xn_done, t + 1)
                sp.dma_start(dram["tab1"][bass.ds(r, P), 0:D], xn[b][:, :]).then_inc(xn_out[b], 16)
                sp.wait_ge(v_done, t * 4 + 4)
                sp.dma_start(dram["vx"][bass.ds(r, P), :], v[b][:, :]).then_inc(v_out[b], 16)
                sp.dma_start(dram["tab1"][bass.ds(r, P), D:TROW1], al[b][:, :]).then_inc(v_out[b], 16)
                sp.dma_start(dram["ald1"][bass.ds(r, P), :], al[b][:, 1 + GH:]).then_inc(v_out[b], 16)
                sp.wait_ge(qhi_done, t * 4 + 4)
                sp.wait_ge(qlo_done, t * 4 + 4)
                for i, (hi, lo) in enumerate((("qt_h", "qt_l"), ("kt_h", "kt_l"))):
                    sp.dma_start(dram[hi][bass.ds(tt, 1), :, :].rearrange("a p n -> (a p) n"),
                                 qt_h[b][:, i * KC:(i + 1) * KC, :].rearrange("p k n -> p (k n)").bitcast(F32)).then_inc(q_out[b], 16)
                    sp.dma_start(dram[lo][bass.ds(tt, 1), :, :].rearrange("a p n -> (a p) n"),
                                 qt_l[b][:, i * KC:(i + 1) * KC, :].rearrange("p k n -> p (k n)").bitcast(F32)).then_inc(q_out[b], 16)

            loads_ahead(sp, load, store)
            for b, n in ((0, NT - NT // 2), (1, NT // 2)):
                sp.wait_ge(xn_out[b], 16 * n)
                sp.wait_ge(v_out[b], 48 * n)
                sp.wait_ge(q_out[b], 64 * n)

        @blk.vector
        def _(dve):
            dve.memset(keep["kmx"][:, :], -BIG).then_inc(kmax_set, 1)
            dve.wait_ge(kmax_set, 1)

            def norm(t, b, first):
                dve.wait_ge(x_in[b], t * 8 + (16 - 8 * b))
                dve.wait_ge(rstd_done, t)
                layernorm_stats(dve, x[b], st, mv, stats_done, stats_seen, mean_done, t)
                dve.wait_ge(rstd_done, t + 1)
                if not first:
                    dve.wait_ge(xn_out[b], t * 8 - 8 * b)
                    dve.wait_ge(xt_full, t * 2 - 2)
                dve.tensor_scalar(xn[b][:, :], x[b][:, :], mv[:, 0:1], rstd[:, 0:1],
                                  ALU.subtract, ALU.mult).then_inc(xn_done, 1)

            def xt_low(t, b, first):
                for g in range(2):
                    dve.wait_ge(hi_done, t * 2 + g + 1)
                    if not first:
                        dve.wait_ge(gemm_full, t * 5 - 5)
                    o = xt_l[b][:, 3 * g:3 * g + 3, :].rearrange("p k n -> p (k n)")
                    dve.tensor_tensor(o, bank[g][:, 0:384],
                                      xt_h[b][:, 3 * g:3 * g + 3, :].rearrange("p k n -> p (k n)").bitcast(F32),
                                      ALU.subtract).then_inc(lo_done, 1)

            def diag(t, b):
                dve.wait_ge(sq_done, t + 1)
                dve.wait_ge(diag_done, t)
                dve.tensor_reduce(dsum[:, :], sq[:, :].rearrange("p (h d) -> p h d", d=DH), AX.X,
                                  ALU.add).then_inc(dsum_done, 1)
                dve.wait_ge(dsum_done, t + 1)
                dve.tensor_scalar(keep["diag"][:, bass.ds(t * 2 * HEADS, 2 * HEADS)].rearrange("p (g e i) -> p g e i", e=2, i=2),
                                  dsum[:, :].rearrange("p (g i e) -> p g e i", i=2, e=2),
                                  -0.5 * DH ** -0.5, None, ALU.mult).then_inc(diag_done, 1)

            def key_max(t, last):
                rows = LAST if last else P
                for g in range(6):
                    dve.wait_ge(dash_full, t * 6 + g + 1)
                    dve.tensor_reduce(keep["kmx"][0:rows, bass.ds(t * 6 + g, 1)],
                                      bank[2 + g % 5][0:rows, :], AX.X, ALU.max).then_inc(kmax_done, 1)

            def qt_low(t, b, first):
                if not first:
                    dve.wait_ge(q_out[b], t * 32 - 32 * b)
                    dve.wait_ge(dash_full, t * 6 - 6)
                for g in range(4):
                    dve.wait_ge(qhi_done, t * 4 + g + 1)
                    o = slice(3 * g, 3 * g + 3)
                    dve.tensor_tensor(qt_l[b][:, o, :].rearrange("p k n -> p (k n)"), bank[[7, 0, 1, 7][g]][:, 0:384],
                                      qt_h[b][:, o, :].rearrange("p k n -> p (k n)").bitcast(F32),
                                      ALU.subtract).then_inc(qlo_done, 1)

            norm(0, 0, True)
            xt_low(0, 0, True)

            def step(p, b, first, last):
                t = p * 2 + b
                if not last:
                    norm(t + 1, 1 - b, first and b == 0)
                    xt_low(t + 1, 1 - b, first and b == 0)
                if not (first and b == 0):
                    key_max(t - 1, False)
                diag(t, b)
                qt_low(t, b, first)
            tile_pairs(dve, step)
            key_max(NT - 1, True)

        @blk.gpsimd
        def _(pool):
            for b in range(2):
                ones = v[b][:, :].rearrange("p (h d) -> p h d", d=VW)[:, :, DH:VW]
                pool.memset(ones, 1.0).then_inc(ones_set, 1)
                pool.memset(al[b][:, 0:1], 1.0).then_inc(ones_set, 1)

            def rstd_of(t):
                layernorm_rstd(pool, mv, vps, rstd, keep["ln_eps"], keep["minus_half"], mean_done, vps_done, rstd_done, t)

            def squares(t, b):
                pool.wait_ge(dsum_done, t)
                pool.wait_ge(qk_done, t * 3 + 3)
                pool.tensor_tensor(sq[:, :], qk[b][:, :], qk[b][:, :], ALU.mult).then_inc(sq_done, 1)

            rstd_of(0)

            def step(p, b, first, last):
                t = p * 2 + b
                if not last:
                    rstd_of(t + 1)
                squares(t, b)
                if last:
                    ones = v[b][:, :].rearrange("p (h d) -> p h d", d=VW)[:, :, DH:VW]
                    pool.wait_ge(v_out[0], 48 * (NT // 2))
                    pool.memset(ones, 0.0).then_inc(ones_set, 1)
                    pool.wait_ge(ones_set, 5)
                    pool.memset(ones[0:LAST], 1.0).then_inc(ones_set, 1)
            tile_pairs(pool, step)

        @blk.scalar
        def _(act):
            def xt_high(t, b, first):
                for g in range(2):
                    act.wait_ge(xt_full, t * 2 + g + 1)
                    if not first:
                        act.wait_ge(gemm_full, t * 5 - 5)
                    act.activation(xt_h[b][:, 3 * g:3 * g + 3, :].rearrange("p k n -> p (k n)"),
                                   bank[g][:, 0:384], ACT.Copy).then_inc(hi_done, 1)

            def step(p, b, first, last):
                t = p * 2 + b
                if not last:
                    xt_high(t + 1, 1 - b, first and b == 0)
                if not first:
                    act.wait_ge(sq_done, t - 1)
                    act.wait_ge(qt_full, t * 4 - 4)
                for c in range(3):
                    act.wait_ge(gemm_full, t * 5 + c + 1)
                    act.activation(qk[b][:, 512 * c:512 * c + 512], bank[2 + c][:, :], ACT.Copy).then_inc(qk_done, 1)
                if first:
                    act.wait_ge(ones_set, 4)
                else:
                    act.wait_ge(v_out[b], t * 24 - 24 * b)
                if last:
                    act.wait_ge(ones_set, 6)
                vh = v[b][:, :].rearrange("p (h d) -> p h d", d=VW)[:, :, 0:DH]
                act.wait_ge(gemm_full, t * 5 + 4)
                act.activation(vh[:, 0:8, :], bank[5][:, :].rearrange("p (h d) -> p h d", d=DH), ACT.Copy).then_inc(v_done, 1)
                act.wait_ge(gemm_full, t * 5 + 5)
                act.activation(vh[:, 8:12, :], bank[6][:, 0:256].rearrange("p (h d) -> p h d", d=DH), ACT.Copy).then_inc(v_done, 1)
                act.activation(al[b][:, 1:1 + GH], bank[6][:, 256:256 + GH], ACT.Copy).then_inc(v_done, 1)
                act.activation(al[b][:, 1 + GH:], bank[6][:, 256 + GH:256 + 2 * GH], ACT.Copy).then_inc(v_done, 1)
                if not first:
                    act.wait_ge(q_out[b], t * 32 - 32 * b)
                    act.wait_ge(dash_full, t * 6 - 6)
                for g in range(4):
                    act.wait_ge(qt_full, t * 4 + g + 1)
                    act.activation(qt_h[b][:, 3 * g:3 * g + 3, :].rearrange("p k n -> p (k n)"),
                                   bank[[7, 0, 1, 7][g]][:, 0:384], ACT.Copy).then_inc(qhi_done, 1)

            xt_high(0, 0, True)
            tile_pairs(act, step)

        @blk.tensor
        def _(pe):
            def x_transposes(t, b, first):
                pe.wait_ge(xn_done, t + 1)
                for g in range(2):
                    if not first:
                        pe.wait_ge(qlo_done, t * 4 - 8 + g + 2)
                    for i in range(3):
                        k = 3 * g + i
                        mm = pe.transpose(bank[g][:, P * i:P * i + P], xn[b][:, k * P:(k + 1) * P], ident[:, :])
                    mm.then_inc(xt_full, 1)

            def products(t, b, first):
                pe.wait_ge(lo_done, t * 2 + 2)
                if first and b == 1:
                    pe.wait_ge(qk_done, 3)
                    pe.wait_ge(v_done, 4)
                for c, (a, n) in enumerate(CH):
                    if not first:
                        pe.wait_ge(kmax_done, t * 6 - 12 + (6 if c == 0 else c + 1))
                    product3(pe, bank[2 + c][:, 0:n], [xt_h[b][:, k, :] for k in range(KC)],
                             [xt_l[b][:, k, :] for k in range(KC)],
                             [w_hi[:, k, a:a + n] for k in range(KC)],
                             [w_lo[:, k, a:a + n] for k in range(KC)]).then_inc(gemm_full, 1)

            def dash(t, b, gemm_tile):
                pe.wait_ge(qlo_done, t * 4 + 4)
                for g in range(6):
                    if g < 5 and gemm_tile is not None:
                        if g < 3:
                            pe.wait_ge(qk_done, gemm_tile * 3 + g + 1)
                        else:
                            pe.wait_ge(v_done, gemm_tile * 4 + (1 if g == 3 else 4))
                    elif g == 5:
                        pe.wait_ge(kmax_done, t * 6 + 1)
                    elif gemm_tile is None:
                        pe.wait_ge(kmax_done, t * 6 - 6 + (6 if g == 0 else g + 1))
                    if g % 2 == 1:
                        dash_pair(pe, (bank[1 + g], bank[2 + g % 5]), qt_h[b], qt_l[b], KC + g - 1, pj_h, pj_l, dash_full)

            def q_transposes(t, b, first, last):
                pe.wait_ge(qk_done, t * 3 + 3)
                for g in range(4):
                    if g == 0 and not (first and b == 0):
                        pe.wait_ge(qlo_done, t * 4)
                    if g in (1, 2) and not last:
                        pe.wait_ge(lo_done, t * 2 + 2 + g)
                    if g in (1, 2) and last:
                        pe.wait_ge(qlo_done, t * 4 - 2 + g - 1)
                    if g == 3:
                        pe.wait_ge(qlo_done, t * 4 + 1)
                    for i in range(3):
                        k = 3 * g + i
                        mm = pe.transpose(bank[[7, 0, 1, 7][g]][:, P * i:P * i + P], qk[b][:, k * P:(k + 1) * P],
                                          ident[:, :])
                    mm.then_inc(qt_full, 1)

            x_transposes(0, 0, True)

            def step(p, b, first, last):
                t = p * 2 + b
                products(t, b, first)
                if not last:
                    x_transposes(t + 1, 1 - b, first and b == 0)
                if not (first and b == 0):
                    dash(t - 1, 1 - b, t)
                q_transposes(t, b, first, last)
            tile_pairs(pe, step)
            dash(NT - 1, 0, None)


def global_key_max(nc, keep):
    with Pool(nc, "gm") as s:
        col, row, one = s.sb("col", [P, 1]), s.sb("row", [1, 1]), s.sb("one", [1, P])
        pt, pb = s.bank("pt"), s.bank("pb")
        col_done, turned, row_done, spread = s.sem("col_done"), s.sem("turned"), s.sem("row_done"), s.sem("spread")
        one_set, neg_done, bias_done = s.sem("one_set"), s.sem("neg_done"), s.sem("bias_done")
        blk = s.block()

        @blk.vector
        def _(dve):
            dve.memset(one[:, :], -1.0).then_inc(one_set, 1)
            dve.tensor_reduce(col[:, :], keep["kmx"][:, :], AX.X, ALU.max).then_inc(col_done, 1)
            dve.wait_ge(turned, 1)
            dve.tensor_reduce(row[:, :], pt[0:1, 0:P], AX.X, ALU.max).then_inc(row_done, 1)
            dve.wait_ge(spread, 1)
            dve.tensor_copy(keep["negm"][:, :], pb[:, 0:1]).then_inc(neg_done, 1)
            dve.wait_ge(neg_done, 1)
            kd = keep["diag"][:, :].rearrange("p (t s h) -> p t s h", s=2, h=HEADS)[:, :, 1, :]
            dve.tensor_scalar(keep["kbias"][:, :].rearrange("p (t h) -> p t h", h=HEADS), kd,
                              keep["negm"][:, 0:1], None, ALU.add).then_inc(bias_done, 1)

        @blk.tensor
        def _(pe):
            pe.wait_ge(col_done, 1)
            pe.transpose(pt[0:1, 0:P], col[:, :], keep["ident"][:, :]).then_inc(turned, 1)
            pe.wait_ge(row_done, 1)
            pe.wait_ge(one_set, 1)
            pe.matmul(pb[:, 0:1], one[0:1, :], row[0:1, 0:1], start=True, stop=True).then_inc(spread, 1)


def phase_b(nc, io, dram, keep):
    with Pool(nc, "b") as s:
        kt_h, kt_l = s.sb2("kt_h", [P, KC, P], F32R), s.sb2("kt_l", [P, KC, P], F32R)
        vx = s.sb2("vx", [P, HEADS * VW])
        kp = s.sb2("kp", [P, HEADS * M])
        zl, zr = s.sb("zl", [P, P]), s.sb("zr", [P, 512])
        dash = [s.bank(f"dash{i}") for i in range(4)]
        cacc = [s.bank(f"cacc{i}") for i in range(4)]
        kt_in, vx_in = s.sem2("kt_in"), s.sem2("vx_in")
        z_set, dash_full, exp_done, kp_done, ctx_done = (s.sem(n) for n in (
            "z_set", "dash_full", "exp_done", "kp_done", "ctx_done"))
        ctx_out = s.sem("ctx_out")
        blk = s.block()

        @blk.sync
        def _(sp):
            def step(p, b, first, last):
                t = p * 2 + b
                tt = sp.snap(t) if not first else t
                r = sp.snap(t * P) if not first else t * P
                if not first:
                    sp.wait_ge(dash_full, t * 6 - 6)
                sp.dma_start(kt_h[b][:, :, :].rearrange("p k n -> p (k n)").bitcast(F32),
                             dram["kt_h"][bass.ds(tt, 1), :, :].rearrange("a p n -> (a p) n")).then_inc(kt_in[b], 16)
                sp.dma_start(kt_l[b][:, :, :].rearrange("p k n -> p (k n)").bitcast(F32),
                             dram["kt_l"][bass.ds(tt, 1), :, :].rearrange("a p n -> (a p) n")).then_inc(kt_in[b], 16)
                if not first:
                    sp.wait_ge(ctx_done, t * 6 - 6)
                sp.dma_start(vx[b][:, :], dram["vx"][bass.ds(r, P), :]).then_inc(vx_in[b], 16)
            tile_pairs(sp, step)

        @blk.scalar
        def _(act):
            def step(p, b, first, last):
                t = p * 2 + b
                if not first:
                    act.wait_ge(ctx_done, t * 6 - 6)
                for g in range(6):
                    act.wait_ge(dash_full, t * 6 + g + 1)
                    for e in range(2):
                        h = 2 * g + e
                        act.activation(kp[b][:, h * M:(h + 1) * M], dash[(g + 2 * b) % 4][:, e * M:e * M + M],
                                       ACT.Exp, bias=keep["kbias"][:, bass.ds(t * HEADS + h, 1)]).then_inc(exp_done, 1)
            tile_pairs(act, step)

        @blk.vector
        def _(dve):
            dve.memset(zl[:, :], 0.0).then_inc(z_set, 1)
            dve.memset(zr[:, :], 0.0).then_inc(z_set, 1)

            def step(p, b, first, last):
                t = p * 2 + b
                for g in range(6):
                    dve.wait_ge(exp_done, t * 12 + 2 * g + 2)
                    kg = kp[b][:, 2 * g * M:2 * (g + 1) * M]
                    dve.tensor_scalar(kg, kg, MIX_EPS, None, ALU.add).then_inc(kp_done, 1)
            tile_pairs(dve, step)
            dve.wait_ge(ctx_done, NT * 6)
            for i in range(4):
                dve.tensor_copy(keep["ctx"][:, i * 6 * VW:(i + 1) * 6 * VW], cacc[i][:, 0:6 * VW]).then_inc(ctx_out, 1)

        @blk.tensor
        def _(pe):
            pe.wait_ge(z_set, 2)
            for i in range(4):
                pe.matmul(cacc[i][:, :], zl[:, :], zr[:, :], start=True, stop=True, skip_group_check=True)

            def dashes(t, b, g, first):
                if g == 0:
                    pe.wait_ge(kt_in[b], t * 16 + (32 - 16 * b))
                if not (first and g < 4):
                    pe.wait_ge(exp_done, t * 12 + 2 * g - 4)
                dash_pair(pe, [dash[(g + e + 2 * b) % 4] for e in range(2)], kt_h[b], kt_l[b], g,
                          keep["pj_h"], keep["pj_l"], dash_full)

            def contexts(t, b, g):
                if g == 0:
                    pe.wait_ge(vx_in[b], t * 8 + (16 - 8 * b))
                pe.wait_ge(kp_done, t * 6 + g + 1)
                for a, h in enumerate(group_heads(g)):
                    for m in range(2):
                        i = 2 * h + m
                        c = (2 * g + a) * M + m * P
                        mm = pe.matmul(cacc[i // 6][:, (i % 6) * VW:(i % 6 + 1) * VW], kp[b][:, c:c + P], vx[b][:, h * VW:(h + 1) * VW],
                                       start=False, stop=True, skip_group_check=True)
                mm.then_inc(ctx_done, 1)

            for g in (0, 2, 4):
                dashes(0, 0, g, True)

            def step(p, b, first, last):
                t = p * 2 + b
                for g in range(6):
                    contexts(t, b, g)
                    if not last and g % 2 == 0:
                        dashes(t + 1, 1 - b, g, False)
            tile_pairs(pe, step)


def setup(nc, io, keep, s):
    keep["ident"] = s.sb("ident", [P, P])
    keep["rows_in"] = [[s.stack.enter_context(nc.semaphore(f"rows_in{n}_{b}")) for b in range(4)] for n in range(2)]
    keep["rows_in_general"] = [s.stack.enter_context(nc.semaphore(f"rows_in_general{n}")) for n in range(2)]
    keep["minus_half"] = s.sb("minus_half", [P, 1])
    keep["ln_eps"] = s.sb("ln_eps", [P, 1])
    keep["minus_one"] = s.sb("minus_one", [P, 1])
    with Pool(nc, "st") as t:
        loaded, made = t.sem("loaded"), t.sem("made")
        blk = t.block()

        @blk.sync
        def _(sp):
            sp.dma_start(keep["ident"][:, :], io["ident"]).then_inc(loaded, 16)
            sp.wait_ge(loaded, 16)

        @blk.vector
        def _(dve):
            dve.memset(keep["minus_half"][:, :], -0.5).then_inc(made, 1)
            dve.memset(keep["ln_eps"][:, :], LN_EPS).then_inc(made, 1)
            dve.memset(keep["minus_one"][:, :], -1.0).then_inc(made, 1)


def setup_mix(nc, io, keep, s):
    keep["pj_h"], keep["pj_l"] = s.sb("pj_h", [P, M], F32R), s.sb("pj_l", [P, M], F32R)
    keep["kmx"] = s.sb("kmx", [P, NT * 6])
    keep["diag"] = s.sb("diag", [P, NT * 2 * HEADS])
    keep["negm"] = s.sb("negm", [P, 1])
    keep["kbias"] = s.sb("kbias", [P, NT * HEADS])
    keep["ctx"] = s.sb("ctx", [P, HEADS * 2 * VW])
    with Pool(nc, "sm") as t:
        raw, scaled = t.sb("raw", [P, M]), t.sb("scaled", [P, M])
        loaded, scale_done, hi_done, lo_done = (t.sem(n) for n in ("loaded", "scale_done", "hi_done", "lo_done"))
        blk = t.block()

        @blk.sync
        def _(sp):
            for e in range(2):
                sp.dma_start(raw[e * DH:(e + 1) * DH, :], io["projT"]).then_inc(loaded, 16)

        @blk.vector
        def _(dve):
            dve.wait_ge(loaded, 32)
            dve.tensor_scalar(scaled[:, :], raw[:, :], DH ** -0.25, None, ALU.mult).then_inc(scale_done, 1)
            dve.wait_ge(scale_done, 1)
            dve.tensor_copy(keep["pj_h"][:, :], scaled[:, :]).then_inc(hi_done, 1)
            dve.wait_ge(hi_done, 1)
            dve.tensor_tensor(keep["pj_l"][:, :], scaled[:, :], keep["pj_h"][:, :].bitcast(F32),
                              ALU.subtract).then_inc(lo_done, 1)


def phase_c(nc, io, dram, keep):
    with Pool(nc, "c") as s:
        w_hi, w_lo = s.sb("w_hi", [P, KC, D], F32R), s.sb("w_lo", [P, KC, D], F32R)
        split_weights(nc, "cs", [(io["wprojT"][k * P:(k + 1) * P, :], w_hi[:, k, :], w_lo[:, k, :])
                                 for k in range(KC)], D)
        ident, ctx = keep["ident"], keep["ctx"]
        qt_h, qt_l = s.sb2("qt_h", [P, KC, P], F32R), s.sb2("qt_l", [P, KC, P], F32R)
        qp = s.sb2("qp", [P, HEADS * M])
        qpt = s.sb2("qpt", [P, 4 * P])
        mx, nb = s.sb("mx", [P, 2]), s.sb2("nb", [P, HEADS])
        rden = s.sb("rden", [P, HEADS])
        att = s.sb2("att", [P, D])
        at_h, at_l = s.sb("at_h", [P, KC, P], F32R), s.sb("at_l", [P, KC, P], F32R)
        x = s.sb2("x", [P, D])
        res = s.sb2("res", [P, D])
        bias = s.sb("bias", [P, D])
        eps = s.sb("eps", [P, 1])
        dash = [s.bank(f"dash{i}") for i in range(2)]
        turn = [s.bank(f"turn{i}") for i in range(2)]
        num = [s.bank(f"num{i}") for i in range(2)]
        proj = [s.bank(f"proj{i}") for i in range(2)]

        bias_in, q_in, x_in, res_out = s.sem("bias_in"), s.sem2("q_in"), s.sem2("x_in"), s.sem2("res_out")
        (eps_set, dash_full, mx_done, nb_done, exp_done, turn_full, qpa_done, qpd_done, num_full, rden_done,
         att_done, atr_full, ahi_done, alo_done, proj_full, xb_done, res_done) = (s.sem(n) for n in (
             "eps_set", "dash_full", "mx_done", "nb_done", "exp_done", "turn_full", "qpa_done", "qpd_done",
             "num_full", "rden_done", "att_done", "atr_full", "ahi_done", "alo_done", "proj_full", "xb_done",
             "res_done"))
        blk = s.block()

        @blk.sync
        def _(sp):
            sp.dma_start(bias[:, :], io["bproj"].partition_broadcast(P)).then_inc(bias_in, 16)

            def load(p, b, first, last):
                t = p * 2 + b
                tt = sp.snap(t) if not first else t
                if not first:
                    sp.wait_ge(dash_full, t * 6 - 6)
                for i, (buf, src) in enumerate(((qt_h, "qt_h"), (qt_l, "qt_l"))):
                    sp.dma_start(buf[b][:, :, :].rearrange("p k n -> p (k n)").bitcast(F32),
                                 dram[src][bass.ds(tt, 1), :, :].rearrange("a p n -> (a p) n")).then_inc(q_in[b], 16)

            def load_x(p, b, first):
                t = p * 2 + b
                r = sp.snap(t * P) if not isinstance(p, int) else t * P
                if not first:
                    sp.wait_ge(res_done, t * 2 - 2)
                sp.dma_start(x[b][:, :], io["x"][bass.ds(r, P), :]).then_inc(x_in[b], 16)

            def store_res(p, b):
                t = p * 2 + b
                r = sp.snap(t * P) if not isinstance(p, int) else t * P
                sp.wait_ge(res_done, t * 2 + 2)
                sp.dma_start(dram["res"][bass.ds(r, P), :], res[b][:, :]).then_inc(res_out[b], 16)

            def store(p, b, first, last):
                if not last:
                    load_x(p if b == 0 else p + 1, 1 - b, first and b == 0)
                if not (first and b == 0):
                    store_res(p if b == 1 else p - 1, 1 - b)

            load_x(0, 0, True)
            loads_ahead(sp, load, store)
            store_res(NT // 2, 0)
            sp.wait_ge(res_out[0], 16 * (NT - NT // 2))
            sp.wait_ge(res_out[1], 16 * (NT // 2))

        @blk.gpsimd
        def _(pool):
            pool.memset(eps[:, :], MIX_EPS).then_inc(eps_set, 1)
            pool.wait_ge(bias_in, 16)

            def step(p, b, first, last):
                t = p * 2 + b
                pool.wait_ge(x_in[b], t * 8 + (16 - 8 * b))
                pool.tensor_tensor(x[b][:, :], x[b][:, :], bias[:, :], ALU.add).then_inc(xb_done, 1)
            tile_pairs(pool, step)

        @blk.scalar
        def _(act):
            def exps(t, b, g, first):
                act.wait_ge(nb_done, t * 6 + g + 1)
                if g == 0 and not first:
                    act.wait_ge(turn_full, t * 6 - 6)
                for h in (2 * g, 2 * g + 1):
                    act.activation(qp[b][:, h * M:(h + 1) * M], dash[g % 2][:, (h % 2) * M:(h % 2 + 1) * M], ACT.Exp,
                                   bias=nb[b][:, h:h + 1]).then_inc(exp_done, 1)

            def att_high(t):
                act.wait_ge(proj_full, t * 2)
                for g in range(2):
                    act.wait_ge(atr_full, t * 2 + g + 1)
                    act.activation(at_h[:, 3 * g:3 * g + 3, :].rearrange("p k n -> p (k n)"), proj[g][:, 0:384],
                                   ACT.Copy).then_inc(ahi_done, 1)

            act.wait_ge(eps_set, 1)
            for g in range(6):
                exps(0, 0, g, True)

            def step(p, b, first, last):
                t = p * 2 + b
                for g in range(6):
                    if not last:
                        exps(t + 1, 1 - b, g, first and b == 0)
                    if g % 2 == 0:
                        act.wait_ge(turn_full, t * 6 + g + 1)
                        if not (first and b == 0 and g < 2):
                            act.wait_ge(num_full, t * 6 + g - 1)
                        act.activation(qpt[0][:, :], turn[0][:, :], ACT.Identity, bias=eps[:, 0:1]).then_inc(qpa_done, 1)
                    if g == 2 and not (first and b == 0):
                        att_high(t - 1)
            tile_pairs(act, step)
            att_high(NT - 1)

        @blk.vector
        def _(dve):
            def maxima(t, b, g, first):
                dve.wait_ge(dash_full, t * 6 + g + 1)
                dve.wait_ge(nb_done, t * 6 + g)
                dve.tensor_reduce(mx[:, :], dash[g % 2][:, :].rearrange("p (e m) -> p e m", m=M), AX.X,
                                  ALU.max).then_inc(mx_done, 1)
                dve.wait_ge(mx_done, t * 6 + g + 1)
                if g == 0 and not first:
                    dve.wait_ge(exp_done, t * 12 - 12)
                dve.scalar_tensor_tensor(out=nb[b][:, 2 * g:2 * g + 2], in0=mx[:, :], scalar=-1.0,
                                         in1=keep["diag"][:, bass.ds(t * 2 * HEADS + 2 * g, 2)],
                                         op0=ALU.mult, op1=ALU.add).then_inc(nb_done, 1)

            def att_low(t):
                for g in range(2):
                    dve.wait_ge(ahi_done, t * 2 + g + 1)
                    dve.tensor_tensor(at_l[:, 3 * g:3 * g + 3, :].rearrange("p k n -> p (k n)"), proj[g][:, 0:384],
                                      at_h[:, 3 * g:3 * g + 3, :].rearrange("p k n -> p (k n)").bitcast(F32),
                                      ALU.subtract).then_inc(alo_done, 1)

            def residual(t, b, first):
                dve.wait_ge(xb_done, t + 1)
                if not first:
                    dve.wait_ge(res_out[b], t * 8 - 8 * b)
                for c in range(2):
                    dve.wait_ge(proj_full, t * 2 + c + 1)
                    o = slice(384 * c, 384 * c + 384)
                    dve.tensor_tensor(res[b][:, o], proj[c][:, 0:384], x[b][:, o], ALU.add).then_inc(res_done, 1)

            def divide(t, b, first):
                dve.wait_ge(num_full, t * 6 + 6)
                dve.wait_ge(att_done, t * 2)
                for i in range(2):
                    nv = num[i][:, 0:6 * VW].rearrange("p (h d) -> p h d", d=VW)
                    dve.reciprocal(rden[:, 6 * i:6 * i + 6].rearrange("p (h a) -> p h a", a=1), nv[:, :, DH:VW]).then_inc(rden_done, 1)
                dve.wait_ge(rden_done, t * 2 + 2)
                if not first:
                    dve.wait_ge(atr_full, t * 2 - 2)
                for i in range(2):
                    nv = num[i][:, 0:6 * VW].rearrange("p (h d) -> p h d", d=VW)
                    dve.tensor_tensor(att[b][:, 384 * i:384 * i + 384].rearrange("p (h d) -> p h d", d=DH), nv[:, :, 0:DH],
                                      rden[:, 6 * i:6 * i + 6].unsqueeze(2).to_broadcast([P, 6, DH]),
                                      ALU.mult).then_inc(att_done, 1)

            for g in range(6):
                maxima(0, 0, g, True)

            def step(p, b, first, last):
                t = p * 2 + b
                for g in range(6):
                    if not last:
                        maxima(t + 1, 1 - b, g, first and b == 0)
                    if g % 2 == 1:
                        dve.wait_ge(turn_full, t * 6 + g + 1)
                        if not (first and b == 0 and g < 2):
                            dve.wait_ge(num_full, t * 6 + g - 1)
                        dve.tensor_scalar(qpt[1][:, :], turn[1][:, :], MIX_EPS, None, ALU.add).then_inc(qpd_done, 1)
                    if g == 2 and not (first and b == 0):
                        att_low(t - 1)
                    if g == 5 and not (first and b == 0):
                        residual(t - 1, 1 - b, first)
                divide(t, b, first)
            tile_pairs(dve, step)
            att_low(NT - 1)
            residual(NT - 1, 0, False)

        @blk.tensor
        def _(pe):
            def dashes(t, b, g):
                if g == 0:
                    pe.wait_ge(q_in[b], t * 16 + (32 - 16 * b))
                dash_pair(pe, dash, qt_h[b], qt_l[b], g, keep["pj_h"], keep["pj_l"], dash_full)

            def turns(t, b, g, first):
                pe.wait_ge(exp_done, t * 12 + 2 * g + 2)
                if not (first and b == 0 and g < 2):
                    pe.wait_ge((qpa_done, qpd_done)[g % 2], t * 3 + g // 2)
                for i in range(4):
                    mm = pe.transpose(turn[g % 2][:, i * P:(i + 1) * P],
                                      qp[b][:, 2 * g * M + i * P:2 * g * M + (i + 1) * P], ident[:, :])
                mm.then_inc(turn_full, 1)

            def heads_out(t, b, g):
                pe.wait_ge((qpa_done, qpd_done)[g % 2], t * 3 + g // 2 + 1)
                if g == 0:
                    pe.wait_ge(att_done, t * 2)
                for a, h in enumerate(group_heads(g)):
                    for m in range(2):
                        c = (h % 6) * VW
                        mm = pe.matmul(num[h // 6][:, c:c + VW], qpt[g % 2][:, (2 * a + m) * P:(2 * a + m + 1) * P],
                                       ctx[:, (2 * h + m) * VW:(2 * h + m + 1) * VW], start=(m == 0), stop=(m == 1),
                                       skip_group_check=True)
                mm.then_inc(num_full, 1)

            def att_turns(t, b):
                for g in range(2):
                    pe.wait_ge(att_done, t * 2 + 2)
                    pe.wait_ge(res_done, t * 2)
                    for i in range(3):
                        k = 3 * g + i
                        mm = pe.transpose(proj[g][:, i * P:(i + 1) * P], att[b][:, k * P:(k + 1) * P], ident[:, :])
                    mm.then_inc(atr_full, 1)

            def project(t):
                pe.wait_ge(alo_done, t * 2 + 2)
                for c in range(2):
                    product3(pe, proj[c][:, 0:384], [at_h[:, k, :] for k in range(KC)],
                             [at_l[:, k, :] for k in range(KC)],
                             [w_hi[:, k, 384 * c:384 * c + 384] for k in range(KC)],
                             [w_lo[:, k, 384 * c:384 * c + 384] for k in range(KC)]).then_inc(proj_full, 1)

            for g in (0, 2, 4):
                if g:
                    pe.wait_ge(exp_done, 2 * g)
                dashes(0, 0, g)

            def step(p, b, first, last):
                t = p * 2 + b
                for g in range(6):
                    if not last and g % 2 == 0:
                        pe.wait_ge(exp_done, t * 12 + 2 * g + 12)
                        dashes(t + 1, 1 - b, g)
                    turns(t, b, g, first)
                    if g >= 1:
                        heads_out(t, b, g - 1)
                    if g == 2 and not (first and b == 0):
                        att_turns(t - 1, 1 - b)
                    if g == 4 and not (first and b == 0):
                        project(t - 1)
                heads_out(t, b, 5)
            tile_pairs(pe, step)
            att_turns(NT - 1, 0)
            project(NT - 1)


def step_quads(eng, step, quads=NT):
    for b in range(4):
        step(0, b, True, False)
    with eng.Fori(1, quads - 1) as q:
        for b in range(4):
            step(q, b, False, False)
    for b in range(4):
        step(quads - 1, b, False, True)


def phase_ranges(nc, io, dram, keep, s):
    NB = EP // 8
    keep["ranges"], keep["longest"] = s.sb("ranges", [1, 2 * P], I32), s.sb("longest", [1, 1], I32)
    with Pool(nc, "r") as t:
        d = t.sb("d", [120, EP // 120], I32)
        q = t.sb("q", [120, EP // 120], I32)
        blk_min, blk_max = t.sb("blk_min", [120, NB // 120]), t.sb("blk_max", [120, NB // 120])
        every_min, every_max = t.sb("every_min", [P, NB]), t.sb("every_max", [P, NB])
        ramps = t.sb("ramps", [P, 2, NB])
        hit = t.sb("hit", [P, NB])
        step_no, ends, span = t.sb("step_no", [P, 1]), t.sb("ends", [P, 2]), t.sb("span", [P, 1])
        ints = t.sb("ints", [P, 2], I32)
        span_row, span_max = t.sb("span_row", [1, P]), t.sb("span_max", [1, 1])
        d_in, c_in, blocks_out, blocks_in, ints_out, ints_in = (t.sem(n) for n in (
            "d_in", "c_in", "blocks_out", "blocks_in", "ints_out", "ints_in"))
        q_done, blk_done, hit_done, end_done, int_done, long_done = (t.sem(n) for n in (
            "q_done", "blk_done", "hit_done", "end_done", "int_done", "long_done"))
        blk = t.block()

        @blk.sync
        def _(sp):
            sp.dma_start(d[:, :], io["edges"][1, 0:EP].rearrange("(p c) -> p c", p=120)).then_inc(d_in, 16)
            sp.dma_start(ramps[:, :, :].rearrange("p s n -> p (s n)"),
                         io["block_ramps"].rearrange("s n -> (s n)").partition_broadcast(P)).then_inc(c_in, 16)
            sp.dma_start(step_no[:, :], io["steps"]).then_inc(c_in, 16)
            sp.wait_ge(blk_done, 2)
            sp.dma_start(dram["blocks"][0, :].rearrange("(p c) -> p c", p=120), blk_min[:, :]).then_inc(blocks_out, 16)
            sp.dma_start(dram["blocks"][1, :].rearrange("(p c) -> p c", p=120), blk_max[:, :]).then_inc(blocks_out, 16)
            sp.wait_ge(blocks_out, 32)
            sp.dma_start(every_min[:, :], dram["blocks"][0, :].partition_broadcast(P)).then_inc(blocks_in, 16)
            sp.dma_start(every_max[:, :], dram["blocks"][1, :].partition_broadcast(P)).then_inc(blocks_in, 16)
            sp.wait_ge(int_done, 3)
            sp.dma_start(dram["ranges"], ints[:, :]).then_inc(ints_out, 16)
            sp.dma_start(dram["spans"].rearrange("(p a) -> p a", a=1), span[:, :]).then_inc(ints_out, 16)
            sp.wait_ge(ints_out, 32)
            sp.dma_start(keep["ranges"][:, :], dram["ranges"].rearrange("(a p) c -> a (p c)", a=1)).then_inc(ints_in, 16)
            sp.dma_start(span_row[:, :], dram["spans"].rearrange("(a p) -> a p", a=1)).then_inc(ints_in, 16)
            sp.wait_ge(ints_in, 32)

        @blk.vector
        def _(dve):
            dve.wait_ge(d_in, 16)
            dve.tensor_scalar(q[:, :], d[:, :], 5, None, ALU.logical_shift_right).then_inc(q_done, 1)
            dve.wait_ge(q_done, 1)
            qb = q[:, :].rearrange("p (b e) -> p b e", e=8)
            dve.tensor_reduce(blk_min[:, :], qb, AX.X, ALU.min).then_inc(blk_done, 1)
            dve.tensor_reduce(blk_max[:, :], qb, AX.X, ALU.max).then_inc(blk_done, 1)
            dve.wait_ge(c_in, 32)
            dve.wait_ge(blocks_in, 32)
            for i in range(2):
                if i:
                    dve.wait_ge(end_done, 1)
                dve.scalar_tensor_tensor(out=hit[:, :], in0=every_min[:, :], scalar=step_no[:, 0:1],
                                         in1=ramps[:, i, :], op0=ALU.is_le, op1=ALU.mult).then_inc(hit_done, 1)
                dve.wait_ge(hit_done, 2 * i + 1)
                dve.scalar_tensor_tensor(out=hit[:, :], in0=every_max[:, :], scalar=step_no[:, 0:1],
                                         in1=hit[:, :], op0=ALU.is_ge, op1=ALU.mult).then_inc(hit_done, 1)
                dve.wait_ge(hit_done, 2 * i + 2)
                dve.tensor_reduce(ends[:, i:i + 1], hit[:, :], AX.X, ALU.max).then_inc(end_done, 1)
            dve.wait_ge(end_done, 2)
            dve.tensor_scalar(ints[:, 0:1], ends[:, 0:1], -8.0, 8.0 * NB, ALU.mult, ALU.add).then_inc(int_done, 1)
            dve.tensor_scalar(ints[:, 1:2], ends[:, 1:2], 8.0, None, ALU.mult).then_inc(int_done, 1)
            dve.tensor_tensor(span[:, :], ends[:, 0:1], ends[:, 1:2], ALU.add).then_inc(int_done, 1)
            dve.wait_ge(ints_in, 32)
            dve.tensor_reduce(span_max[:, :], span_row[:, :], AX.X, ALU.max).then_inc(long_done, 1)
            dve.wait_ge(long_done, 1)
            dve.tensor_scalar(keep["longest"][:, :], span_max[:, :], 8.0, -8.0 * NB, ALU.mult, ALU.add).then_inc(long_done, 1)


def aggregate(nc, io, dram, keep, layer):
    H = GH if layer == 1 else 1
    HD = H * TW
    TROW = TROW1 if layer == 1 else TROW2
    tab, ald_d = dram[f"tab{layer}"], dram[f"ald{layer}"]
    HALF = ((0, 384), (384, D + 1 - 384))
    with Pool(nc, f"e{layer}") as s:
        ids = s.sb("ids", [P, NP])
        pick = s.sb("pick", [P, 2 * GH])
        ones = s.sb("ones", [P, P])
        e = [s.sb(f"e{b}", [P, 2, SLOTS], I32) for b in range(4)]
        rows = [s.sb(f"rows{b}", [P, SLOTS, TROW]) for b in range(4)]
        ald = [s.sb(f"ald{b}", [P, HD]) for b in range(4)]
        own = [s.sb(f"own{b}", [HD, TROW]) for b in range(4)]
        mask, pen = s.sb("mask", [P, SLOTS, TW]), s.sb("pen", [P, SLOTS, TW])
        z = s.sb("z", [P, SLOTS, HD])
        zmax = s.sb("zmax", [P, HD])
        mcol, zs, zself, m2, dself = (s.sb(n, [HD, 1]) for n in ("mcol", "zs", "zself", "m2", "dself"))
        junk = s.sb("junk", [HD, 2 * GH])
        dg = s.sb("dg", [HD, HD])
        wt = s.sb2("wt", [P, SLOTS, HD])
        wself = s.sb2("wself", [HD, 1])
        acc = s.sb("acc", [HD, D + 1])
        den, rden = s.sb("den", [HD, 1]), s.sb("rden", [HD, 1])
        outb = s.sb2("outb", [HD, D])
        if layer == 2:
            bias = s.sb("bias", [TW, D])
            resb = s.sb2("resb", [TW, D])
        zt, mrow = s.bank("zt"), s.bank("mrow")
        num = [[s.bank(f"num{b}{i}") for i in range(2)] for b in range(2)]
        const_in = s.sem("const_in")
        e_in, ald_in, own_in = ([s.sem(f"{n}{b}") for b in range(4)] for n in ("e_in", "ald_in", "own_in"))
        rows_in = keep["rows_in"][layer - 1]
        stored, res_in = s.sem2("stored"), s.sem2("res_in")
        (load_go, ones_set, gather_go, mask_done, pen_done, z1_done, z2_done, z3_done, zmax_done, zt_full, mcol_done, zs_done,
         zself_done, m2_done, dg_done, dself_done, mrow_full, shift_done, wself_done, exp_done, num_full, acc_done,
         den_done, rden_done, out_done, resb_done) = (s.sem(n) for n in (
             "load_go", "ones_set", "gather_go", "mask_done", "pen_done", "z1_done", "z2_done", "z3_done", "zmax_done", "zt_full",
             "mcol_done", "zs_done", "zself_done", "m2_done", "dg_done", "dself_done", "mrow_full", "shift_done",
             "wself_done", "exp_done", "num_full", "acc_done", "den_done", "rden_done", "out_done", "resb_done"))
        blk = s.block()

        def fits(eng):
            return eng.value_load(keep["longest"][0:1, 0:1], min_val=0, max_val=2 * EP) <= CAP

        @blk.sync
        def _(sp):
            with sp.If(fits(sp)):
                sp.dma_start(ids[:, :], io["node_ids"].partition_broadcast(P)).then_inc(const_in, 16)
                sp.dma_start(pick[:, :], io["head_pick"]).then_inc(const_in, 16)
                if layer == 2:
                    sp.dma_start(bias[:, :], io["b2"].partition_broadcast(TW)).then_inc(const_in, 16)

                def step(q, b, first, last):
                    T = q * 4 + b
                    n0 = sp.snap(T * TW) if not first else T * TW
                    lo = sp.value_load(keep["ranges"][0:1, bass.ds(T * 2, 1)], min_val=0, max_val=EP)
                    if not first:
                        sp.wait_ge(num_full, T * 2 - 6)
                        sp.wait_ge(acc_done, T * 2 - 6)
                        sp.sem_inc(load_go, 1)
                    sp.dma_start(e[b][:, :, :], io["edges"][:, bass.ds(lo, CAP)].rearrange("s (p c) -> p s c", c=SLOTS)).then_inc(e_in[b], 16)
                    sp.dma_start(ald[b][:, :], ald_d[bass.ds(n0, TW), :].rearrange("d h -> (d h)").partition_broadcast(P)).then_inc(ald_in[b], 16)
                    for h in range(H):
                        sp.dma_start(own[b][h * TW:(h + 1) * TW, :], tab[bass.ds(n0, TW), :]).then_inc(own_in[b], 16)
                step_quads(sp, step)

        @blk.gpsimd
        def _(pool):
            with pool.If(fits(pool)):
                pool.memset(ones[:, :], 1.0).then_inc(ones_set, 1)
                if layer == 2:
                    pool.wait_ge(const_in, 48)

                def step(q, b, first, last):
                    T = q * 4 + b
                    pool.wait_ge(e_in[b], q * 16 + 16)
                    pool.sem_inc(gather_go, 1)
                    if not first:
                        pool.wait_ge(num_full, T * 2 - 6)
                        pool.sem_inc(gather_go, 1)
                    for c in range(SLOTS):
                        pool.indirect_dma_start(rows[b][:, c, :], None, tab,
                                                bass.IndirectOffsetOnAxis(ap=e[b][:, 0, c:c + 1], axis=0)).then_inc(rows_in[b], 16)
                    if layer == 2:
                        pool.wait_ge(res_in[b % 2], q * 32 + (16 + 16 * (b // 2)))
                        pool.tensor_tensor(resb[b % 2][:, :], resb[b % 2][:, :], bias[:, :], ALU.add).then_inc(resb_done, 1)
                step_quads(pool, step)

        @blk.vector
        def _(dve):
            with dve.If(fits(dve)):
                dve.wait_ge(const_in, 48 if layer == 2 else 32)

                def logits(q, b):
                    T = q * 4 + b
                    dve.wait_ge(rows_in[b], q * (16 * SLOTS) + 16 * SLOTS)
                    dve.wait_ge(ald_in[b], q * 16 + 16)
                    dve.wait_ge(pen_done, T)
                    dve.tensor_tensor(mask[:, :, :], e[b][:, 1, :].unsqueeze(2).to_broadcast([P, SLOTS, TW]),
                                      ids[:, bass.ds(T * TW, TW)].unsqueeze(1).to_broadcast([P, SLOTS, TW]),
                                      ALU.is_equal).then_inc(mask_done, 1)
                    dve.wait_ge(mask_done, T + 1)
                    dve.wait_ge(z1_done, T)
                    dve.tensor_scalar(pen[:, :, :], mask[:, :, :], BIG, -BIG, ALU.mult, ALU.add).then_inc(pen_done, 1)
                    dve.wait_ge(pen_done, T + 1)
                    dve.wait_ge(shift_done, T)
                    z4 = z[:, :, :].rearrange("p c (h d) -> p c h d", h=H)
                    dve.tensor_tensor(z4, rows[b][:, :, D + 1:D + 1 + H].unsqueeze(3).to_broadcast([P, SLOTS, H, TW]),
                                      pen[:, :, :].unsqueeze(2).to_broadcast([P, SLOTS, H, TW]), ALU.add).then_inc(z1_done, 1)
                    dve.wait_ge(z1_done, T + 1)
                    dve.tensor_tensor(z4, z4, ald[b][:, :].rearrange("p (d h) -> p h d", h=H).unsqueeze(1)
                                      .to_broadcast([P, SLOTS, H, TW]), ALU.add).then_inc(z2_done, 1)
                    dve.wait_ge(z2_done, T + 1)
                    zf = z[:, :, :].rearrange("p c n -> p (c n)")
                    dve.scalar_tensor_tensor(out=zf, in0=zf, scalar=SLOPE, in1=zf, op0=ALU.mult, op1=ALU.max).then_inc(z3_done, 1)
                    dve.wait_ge(z3_done, T + 1)
                    dve.wait_ge(zt_full, T)
                    dve.tensor_reduce(zmax[:, :], z[:, :, :].rearrange("p c n -> p n c"), AX.X, ALU.max).then_inc(zmax_done, 1)

                def weights(q, b, first):
                    T = q * 4 + b
                    dve.wait_ge(own_in[b], q * (16 * H) + 16 * H)
                    dve.wait_ge(zself_done, T)
                    if layer == 1:
                        dve.tensor_tensor_reduce(junk[:, :], own[b][:, D + 1:D + 1 + 2 * H], pick[:, :], 1.0, 0.0, ALU.mult,
                                                 ALU.add, zs[:, :]).then_inc(zs_done, 1)
                    else:
                        dve.tensor_tensor(zs[:, :], own[b][:, D + 1:D + 2], own[b][:, D + 2:D + 3], ALU.add).then_inc(zs_done, 1)
                    dve.wait_ge(zs_done, T + 1)
                    dve.wait_ge(dself_done, T)
                    dve.scalar_tensor_tensor(out=zself[:, :], in0=zs[:, :], scalar=SLOPE, in1=zs[:, :], op0=ALU.mult,
                                             op1=ALU.max).then_inc(zself_done, 1)
                    dve.wait_ge(zt_full, T + 1)
                    dve.tensor_reduce(mcol[:, :], zt[0:HD, 0:P], AX.X, ALU.max).then_inc(mcol_done, 1)
                    dve.wait_ge(mcol_done, T + 1)
                    dve.wait_ge(zself_done, T + 1)
                    dve.wait_ge(dg_done, T)
                    dve.tensor_tensor(m2[:, :], mcol[:, :], zself[:, :], ALU.max).then_inc(m2_done, 1)
                    dve.wait_ge(m2_done, T + 1)
                    dve.wait_ge(mrow_full, T)
                    dve.tensor_scalar(dg[:, :], keep["ident"][0:HD, 0:HD], m2[:, 0:1], None, ALU.mult).then_inc(dg_done, 1)
                    dve.wait_ge(wself_done, T)
                    dve.tensor_tensor(dself[:, :], zself[:, :], m2[:, :], ALU.subtract).then_inc(dself_done, 1)
                    dve.wait_ge(mrow_full, T + 1)
                    if not first or b >= 2:
                        dve.wait_ge(num_full, T * 2 - 2)
                    dve.tensor_tensor(wt[b % 2][:, :, :], z[:, :, :], mrow[:, 0:HD].unsqueeze(1).to_broadcast([P, SLOTS, HD]),
                                      ALU.subtract).then_inc(shift_done, 1)

                def sums(q, b, first):
                    T = q * 4 + b
                    dve.wait_ge(wself_done, T + 1)
                    dve.wait_ge(out_done, T)
                    for i, (a, n) in enumerate(HALF):
                        dve.wait_ge(num_full, T * 2 + i + 1)
                        dve.scalar_tensor_tensor(out=acc[:, a:a + n], in0=own[b][:, a:a + n], scalar=wself[b % 2][:, 0:1],
                                                 in1=num[b % 2][i][0:HD, 0:n], op0=ALU.mult, op1=ALU.add).then_inc(acc_done, 1)
                    dve.wait_ge(acc_done, T * 2 + 2)
                    dve.tensor_scalar(den[:, :], acc[:, D:D + 1], 1e-16, None, ALU.add).then_inc(den_done, 1)
                    dve.wait_ge(den_done, T + 1)
                    dve.reciprocal(rden[:, :], den[:, :]).then_inc(rden_done, 1)
                    if layer == 2:
                        dve.wait_ge(rden_done, T + 1)
                        dve.wait_ge(resb_done, T + 1)
                        if not first or b >= 2:
                            dve.wait_ge(stored[b % 2], q * 32 + 16 * (b // 2))
                        dve.scalar_tensor_tensor(out=outb[b % 2][:, :], in0=acc[:, 0:D], scalar=rden[:, 0:1],
                                                 in1=resb[b % 2][:, :], op0=ALU.mult, op1=ALU.add).then_inc(out_done, 1)

                logits(0, 0)
                weights(0, 0, True)

                def step(q, b, first, last):
                    q1, b1 = (q, b + 1) if b < 3 else (q + 1, 0)
                    if not (last and b == 3):
                        logits(q1, b1)
                        weights(q1, b1, first and b < 3)
                    sums(q, b, first)
                step_quads(dve, step)

        @blk.scalar
        def _(act):
            with act.If(fits(act)):
                def exps(q, b):
                    T = q * 4 + b
                    act.wait_ge(dself_done, T + 1)
                    if isinstance(q, int) and q == 0 and b < 2:
                        pass
                    else:
                        act.wait_ge(acc_done, T * 2 - 2)
                    act.activation(wself[b % 2][:, :], dself[:, :], ACT.Exp).then_inc(wself_done, 1)
                    act.wait_ge(shift_done, T + 1)
                    for c in range(SLOTS):
                        act.activation(wt[b % 2][:, c, :], wt[b % 2][:, c, :], ACT.Exp).then_inc(exp_done, 1)

                exps(0, 0)

                def step(q, b, first, last):
                    T = q * 4 + b
                    n0 = act.snap(T * TW) if not first else T * TW
                    q1, b1 = (q, b + 1) if b < 3 else (q + 1, 0)
                    if not (last and b == 3):
                        exps(q1, b1)
                    if layer == 2 and not (last and b >= 2):
                        n2 = act.snap((T + 2) * TW) if not first else (T + 2) * TW
                        act.wait_ge(out_done, T + 1)
                        act.dma_start(resb[b % 2][:, :], dram["res"][bass.ds(n2, TW), :]).then_inc(res_in[b % 2], 16)
                    if layer == 1:
                        act.wait_ge(rden_done, T + 1)
                        if not first or b >= 2:
                            act.wait_ge(stored[b % 2], q * (64 * 2) + 64 * (b // 2))
                        act.activation(outb[b % 2][:, :], acc[:, 0:D], ACT.Copy, scale=rden[:, 0:1]).then_inc(out_done, 1)
                    act.wait_ge(out_done, T + 1)
                    if layer == 1:
                        for h in range(H):
                            act.dma_start(dram["agg1"][h, bass.ds(n0, TW), :], outb[b % 2][h * TW:(h + 1) * TW, :]).then_inc(stored[b % 2], 16)
                    else:
                        act.dma_start(dram["x2"][bass.ds(n0, TW), :], outb[b % 2][:, :]).then_inc(stored[b % 2], 16)
                if layer == 2:
                    for b in range(2):
                        act.dma_start(resb[b][:, :], dram["res"][b * TW:(b + 1) * TW, :]).then_inc(res_in[b], 16)
                step_quads(act, step)
                for b in range(2):
                    act.wait_ge(stored[b], 16 * H * 2 * NT)

        @blk.tensor
        def _(pe):
            with pe.If(fits(pe)):
                def turn(q, b):
                    T = q * 4 + b
                    pe.wait_ge(zmax_done, T + 1)
                    pe.wait_ge(mcol_done, T)
                    pe.transpose(zt[0:HD, 0:P], zmax[:, :], keep["ident"][:, :]).then_inc(zt_full, 1)

                def spread(q, b):
                    T = q * 4 + b
                    pe.wait_ge(dg_done, T + 1)
                    pe.wait_ge(shift_done, T)
                    pe.matmul(mrow[:, 0:HD], ones[0:HD, :], dg[:, :], start=True, stop=True).then_inc(mrow_full, 1)

                def sum_slot(q, b, c, first):
                    T = q * 4 + b
                    pe.wait_ge(exp_done, T * SLOTS + c + 1)
                    if c == 0 and (not first or b >= 2):
                        pe.wait_ge(acc_done, T * 2 - 2)
                    for i, (a, n) in enumerate(HALF):
                        mm = pe.matmul(num[b % 2][i][0:HD, 0:n], wt[b % 2][:, c, :], rows[b][:, c, a:a + n], start=(c == 0),
                                       stop=(c == SLOTS - 1))
                        if c == SLOTS - 1:
                            mm.then_inc(num_full, 1)

                pe.wait_ge(ones_set, 1)
                turn(0, 0)
                spread(0, 0)

                def step(q, b, first, last):
                    q1, b1 = (q, b + 1) if b < 3 else (q + 1, 0)
                    for c in range(SLOTS):
                        sum_slot(q, b, c, first)
                        if c == 2 and not (last and b == 3):
                            turn(q1, b1)
                        if c == 3 and not (last and b == 3):
                            spread(q1, b1)
                step_quads(pe, step)


def phase_f(nc, io, dram, keep):
    with Pool(nc, "f") as s:
        w_hi, w_lo = s.sb("w_hi", [P, KC, HID], F32R), s.sb("w_lo", [P, KC, HID], F32R)
        split_weights(nc, "fs", [(io["W1"][k * P:(k + 1) * P, :], w_hi[:, k, :], w_lo[:, k, :]) for k in range(KC)], HID)
        ident = keep["ident"]
        NK = GH * KC
        a_in = s.sb2("a_in", [P, GH, D])
        a_h, a_l = s.sb2("a_h", [P, NK, P], F32R), s.sb2("a_l", [P, NK, P], F32R)
        b1p = s.sb("b1p", [P, HID])
        r1 = s.sb("r1", [P, HID])
        e = s.sb2("e", [P, HID])
        turn = [s.bank(f"turn{i}") for i in range(4)]
        prod = [s.bank(f"prod{i}") for i in range(GH)]
        b_in, in_sem, out_sem = s.sem("b_in"), s.sem2("in"), s.sem2("out")
        bias_done, turn_full, hi_done, lo_done, prod_full, r1_done, exp_done, elu_done = (s.sem(n) for n in (
            "bias_done", "turn_full", "hi_done", "lo_done", "prod_full", "r1_done", "exp_done", "elu_done"))
        blk = s.block()

        @blk.sync
        def _(sp):
            sp.dma_start(b1p[:, :], io["b1"].partition_broadcast(P)).then_inc(b_in, 16)

            def load(p, b, first, last):
                t = p * 2 + b
                r = sp.snap(t * P) if not first else t * P
                if not first:
                    sp.wait_ge(turn_full, t * 8 - 8)
                sp.dma_start(a_in[b][:, :, :], dram["agg1"][:, bass.ds(r, P), :].rearrange("h p n -> p h n")).then_inc(in_sem[b], 16)

            def store(p, b, first, last):
                t = p * 2 + b
                r = sp.snap(t * P) if not first else t * P
                sp.wait_ge(elu_done, t * 4 + 4)
                sp.dma_start(dram["h1"][bass.ds(r, P), :], e[b][:, :]).then_inc(out_sem[b], 16)
            loads_ahead(sp, load, store)
            sp.wait_ge(out_sem[0], 16 * (NT - NT // 2))
            sp.wait_ge(out_sem[1], 16 * (NT // 2))

        @blk.scalar
        def _(act):
            def high(t, b, g, first):
                act.wait_ge(turn_full, t * 8 + g + 1)
                if g == 0 and not first:
                    act.wait_ge(prod_full, t * 4 - 4)
                act.activation(a_h[b][:, 3 * g:3 * g + 3, :].rearrange("p k n -> p (k n)"), turn[g % 4][:, 0:384],
                               ACT.Copy).then_inc(hi_done, 1)

            for g in range(8):
                high(0, 0, g, True)

            def step(p, b, first, last):
                t = p * 2 + b
                for h in range(GH):
                    if not last:
                        high(t + 1, 1 - b, 2 * h, first and b == 0)
                        high(t + 1, 1 - b, 2 * h + 1, first and b == 0)
                    act.wait_ge(r1_done, t * 4 + h + 1)
                    if h == 0 and not first:
                        act.wait_ge(out_sem[b], t * 8 - 8 * b)
                    c = slice(h * GC, (h + 1) * GC)
                    act.activation(e[b][:, c], r1[:, c], ACT.Exp, bias=keep["minus_one"][:, 0:1]).then_inc(exp_done, 1)
            tile_pairs(act, step)

        @blk.vector
        def _(dve):
            def low(t, b, g):
                dve.wait_ge(hi_done, t * 8 + g + 1)
                o = a_h[b][:, 3 * g:3 * g + 3, :].rearrange("p k n -> p (k n)")
                dve.tensor_tensor(a_l[b][:, 3 * g:3 * g + 3, :].rearrange("p k n -> p (k n)"), turn[g % 4][:, 0:384],
                                  o.bitcast(F32), ALU.subtract).then_inc(lo_done, 1)

            def elu(t, b, h):
                c = slice(h * GC, (h + 1) * GC)
                dve.wait_ge(exp_done, t * 4 + h + 1)
                dve.scalar_tensor_tensor(out=e[b][:, c], in0=e[b][:, c], scalar=1.0, in1=r1[:, c], op0=ALU.min,
                                         op1=ALU.max).then_inc(elu_done, 1)

            dve.wait_ge(b_in, 16)
            dve.tensor_scalar(b1p[:, :], b1p[:, :], 1.0, None, ALU.add).then_inc(bias_done, 1)
            dve.wait_ge(bias_done, 1)
            for g in range(8):
                low(0, 0, g)

            def step(p, b, first, last):
                t = p * 2 + b
                for h in range(GH):
                    c = slice(h * GC, (h + 1) * GC)
                    if not last:
                        low(t + 1, 1 - b, 2 * h)
                    dve.wait_ge(prod_full, t * 4 + h + 1)
                    if not (first and b == 0):
                        dve.wait_ge(elu_done, t * 4 + h - 3)
                    dve.tensor_tensor(r1[:, c], prod[h][:, :], b1p[:, c], ALU.add).then_inc(r1_done, 1)
                    if not last:
                        low(t + 1, 1 - b, 2 * h + 1)
                    if h:
                        elu(t, b, h - 1)
                elu(t, b, GH - 1)
            tile_pairs(dve, step)

        @blk.tensor
        def _(pe):
            def turns(t, b, g, first):
                if g == 0:
                    pe.wait_ge(in_sem[b], t * 8 + (16 - 8 * b))
                if not (first and g < 4):
                    pe.wait_ge(lo_done, t * 8 + g - 3)
                for i in range(3):
                    k = 3 * g + i
                    mm = pe.transpose(turn[g % 4][:, i * P:(i + 1) * P],
                                      a_in[b][:, k // KC, (k % KC) * P:(k % KC + 1) * P], ident[:, :])
                mm.then_inc(turn_full, 1)

            for g in range(8):
                turns(0, 0, g, True)

            def step(p, b, first, last):
                t = p * 2 + b
                for h in range(GH):
                    pe.wait_ge(lo_done, t * 8 + 2 * h + 2)
                    if not (first and b == 0):
                        pe.wait_ge(r1_done, t * 4 + h - 3)
                    ks = range(KC)
                    product3(pe, prod[h][:, :], [a_h[b][:, h * KC + k, :] for k in ks], [a_l[b][:, h * KC + k, :] for k in ks],
                             [w_hi[:, k, h * GC:(h + 1) * GC] for k in ks],
                             [w_lo[:, k, h * GC:(h + 1) * GC] for k in ks]).then_inc(prod_full, 1)
                    if not last:
                        turns(t + 1, 1 - b, 2 * h, False)
                        turns(t + 1, 1 - b, 2 * h + 1, False)
            tile_pairs(pe, step)


def phase_g(nc, io, dram, keep):
    NK = HID // P
    with Pool(nc, "g") as s:
        w_hi, w_lo = s.sb("w_hi", [P, NK, D], F32R), s.sb("w_lo", [P, NK, D], F32R)
        split_weights(nc, "gs", [(io["W2"][k * P:(k + 1) * P, :], w_hi[:, k, :], w_lo[:, k, :]) for k in range(NK)], D)
        h = s.sb2("h", [P, HID])
        h_h, h_l = s.sb2("h_h", [P, NK, P], F32R), s.sb2("h_l", [P, NK, P], F32R)
        row = s.sb2("row", [P, TROW2])
        a2 = s.sb("a2", [P, 2, D])
        junk = s.sb("junk", [P, D])
        turn = [s.bank(f"turn{i}") for i in range(4)]
        prod = [s.bank(f"prod{i}") for i in range(2)]
        a_in, in_sem, out_sem = s.sem("a_in"), s.sem2("in"), s.sem2("out")
        ones_set, turn_full, hi_done, lo_done, prod_full, row_done, dot_done = (s.sem(n) for n in (
            "ones_set", "turn_full", "hi_done", "lo_done", "prod_full", "row_done", "dot_done"))
        blk = s.block()

        @blk.sync
        def _(sp):
            for i, n in enumerate(("asrc2", "adst2")):
                sp.dma_start(a2[:, i, :], io[n].partition_broadcast(P)).then_inc(a_in, 16)

            def load(p, b, first, last):
                t = p * 2 + b
                r = sp.snap(t * P) if not first else t * P
                if not first:
                    sp.wait_ge(turn_full, t * 4 - 4)
                sp.dma_start(h[b][:, :], dram["h1"][bass.ds(r, P), :]).then_inc(in_sem[b], 16)

            def store(p, b, first, last):
                t = p * 2 + b
                r = sp.snap(t * P) if not first else t * P
                sp.wait_ge(dot_done, t * 2 + 2)
                sp.dma_start(dram["tab2"][bass.ds(r, P), :], row[b][:, :]).then_inc(out_sem[b], 16)
                sp.dma_start(dram["ald2"][bass.ds(r, P), :], row[b][:, D + 2:D + 3]).then_inc(out_sem[b], 16)
            loads_ahead(sp, load, store)
            sp.wait_ge(out_sem[0], 32 * (NT - NT // 2))
            sp.wait_ge(out_sem[1], 32 * (NT // 2))

        @blk.gpsimd
        def _(pool):
            for b in range(2):
                pool.memset(row[b][:, D:D + 1], 1.0).then_inc(ones_set, 1)

        @blk.scalar
        def _(act):
            def high(t, b, g, first):
                act.wait_ge(turn_full, t * 4 + g + 1)
                if g == 0 and not first:
                    act.wait_ge(prod_full, t * 2 - 2)
                act.activation(h_h[b][:, 4 * g:4 * g + 4, :].rearrange("p k n -> p (k n)"), turn[g][:, :], ACT.Identity,
                               bias=keep["minus_one"][:, 0:1]).then_inc(hi_done, 1)

            for g in range(4):
                high(0, 0, g, True)

            def step(p, b, first, last):
                t = p * 2 + b
                for c in range(2):
                    if not last:
                        high(t + 1, 1 - b, 2 * c, first and b == 0)
                        high(t + 1, 1 - b, 2 * c + 1, first and b == 0)
                    if c == 0 and not first:
                        act.wait_ge(out_sem[b], t * 16 - 16 * b)
                    act.wait_ge(prod_full, t * 2 + c + 1)
                    act.activation(row[b][:, 384 * c:384 * c + 384], prod[c][:, 0:384], ACT.Copy).then_inc(row_done, 1)
            tile_pairs(act, step)

        @blk.vector
        def _(dve):
            def low(t, b, g):
                dve.wait_ge(hi_done, t * 4 + g + 1)
                o = h_h[b][:, 4 * g:4 * g + 4, :].rearrange("p k n -> p (k n)")
                dve.scalar_tensor_tensor(out=h_l[b][:, 4 * g:4 * g + 4, :].rearrange("p k n -> p (k n)"), in0=turn[g][:, :],
                                         scalar=-1.0, in1=o.bitcast(F32), op0=ALU.add, op1=ALU.subtract).then_inc(lo_done, 1)

            dve.wait_ge(a_in, 32)
            dve.wait_ge(ones_set, 2)
            for g in range(4):
                low(0, 0, g)

            def step(p, b, first, last):
                t = p * 2 + b
                if not last:
                    for g in range(4):
                        low(t + 1, 1 - b, g)
                dve.wait_ge(row_done, t * 2 + 2)
                for i in range(2):
                    dve.wait_ge(dot_done, t * 2 + i)
                    dve.tensor_tensor_reduce(junk[:, :], row[b][:, 0:D], a2[:, i, :], 1.0, 0.0, ALU.mult, ALU.add,
                                             row[b][:, D + 1 + i:D + 2 + i]).then_inc(dot_done, 1)
            tile_pairs(dve, step)

        @blk.tensor
        def _(pe):
            def turns(t, b, g, first):
                if g == 0:
                    pe.wait_ge(in_sem[b], t * 8 + (16 - 8 * b))
                if not first:
                    pe.wait_ge(lo_done, t * 4 + g - 3)
                for i in range(4):
                    k = 4 * g + i
                    mm = pe.transpose(turn[g][:, i * P:(i + 1) * P], h[b][:, k * P:(k + 1) * P], keep["ident"][:, :])
                mm.then_inc(turn_full, 1)

            for g in range(4):
                turns(0, 0, g, True)

            def step(p, b, first, last):
                t = p * 2 + b
                pe.wait_ge(lo_done, t * 4 + 4)
                for c in range(2):
                    if not (first and b == 0):
                        pe.wait_ge(row_done, t * 2 + c - 1)
                    ks, o = range(NK), slice(384 * c, 384 * c + 384)
                    product3(pe, prod[c][:, 0:384], [h_h[b][:, k, :] for k in ks], [h_l[b][:, k, :] for k in ks],
                             [w_hi[:, k, o] for k in ks], [w_lo[:, k, o] for k in ks]).then_inc(prod_full, 1)
                    if not last:
                        turns(t + 1, 1 - b, 2 * c, False)
                        turns(t + 1, 1 - b, 2 * c + 1, False)
            tile_pairs(pe, step)


def aggregate_general(nc, io, dram, keep, layer):
    H = GH if layer == 1 else 1
    HD = H * TW
    TROW = TROW1 if layer == 1 else TROW2
    tab, ald_d = dram[f"tab{layer}"], dram[f"ald{layer}"]
    HALF = ((0, 384), (384, D + 1 - 384))
    KD = 14
    with Pool(nc, f"x{layer}") as s:
        ids, pick, ones = s.sb("ids", [P, NP]), s.sb("pick", [P, 2 * GH]), s.sb("ones", [P, P])
        e, rows = s.sb("e", [P, 2, SLOTS], I32), s.sb("rows", [P, SLOTS, TROW])
        ald, own = s.sb("ald", [P, HD]), s.sb("own", [HD, TROW])
        mask, pen = s.sb("mask", [P, SLOTS, TW]), s.sb("pen", [P, SLOTS, TW])
        z, zmax, wt = s.sb("z", [P, SLOTS, HD]), s.sb("zmax", [P, HD]), s.sb("wt", [P, SLOTS, HD])
        mcol, zs, mrun, m2, shrink, scale, den, rden = (s.sb(n, [HD, 1]) for n in (
            "mcol", "zs", "mrun", "m2", "shrink", "scale", "den", "rden"))
        junk, dg = s.sb("junk", [HD, 2 * GH]), s.sb("dg", [HD, HD])
        acc, outb = s.sb("acc", [HD, D + 1]), s.sb("outb", [HD, D])
        res, bias = s.sb("res", [TW, D]), s.sb("bias", [TW, D])
        zt, mrow = s.bank("zt"), s.bank("mrow")
        num = [s.bank(f"num{i}") for i in range(2)]
        rows_in = keep["rows_in_general"][layer - 1]
        (const_in, step_in, e_in, stored, ones_set, gather_go, load_go, state_done, state_step, group_step, zt_full,
         mrow_full, exp_done, num_full, end_step) = (s.sem(n) for n in (
             "const_in", "step_in", "e_in", "stored", "ones_set", "gather_go", "load_go", "state_done", "state_step",
             "group_step", "zt_full", "mrow_full", "exp_done", "num_full", "end_step"))
        JS, JE = 4, 4
        IN = 16 * (H + 1 + (layer == 2))
        blk = s.block()

        def too_long(eng):
            return eng.value_load(keep["longest"][0:1, 0:1], min_val=0, max_val=2 * EP) > CAP

        def groups(eng, before, group, after):
            done = eng.alloc_register(f"x{layer}_done")
            eng.reg_mov(done, 0)
            with eng.Fori(0, NP // TW) as T:
                before(T)
                lo = eng.value_load(keep["ranges"][0:1, bass.ds(T * 2, 1)], min_val=0, max_val=EP)
                hi = eng.value_load(keep["ranges"][0:1, bass.ds(T * 2 + 1, 1)], min_val=0, max_val=EP)
                with eng.Fori(lo, hi, CAP) as at:
                    n = eng.snap(done, min_val=0, max_val=NP // TW * (EP // CAP + 1))
                    group(at, n, T)
                    eng.reg_add(done, done, 1)
                after(T, eng.snap(done, min_val=0, max_val=NP // TW * (EP // CAP + 1)))

        @blk.sync
        def _(sp):
            with sp.If(too_long(sp)):
                sp.dma_start(ids[:, :], io["node_ids"].partition_broadcast(P)).then_inc(const_in, 16)
                sp.dma_start(pick[:, :], io["head_pick"]).then_inc(const_in, 16)
                sp.dma_start(bias[:, :], io["b2"].partition_broadcast(TW)).then_inc(const_in, 16)

                def before(T):
                    n0 = sp.snap(T * TW)
                    sp.wait_ge(end_step, T * JE + 1)
                    sp.sem_inc(load_go, 1)
                    sp.dma_start(ald[:, :], ald_d[bass.ds(n0, TW), :].rearrange("d h -> (d h)").partition_broadcast(P)).then_inc(step_in, 16)
                    for h in range(H):
                        sp.dma_start(own[h * TW:(h + 1) * TW, :], tab[bass.ds(n0, TW), :]).then_inc(step_in, 16)
                    if layer == 2:
                        sp.dma_start(res[:, :], dram["res"][bass.ds(n0, TW), :]).then_inc(step_in, 16)

                def group(at, n, T):
                    sp.wait_ge(group_step, n * KD + 1)
                    sp.sem_inc(load_go, 1)
                    sp.dma_start(e[:, :, :], io["edges"][:, bass.ds(at, CAP)].rearrange("s (p c) -> p s c", c=SLOTS)).then_inc(e_in, 16)

                def after(T, n):
                    n0 = sp.snap(T * TW)
                    sp.wait_ge(end_step, T * JE + JE + 1)
                    sp.sem_inc(load_go, 1)
                    for h in range(H):
                        dst_ = dram["agg1"][h, bass.ds(n0, TW), :] if layer == 1 else dram["x2"][bass.ds(n0, TW), :]
                        sp.dma_start(dst_, outb[h * TW:(h + 1) * TW, :]).then_inc(stored, 16)
                    sp.wait_ge(stored, T * (16 * H) + 16 * H)
                    sp.sem_inc(load_go, 1)
                groups(sp, before, group, after)

        @blk.gpsimd
        def _(pool):
            with pool.If(too_long(pool)):
                pool.memset(ones[:, :], 1.0).then_inc(ones_set, 1)

                def group(at, n, T):
                    pool.wait_ge(e_in, n * 16 + 16)
                    pool.sem_inc(gather_go, 1)
                    for c in range(SLOTS):
                        pool.indirect_dma_start(rows[:, c, :], None, tab,
                                                bass.IndirectOffsetOnAxis(ap=e[:, 0, c:c + 1], axis=0)).then_inc(rows_in, 16)
                groups(pool, lambda T: None, group, lambda T, n: None)

        @blk.vector
        def _(dve):
            with dve.If(too_long(dve)):
                dve.wait_ge(const_in, 48)
                dve.sem_inc(group_step, 1)
                dve.sem_inc(end_step, 1)

                def before(T):
                    dve.wait_ge(step_in, T * IN + IN)
                    if layer == 1:
                        dve.tensor_tensor_reduce(junk[:, :], own[:, D + 1:D + 1 + 2 * H], pick[:, :], 1.0, 0.0, ALU.mult,
                                                 ALU.add, zs[:, :]).then_inc(state_step, 1)
                    else:
                        dve.tensor_tensor(zs[:, :], own[:, D + 1:D + 2], own[:, D + 2:D + 3], ALU.add).then_inc(state_step, 1)
                    dve.wait_ge(state_step, T * JS + 1)
                    dve.scalar_tensor_tensor(out=mrun[:, :], in0=zs[:, :], scalar=SLOPE, in1=zs[:, :], op0=ALU.mult,
                                             op1=ALU.max).then_inc(state_step, 1)
                    dve.tensor_copy(acc[:, :], own[:, 0:D + 1]).then_inc(state_step, 1)
                    if layer == 2:
                        dve.tensor_tensor(res[:, :], res[:, :], bias[:, :], ALU.add).then_inc(state_step, 1)
                    else:
                        dve.sem_inc(state_step, 1)
                    dve.wait_ge(state_step, T * JS + JS)

                def group(at, n, T):
                    k = [0]

                    def chain(ins):
                        ins.then_inc(group_step, 1)
                        k[0] += 1
                        dve.wait_ge(group_step, n * KD + k[0] + 1)

                    dve.wait_ge(rows_in, n * (16 * SLOTS) + 16 * SLOTS)
                    chain(dve.tensor_tensor(mask[:, :, :], e[:, 1, :].unsqueeze(2).to_broadcast([P, SLOTS, TW]),
                                            ids[:, bass.ds(T * TW, TW)].unsqueeze(1).to_broadcast([P, SLOTS, TW]), ALU.is_equal))
                    chain(dve.tensor_scalar(pen[:, :, :], mask[:, :, :], BIG, -BIG, ALU.mult, ALU.add))
                    z4 = z[:, :, :].rearrange("p c (h d) -> p c h d", h=H)
                    chain(dve.tensor_tensor(z4, rows[:, :, D + 1:D + 1 + H].unsqueeze(3).to_broadcast([P, SLOTS, H, TW]),
                                            pen[:, :, :].unsqueeze(2).to_broadcast([P, SLOTS, H, TW]), ALU.add))
                    chain(dve.tensor_tensor(z4, z4, ald[:, :].rearrange("p (d h) -> p h d", h=H).unsqueeze(1)
                                            .to_broadcast([P, SLOTS, H, TW]), ALU.add))
                    zf = z[:, :, :].rearrange("p c n -> p (c n)")
                    chain(dve.scalar_tensor_tensor(out=zf, in0=zf, scalar=SLOPE, in1=zf, op0=ALU.mult, op1=ALU.max))
                    chain(dve.tensor_reduce(zmax[:, :], z[:, :, :].rearrange("p c n -> p n c"), AX.X, ALU.max))
                    dve.wait_ge(zt_full, n + 1)
                    chain(dve.tensor_reduce(mcol[:, :], zt[0:HD, 0:P], AX.X, ALU.max))
                    chain(dve.tensor_tensor(m2[:, :], mcol[:, :], mrun[:, :], ALU.max))
                    chain(dve.tensor_scalar(dg[:, :], keep["ident"][0:HD, 0:HD], m2[:, 0:1], None, ALU.mult))
                    chain(dve.tensor_tensor(shrink[:, :], mrun[:, :], m2[:, :], ALU.subtract))
                    chain(dve.tensor_copy(mrun[:, :], m2[:, :]))
                    dve.wait_ge(mrow_full, n + 1)
                    chain(dve.tensor_tensor(wt[:, :, :], z[:, :, :], mrow[:, 0:HD].unsqueeze(1).to_broadcast([P, SLOTS, HD]),
                                            ALU.subtract))
                    dve.wait_ge(exp_done, n * 2 + 2)
                    for i, (a, w) in enumerate(HALF):
                        dve.wait_ge(num_full, n * 2 + i + 1)
                        chain(dve.scalar_tensor_tensor(out=acc[:, a:a + w], in0=acc[:, a:a + w], scalar=scale[:, 0:1],
                                                       in1=num[i][0:HD, 0:w], op0=ALU.mult, op1=ALU.add))

                def after(T, n):
                    dve.tensor_scalar(den[:, :], acc[:, D:D + 1], 1e-16, None, ALU.add).then_inc(end_step, 1)
                    dve.wait_ge(end_step, T * JE + 2)
                    dve.reciprocal(rden[:, :], den[:, :]).then_inc(end_step, 1)
                    dve.wait_ge(end_step, T * JE + 3)
                    dve.tensor_scalar(outb[:, :], acc[:, 0:D], rden[:, 0:1], None, ALU.mult).then_inc(end_step, 1)
                    dve.wait_ge(end_step, T * JE + 4)
                    if layer == 2:
                        dve.tensor_tensor(outb[:, :], outb[:, :], res[:, :], ALU.add).then_inc(end_step, 1)
                    else:
                        dve.tensor_copy(mcol[:, :], den[:, :]).then_inc(end_step, 1)
                groups(dve, before, group, after)

        @blk.scalar
        def _(act):
            with act.If(too_long(act)):
                def group(at, n, T):
                    act.wait_ge(group_step, n * KD + 13)
                    act.activation(scale[:, :], shrink[:, :], ACT.Exp).then_inc(exp_done, 1)
                    act.activation(wt[:, :, :].rearrange("p c n -> p (c n)"), wt[:, :, :].rearrange("p c n -> p (c n)"),
                                   ACT.Exp).then_inc(exp_done, 1)
                groups(act, lambda T: None, group, lambda T, n: None)

        @blk.tensor
        def _(pe):
            with pe.If(too_long(pe)):
                pe.wait_ge(ones_set, 1)

                def group(at, n, T):
                    pe.wait_ge(group_step, n * KD + 7)
                    pe.transpose(zt[0:HD, 0:P], zmax[:, :], keep["ident"][:, :]).then_inc(zt_full, 1)
                    pe.wait_ge(group_step, n * KD + 10)
                    pe.matmul(mrow[:, 0:HD], ones[0:HD, :], dg[:, :], start=True, stop=True).then_inc(mrow_full, 1)
                    pe.wait_ge(exp_done, n * 2 + 2)
                    for c in range(SLOTS):
                        for i, (a, w) in enumerate(HALF):
                            mm = pe.matmul(num[i][0:HD, 0:w], wt[:, c, :], rows[:, c, a:a + w], start=(c == 0),
                                           stop=(c == SLOTS - 1))
                            if c == SLOTS - 1:
                                mm.then_inc(num_full, 1)
                groups(pe, lambda T: None, group, lambda T, n: None)


def aggregate_one_head(nc, io, dram, keep):
    GR = P // TW
    S = GR * SLOTS
    HALF = ((0, 384), (384, D + 1 - 384))
    tab = dram["tab2"]
    with Pool(nc, "h") as s:
        ids, ones = s.sb("ids", [P, NP]), s.sb("ones", [P, P])
        e, rows = s.sb2("e", [P, 2, S], I32), s.sb2("rows", [P, S, TROW2])
        ald, own, resb = s.sb2("ald", [P, P]), s.sb2("own", [P, TROW2]), s.sb2("resb", [P, D])
        bias, mask, pen, z = s.sb("bias", [P, D]), s.sb("mask", [P, S, TW]), s.sb("pen", [P, S, TW]), s.sb("z", [P, S, TW])
        zmax, dg = s.sb("zmax", [P, P]), s.sb("dg", [P, P])
        mcol, zs, zself, m2, dself, den, rden = (s.sb(n, [P, 1]) for n in ("mcol", "zs", "zself", "m2", "dself", "den", "rden"))
        wt, wself = s.sb2("wt", [P, S, TW]), s.sb2("wself", [P, 1])
        acc, outb = s.sb("acc", [P, D + 1]), s.sb2("outb", [P, D])
        zt, mrow = s.bank("zt"), s.bank("mrow")
        num = [[s.bank(f"num{b}{i}") for i in range(2)] for b in range(2)]
        const_in = s.sem("const_in")
        e_in, ald_in, own_in, res_in, stored = (s.sem2(n) for n in ("e_in", "ald_in", "own_in", "res_in", "stored"))
        rows_in = keep["rows_in"][1]
        (ones_set, gather_go, mask_done, pen_done, z1_done, z2_done, z3_done, zmax_done, zt_full, mcol_done, zs_done,
         zself_done, m2_done, dg_done, dself_done, mrow_full, shift_done, wself_done, exp_done, num_full, acc_done,
         den_done, rden_done, out_done, resb_done) = (s.sem(n) for n in (
             "ones_set", "gather_go", "mask_done", "pen_done", "z1_done", "z2_done", "z3_done", "zmax_done", "zt_full",
             "mcol_done", "zs_done", "zself_done", "m2_done", "dg_done", "dself_done", "mrow_full", "shift_done",
             "wself_done", "exp_done", "num_full", "acc_done", "den_done", "rden_done", "out_done", "resb_done"))
        blk = s.block()

        def fits(eng):
            return eng.value_load(keep["longest"][0:1, 0:1], min_val=0, max_val=2 * EP) <= CAP

        @blk.sync
        def _(sp):
            with sp.If(fits(sp)):
                sp.dma_start(ids[:, :], io["node_ids"].partition_broadcast(P)).then_inc(const_in, 16)
                sp.dma_start(bias[:, :], io["b2"].partition_broadcast(P)).then_inc(const_in, 16)

                def load(p, b, first, last):
                    t = p * 2 + b
                    r = sp.snap(t * P) if not first else t * P
                    for k in range(GR):
                        lo = sp.value_load(keep["ranges"][0:1, bass.ds(t * (2 * GR) + 2 * k, 1)], min_val=0, max_val=EP)
                        sp.dma_start(e[b][:, :, k * SLOTS:(k + 1) * SLOTS],
                                     io["edges"][:, bass.ds(lo, CAP)].rearrange("s (p c) -> p s c", c=SLOTS)).then_inc(e_in[b], 16)
                    sp.dma_start(ald[b][:, :], dram["ald2"][bass.ds(r, P), :].rearrange("d h -> (d h)").partition_broadcast(P)).then_inc(ald_in[b], 16)
                    sp.dma_start(own[b][:, :], tab[bass.ds(r, P), :]).then_inc(own_in[b], 16)
                    sp.dma_start(resb[b][:, :], dram["res"][bass.ds(r, P), :]).then_inc(res_in[b], 16)

                def store(p, b, first, last):
                    t = p * 2 + b
                    r = sp.snap(t * P) if not first else t * P
                    sp.wait_ge(out_done, t + 1)
                    sp.dma_start(dram["x2"][bass.ds(r, P), :], outb[b][:, :]).then_inc(stored[b], 16)
                loads_ahead(sp, load, store)
                sp.wait_ge(stored[0], 16 * (NT - NT // 2))
                sp.wait_ge(stored[1], 16 * (NT // 2))

        @blk.gpsimd
        def _(pool):
            with pool.If(fits(pool)):
                pool.memset(ones[:, :], 1.0).then_inc(ones_set, 1)

                def step(p, b, first, last):
                    pool.wait_ge(e_in[b], p * (16 * GR) + 16 * GR)
                    pool.sem_inc(gather_go, 1)
                    for c in range(S):
                        pool.indirect_dma_start(rows[b][:, c, :], None, tab,
                                                bass.IndirectOffsetOnAxis(ap=e[b][:, 0, c:c + 1], axis=0)).then_inc(rows_in[b], 16)
                tile_pairs(pool, step)

        @blk.vector
        def _(dve):
            with dve.If(fits(dve)):
                dve.wait_ge(const_in, 32)

                def split4(ap):
                    return ap.rearrange("p (k c) d -> p k c d", k=GR)

                def weights(p, b, first):
                    t = p * 2 + b
                    dve.wait_ge(e_in[b], p * (16 * GR) + 16 * GR)
                    dve.wait_ge(pen_done, t)
                    dve.tensor_tensor(split4(mask[:, :, :]),
                                      e[b][:, 1, :].rearrange("p (k c) -> p k c", k=GR).unsqueeze(3).to_broadcast([P, GR, SLOTS, TW]),
                                      ids[:, bass.ds(t * P, P)].rearrange("p (k d) -> p k d", k=GR).unsqueeze(2)
                                      .to_broadcast([P, GR, SLOTS, TW]), ALU.is_equal).then_inc(mask_done, 1)
                    dve.wait_ge(mask_done, t + 1)
                    dve.wait_ge(z1_done, t)
                    dve.tensor_scalar(pen[:, :, :], mask[:, :, :], BIG, -BIG, ALU.mult, ALU.add).then_inc(pen_done, 1)
                    dve.wait_ge(own_in[b], p * 16 + 16)
                    dve.wait_ge(zself_done, t)
                    dve.tensor_tensor(zs[:, :], own[b][:, D + 1:D + 2], own[b][:, D + 2:D + 3], ALU.add).then_inc(zs_done, 1)
                    dve.wait_ge(zs_done, t + 1)
                    dve.wait_ge(dself_done, t)
                    dve.scalar_tensor_tensor(out=zself[:, :], in0=zs[:, :], scalar=SLOPE, in1=zs[:, :], op0=ALU.mult,
                                             op1=ALU.max).then_inc(zself_done, 1)
                    dve.wait_ge(rows_in[b], p * (16 * S) + 16 * S)
                    dve.wait_ge(ald_in[b], p * 16 + 16)
                    dve.wait_ge(pen_done, t + 1)
                    dve.wait_ge(shift_done, t)
                    dve.tensor_tensor(z[:, :, :], rows[b][:, :, D + 1:D + 2].to_broadcast([P, S, TW]), pen[:, :, :],
                                      ALU.add).then_inc(z1_done, 1)
                    dve.wait_ge(z1_done, t + 1)
                    dve.tensor_tensor(split4(z[:, :, :]), split4(z[:, :, :]),
                                      ald[b][:, :].rearrange("p (k d) -> p k d", k=GR).unsqueeze(2)
                                      .to_broadcast([P, GR, SLOTS, TW]), ALU.add).then_inc(z2_done, 1)
                    dve.wait_ge(z2_done, t + 1)
                    zf = z[:, :, :].rearrange("p c n -> p (c n)")
                    dve.scalar_tensor_tensor(out=zf, in0=zf, scalar=SLOPE, in1=zf, op0=ALU.mult, op1=ALU.max).then_inc(z3_done, 1)
                    dve.wait_ge(z3_done, t + 1)
                    dve.wait_ge(zt_full, t)
                    dve.tensor_reduce(zmax[:, :].rearrange("p (k d) -> p k d", k=GR),
                                      split4(z[:, :, :]).rearrange("p k c d -> p k d c"), AX.X, ALU.max).then_inc(zmax_done, 1)
                    dve.wait_ge(zt_full, t + 1)
                    dve.tensor_reduce(mcol[:, :], zt[:, 0:P], AX.X, ALU.max).then_inc(mcol_done, 1)
                    dve.wait_ge(mcol_done, t + 1)
                    dve.wait_ge(zself_done, t + 1)
                    dve.wait_ge(dg_done, t)
                    dve.tensor_tensor(m2[:, :], mcol[:, :], zself[:, :], ALU.max).then_inc(m2_done, 1)
                    dve.wait_ge(m2_done, t + 1)
                    dve.wait_ge(mrow_full, t)
                    dve.tensor_scalar(dg[:, :], keep["ident"][:, :], m2[:, 0:1], None, ALU.mult).then_inc(dg_done, 1)
                    dve.wait_ge(wself_done, t)
                    dve.tensor_tensor(dself[:, :], zself[:, :], m2[:, :], ALU.subtract).then_inc(dself_done, 1)
                    dve.wait_ge(mrow_full, t + 1)
                    if not first:
                        dve.wait_ge(num_full, t * 2 - 2)
                    dve.tensor_tensor(split4(wt[b][:, :, :]), split4(z[:, :, :]),
                                      mrow[:, 0:P].rearrange("p (k d) -> p k d", k=GR).unsqueeze(2)
                                      .to_broadcast([P, GR, SLOTS, TW]), ALU.subtract).then_inc(shift_done, 1)

                def sums(p, b, first):
                    t = p * 2 + b
                    dve.wait_ge(res_in[b], p * 16 + 16)
                    dve.tensor_tensor(resb[b][:, :], resb[b][:, :], bias[:, :], ALU.add).then_inc(resb_done, 1)
                    dve.wait_ge(wself_done, t + 1)
                    dve.wait_ge(out_done, t)
                    for i, (a, n) in enumerate(HALF):
                        dve.wait_ge(num_full, t * 2 + i + 1)
                        dve.scalar_tensor_tensor(out=acc[:, a:a + n], in0=own[b][:, a:a + n], scalar=wself[b][:, 0:1],
                                                 in1=num[b][i][:, 0:n], op0=ALU.mult, op1=ALU.add).then_inc(acc_done, 1)
                    dve.wait_ge(acc_done, t * 2 + 2)
                    dve.tensor_scalar(den[:, :], acc[:, D:D + 1], 1e-16, None, ALU.add).then_inc(den_done, 1)
                    dve.wait_ge(den_done, t + 1)
                    dve.reciprocal(rden[:, :], den[:, :]).then_inc(rden_done, 1)
                    dve.wait_ge(rden_done, t + 1)
                    dve.wait_ge(resb_done, t + 1)
                    if not first:
                        dve.wait_ge(stored[b], p * 16)
                    dve.scalar_tensor_tensor(out=outb[b][:, :], in0=acc[:, 0:D], scalar=rden[:, 0:1], in1=resb[b][:, :],
                                             op0=ALU.mult, op1=ALU.add).then_inc(out_done, 1)

                def step(p, b, first, last):
                    weights(p, b, first)
                    sums(p, b, first)
                tile_pairs(dve, step)

        @blk.scalar
        def _(act):
            with act.If(fits(act)):
                def step(p, b, first, last):
                    t = p * 2 + b
                    act.wait_ge(dself_done, t + 1)
                    if not first:
                        act.wait_ge(acc_done, t * 2 - 2)
                    act.activation(wself[b][:, :], dself[:, :], ACT.Exp).then_inc(wself_done, 1)
                    act.wait_ge(shift_done, t + 1)
                    wf = wt[b][:, :, :].rearrange("p c n -> p (c n)")
                    act.activation(wf, wf, ACT.Exp).then_inc(exp_done, 1)
                tile_pairs(act, step)

        @blk.tensor
        def _(pe):
            with pe.If(fits(pe)):
                pe.wait_ge(ones_set, 1)

                def step(p, b, first, last):
                    t = p * 2 + b
                    pe.wait_ge(zmax_done, t + 1)
                    pe.transpose(zt[:, 0:P], zmax[:, :], keep["ident"][:, :]).then_inc(zt_full, 1)
                    pe.wait_ge(dg_done, t + 1)
                    pe.matmul(mrow[:, 0:P], ones[:, :], dg[:, :], start=True, stop=True).then_inc(mrow_full, 1)
                    pe.wait_ge(exp_done, t + 1)
                    if not first:
                        pe.wait_ge(acc_done, t * 2 - 2)
                    for i, (a, n) in enumerate(HALF):
                        for c in range(SLOTS):
                            for k in range(GR):
                                mm = pe.matmul(num[b][i][k * TW:(k + 1) * TW, 0:n], wt[b][:, k * SLOTS + c, :],
                                               rows[b][:, k * SLOTS + c, a:a + n], start=(c == 0), stop=(c == SLOTS - 1),
                                               tile_position=(0, k * TW), skip_group_check=True)
                        mm.then_inc(num_full, 1)
                tile_pairs(pe, step)


def phase_i(nc, io, dram, keep, out):
    EH = NEXP * DHID
    NK = EH // P
    with Pool(nc, "i") as s:
        u_hi, u_lo = s.sb("u_hi", [P, KC, EH], F32R), s.sb("u_lo", [P, KC, EH], F32R)
        w_hi, w_lo = s.sb("w_hi", [P, NK, D], F32R), s.sb("w_lo", [P, NK, D], F32R)
        r_hi, r_lo = s.sb("r_hi", [P, KC, NEXP], F32R), s.sb("r_lo", [P, KC, NEXP], F32R)
        split_weights(nc, "is", [(io["eW1"][k * P:(k + 1) * P, :], u_hi[:, k, :], u_lo[:, k, :]) for k in range(KC)]
                      + [(io["eW2"][k * P:(k + 1) * P, :], w_hi[:, k, :], w_lo[:, k, :]) for k in range(NK)]
                      + [(io["Wr"][k * P:(k + 1) * P, :], r_hi[:, k, :], r_lo[:, k, :]) for k in range(KC)], EH)
        ident = keep["ident"]
        x = s.sb2("x", [P, D])
        xn = s.sb("xn", [P, D])
        xt_h, xt_l = s.sb2("xt_h", [P, KC, P], F32R), s.sb2("xt_l", [P, KC, P], F32R)
        hid = s.sb("hid", [P, EH])
        ht_h, ht_l = s.sb("ht_h", [P, NK, P], F32R), s.sb("ht_l", [P, NK, P], F32R)
        y = s.sb("y", [P, D])
        b1, b2 = s.sb("b1", [P, EH]), s.sb("b2", [NEXP, D])
        gain, shift = s.sb("gain", [P, D]), s.sb("shift", [P, D])
        br, ramp = s.sb("br", [P, NEXP]), s.sb("ramp", [P, NEXP])
        st, mv, vps, rstd = s.sb("st", [P, 2, 6]), s.sb("mv", [P, 2]), s.sb("vps", [P, 1]), s.sb("rstd", [P, 1])
        yst, ymv, yvps, yrstd = s.sb("yst", [P, 2, 6]), s.sb("ymv", [P, 2]), s.sb("yvps", [P, 1]), s.sb("yrstd", [P, 1])
        lg, hot = s.sb("lg", [P, NEXP]), s.sb("hot", [P, 2, NEXP])
        score, rest, ex, ew = (s.sb(n, [P, NEXP]) for n in ("score", "rest", "ex", "ew"))
        top, best, negm, den, rden = (s.sb(n, [P, 1]) for n in ("top", "best", "negm", "den", "rden"))
        ewt = s.sb("ewt", [NEXP, P])
        turn = [s.bank(f"turn{i}") for i in range(2)]
        log_b, ewt_b = s.bank("log_b"), s.bank("ewt_b")
        up = [s.bank(f"up{i}") for i in range(2)]
        down = [s.bank(f"down{i}") for i in range(2)]
        c_in, x_in, out_sem = s.sem("c_in"), s.sem2("x_in"), s.sem2("out")
        (stats_done, stats_seen, mean_done, vps_done, rstd_done, xn_done, turn_full, hi_done, lo_done, log_full, route_step, ew_steps,
         exp_done, ew_done, ewt_full, ewt_done, up_full, biased, gelu_done, scaled, ht_full, hth_done, htl_done, down_full,
         y_done, ystats_done, ystats_seen, ymean_done, yvps_done, yrstd_done, gain_done, sum_done, xs_done) = (
            s.sem(n) for n in (
                "stats_done", "stats_seen", "mean_done", "vps_done", "rstd_done", "xn_done", "turn_full", "hi_done",
                "lo_done", "log_full", "route_step", "ew_steps", "exp_done", "ew_done", "ewt_full", "ewt_done", "up_full", "biased",
                "gelu_done", "scaled", "ht_full", "hth_done", "htl_done", "down_full", "y_done", "ystats_done",
                "ystats_seen", "ymean_done", "yvps_done", "yrstd_done", "gain_done", "sum_done", "xs_done"))
        blk = s.block()
        RSTEPS = 11

        @blk.sync
        def _(sp):
            for dst_, src_ in ((b1, "eb1"), (gain, "ln_g"), (shift, "ln_b"), (br, "br"), (ramp, "expert_ramp")):
                sp.dma_start(dst_[:, :], io[src_].partition_broadcast(P)).then_inc(c_in, 16)
            sp.dma_start(b2[:, :], io["eb2"]).then_inc(c_in, 16)

            def load(p, b, first, last):
                t = p * 2 + b
                r = sp.snap(t * P) if not first else t * P
                rows = LAST if last else P
                if not first:
                    sp.wait_ge(out_sem[b], t * 8 - 8 * b)
                sp.dma_start(x[b][0:rows, :], dram["x2"][bass.ds(r, rows), :]).then_inc(x_in[b], 16)

            def store(p, b, first, last):
                t = p * 2 + b
                r = sp.snap(t * P) if not first else t * P
                rows = LAST if last else P
                sp.wait_ge(sum_done, t + 1)
                sp.dma_start(out[bass.ds(r, rows), :], x[b][0:rows, :]).then_inc(out_sem[b], 16)
            loads_ahead(sp, load, store)
            sp.wait_ge(out_sem[0], 16 * (NT - NT // 2))
            sp.wait_ge(out_sem[1], 16 * (NT // 2))

        @blk.gpsimd
        def _(pool):
            pool.wait_ge(c_in, 16 * 6)
            layernorm_rstd(pool, mv, vps, rstd, keep["ln_eps"], keep["minus_half"], mean_done, vps_done, rstd_done, 0)

            def step(p, b, first, last):
                t = p * 2 + b
                if not last:
                    layernorm_rstd(pool, mv, vps, rstd, keep["ln_eps"], keep["minus_half"], mean_done, vps_done, rstd_done, t + 1)
                pool.wait_ge(xn_done, t + 1)
                pool.tensor_tensor(x[b][:, :], x[b][:, :], shift[:, :], ALU.add).then_inc(xs_done, 1)
                layernorm_rstd(pool, ymv, yvps, yrstd, keep["ln_eps"], keep["minus_half"], ymean_done, yvps_done, yrstd_done, t)
            tile_pairs(pool, step)

        @blk.scalar
        def _(act):
            def high(t, b, g, first):
                act.wait_ge(turn_full, t * 2 + g + 1)
                if g == 0 and not first:
                    act.wait_ge(up_full, t * 4 - 4)
                act.activation(xt_h[b][:, 3 * g:3 * g + 3, :].rearrange("p k n -> p (k n)"), turn[g][:, 0:384],
                               ACT.Copy).then_inc(hi_done, 1)

            high(0, 0, 0, True)
            high(0, 0, 1, True)

            def step(p, b, first, last):
                t = p * 2 + b
                act.wait_ge(route_step, t * RSTEPS + 3)
                act.activation(ex[:, :], lg[:, :], ACT.Exp, bias=negm[:, 0:1]).then_inc(exp_done, 1)
                for c in range(4):
                    act.wait_ge(biased, t * 4 + c + 1)
                    act.activation(hid[:, 384 * c:384 * c + 384], hid[:, 384 * c:384 * c + 384],
                                   ACT.Gelu_apprx_tanh).then_inc(gelu_done, 1)
                act.wait_ge(down_full, t * 2)
                for g in range(4):
                    act.wait_ge(ht_full, t * 4 + g + 1)
                    act.activation(ht_h[:, 3 * g:3 * g + 3, :].rearrange("p k n -> p (k n)"), turn[g % 2][:, 0:384],
                                   ACT.Copy).then_inc(hth_done, 1)
                if not last:
                    high(t + 1, 1 - b, 0, first and b == 0)
                    high(t + 1, 1 - b, 1, first and b == 0)
                act.wait_ge(sum_done, t)
                for c in range(2):
                    act.wait_ge(down_full, t * 2 + c + 1)
                    act.activation(y[:, 384 * c:384 * c + 384], down[c][:, 0:384], ACT.Copy).then_inc(y_done, 1)
            tile_pairs(act, step)

        @blk.vector
        def _(dve):
            dve.wait_ge(c_in, 16 * 6)

            def norm(t, b):
                dve.wait_ge(x_in[b], t * 8 + (16 - 8 * b))
                dve.wait_ge(rstd_done, t)
                layernorm_stats(dve, x[b], st, mv, stats_done, stats_seen, mean_done, t)
                dve.wait_ge(rstd_done, t + 1)
                dve.wait_ge(turn_full, t * 2)
                dve.tensor_scalar(xn[:, :], x[b][:, :], mv[:, 0:1], rstd[:, 0:1], ALU.subtract, ALU.mult).then_inc(xn_done, 1)

            def low(t, b):
                for g in range(2):
                    dve.wait_ge(hi_done, t * 2 + g + 1)
                    o = xt_h[b][:, 3 * g:3 * g + 3, :].rearrange("p k n -> p (k n)")
                    dve.tensor_tensor(xt_l[b][:, 3 * g:3 * g + 3, :].rearrange("p k n -> p (k n)"), turn[g][:, 0:384],
                                      o.bitcast(F32), ALU.subtract).then_inc(lo_done, 1)

            def route(t):
                n = [t * RSTEPS]

                def chain(ins):
                    ins.then_inc(route_step, 1)
                    n[0] = n[0] + 1
                    dve.wait_ge(route_step, n[0])

                dve.wait_ge(log_full, t + 1)
                dve.wait_ge(ew_done, t)
                chain(dve.tensor_tensor(lg[:, :], log_b[:, 0:NEXP], br[:, :], ALU.add))
                for i, src_ in enumerate((lg, rest)):
                    chain(dve.tensor_reduce(top[:, :], src_[:, :], AX.X, ALU.max))
                    if i == 0:
                        chain(dve.tensor_scalar(negm[:, :], top[:, :], -1.0, None, ALU.mult))
                    chain(dve.scalar_tensor_tensor(out=score[:, :], in0=src_[:, :], scalar=top[:, 0:1], in1=ramp[:, :],
                                                   op0=ALU.is_equal, op1=ALU.mult))
                    chain(dve.tensor_reduce(best[:, :], score[:, :], AX.X, ALU.max))
                    chain(dve.tensor_scalar(hot[:, i, :], score[:, :], best[:, 0:1], None, ALU.is_equal))
                    if i == 0:
                        chain(dve.scalar_tensor_tensor(out=rest[:, :], in0=hot[:, 0, :], scalar=-BIG, in1=lg[:, :],
                                                       op0=ALU.mult, op1=ALU.add))

            def route_end(t):
                dve.wait_ge(exp_done, t + 1)
                dve.tensor_tensor(hot[:, 0, :], hot[:, 0, :], hot[:, 1, :], ALU.add).then_inc(ew_steps, 1)
                dve.wait_ge(ew_steps, t * 4 + 1)
                dve.tensor_tensor(ex[:, :], ex[:, :], hot[:, 0, :], ALU.mult).then_inc(ew_steps, 1)
                dve.wait_ge(ew_steps, t * 4 + 2)
                dve.tensor_reduce(den[:, :], ex[:, :], AX.X, ALU.add).then_inc(ew_steps, 1)
                dve.wait_ge(ew_steps, t * 4 + 3)
                dve.reciprocal(rden[:, :], den[:, :]).then_inc(ew_steps, 1)
                dve.wait_ge(ew_steps, t * 4 + 4)
                dve.wait_ge(scaled, t * 4)
                dve.wait_ge(ewt_full, t)
                dve.tensor_scalar(ew[:, :], ex[:, :], rden[:, 0:1], None, ALU.mult).then_inc(ew_done, 1)

            def route_turned(t):
                dve.wait_ge(ewt_full, t + 1)
                dve.wait_ge(down_full, t * 2)
                dve.tensor_copy(ewt[:, :], ewt_b[0:NEXP, 0:P]).then_inc(ewt_done, 1)

            def add_bias(t, c):
                dve.wait_ge(up_full, t * 4 + c + 1)
                if c == 0:
                    dve.wait_ge(ht_full, t * 4)
                o = slice(384 * c, 384 * c + 384)
                dve.tensor_tensor(hid[:, o], up[c % 2][:, 0:384], b1[:, o], ALU.add).then_inc(biased, 1)

            def scale(t, c):
                dve.wait_ge(gelu_done, t * 4 + c + 1)
                dve.wait_ge(ew_done, t + 1)
                v = hid[:, 384 * c:384 * c + 384].rearrange("p (e j) -> p e j", j=DHID)
                dve.tensor_tensor(v, v, ew[:, 2 * c:2 * c + 2].unsqueeze(2).to_broadcast([P, 2, DHID]), ALU.mult).then_inc(scaled, 1)

            def hid_low(t):
                for g in range(4):
                    dve.wait_ge(hth_done, t * 4 + g + 1)
                    o = ht_h[:, 3 * g:3 * g + 3, :].rearrange("p k n -> p (k n)")
                    dve.tensor_tensor(ht_l[:, 3 * g:3 * g + 3, :].rearrange("p k n -> p (k n)"), turn[g % 2][:, 0:384],
                                      o.bitcast(F32), ALU.subtract).then_inc(htl_done, 1)

            def finish(t, b):
                dve.wait_ge(y_done, t * 2 + 2)
                dve.wait_ge(yrstd_done, t)
                layernorm_stats(dve, y, yst, ymv, ystats_done, ystats_seen, ymean_done, t)
                dve.wait_ge(yrstd_done, t + 1)
                dve.tensor_scalar(y[:, :], y[:, :], ymv[:, 0:1], yrstd[:, 0:1], ALU.subtract, ALU.mult).then_inc(gain_done, 1)
                dve.wait_ge(gain_done, t * 2 + 1)
                dve.tensor_tensor(y[:, :], y[:, :], gain[:, :], ALU.mult).then_inc(gain_done, 1)
                dve.wait_ge(gain_done, t * 2 + 2)
                dve.wait_ge(xs_done, t + 1)
                dve.tensor_tensor(x[b][:, :], y[:, :], x[b][:, :], ALU.add).then_inc(sum_done, 1)

            norm(0, 0)
            low(0, 0)

            def step(p, b, first, last):
                t = p * 2 + b
                add_bias(t, 0)
                route(t)
                route_end(t)
                scale(t, 0)
                for c in range(1, 4):
                    add_bias(t, c)
                    scale(t, c)
                route_turned(t)
                if not last:
                    norm(t + 1, 1 - b)
                hid_low(t)
                if not last:
                    low(t + 1, 1 - b)
                finish(t, b)
            tile_pairs(dve, step)

        @blk.tensor
        def _(pe):
            def x_turns(t):
                pe.wait_ge(xn_done, t + 1)
                for g in range(2):
                    if not (isinstance(t, int) and t == 0):
                        pe.wait_ge(htl_done, t * 4 - 1 + g)
                    for i in range(3):
                        k = 3 * g + i
                        mm = pe.transpose(turn[g][:, i * P:(i + 1) * P], xn[:, k * P:(k + 1) * P], ident[:, :])
                    mm.then_inc(turn_full, 1)

            x_turns(0)

            def step(p, b, first, last):
                t = p * 2 + b
                ks = range(KC)
                xh, xl = [xt_h[b][:, k, :] for k in ks], [xt_l[b][:, k, :] for k in ks]
                pe.wait_ge(lo_done, t * 2 + 2)
                pe.wait_ge(route_step, t * RSTEPS)
                product3(pe, log_b[:, 0:NEXP], xh, xl, [r_hi[:, k, :] for k in ks], [r_lo[:, k, :] for k in ks]).then_inc(log_full, 1)
                for c in range(4):
                    if not (first and b == 0 and c < 2):
                        pe.wait_ge(biased, t * 4 + c - 1)
                    o = slice(384 * c, 384 * c + 384)
                    product3(pe, up[c % 2][:, 0:384], xh, xl, [u_hi[:, k, o] for k in ks], [u_lo[:, k, o] for k in ks]).then_inc(up_full, 1)
                    if c == 2:
                        pe.wait_ge(ew_done, t + 1)
                        pe.wait_ge(ewt_done, t)
                        pe.transpose(ewt_b[0:NEXP, 0:P], ew[:, :], ident[:, :]).then_inc(ewt_full, 1)
                for g in range(4):
                    pe.wait_ge(scaled, t * 4 + g + 1)
                    if g < 2:
                        pe.wait_ge(lo_done, t * 2 + g + 1)
                    else:
                        pe.wait_ge(htl_done, t * 4 + g - 1)
                    for i in range(3):
                        k = 3 * g + i
                        mm = pe.transpose(turn[g % 2][:, i * P:(i + 1) * P], hid[:, k * P:(k + 1) * P], ident[:, :])
                    mm.then_inc(ht_full, 1)
                if not last:
                    x_turns(t + 1)
                pe.wait_ge(htl_done, t * 4 + 4)
                pe.wait_ge(ewt_done, t + 1)
                for c in range(2):
                    if not (first and b == 0):
                        pe.wait_ge(y_done, t * 2 + c - 1)
                    o = slice(384 * c, 384 * c + 384)
                    product3(pe, down[c][:, 0:384], [ht_h[:, k, :] for k in range(NK)], [ht_l[:, k, :] for k in range(NK)],
                                  [w_hi[:, k, o] for k in range(NK)], [w_lo[:, k, o] for k in range(NK)], last=False)
                    pe.matmul(down[c][:, 0:384], ewt[:, :], b2[:, o], start=False, stop=True).then_inc(down_full, 1)
            tile_pairs(pe, step)


def build(nc, io, out):
    def scratch(name, shape):
        return nc.dram_tensor(name, shape, F32).ap()

    dram = {
        "tab1": scratch("tab1", (NP, TROW1)), "ald1": scratch("ald1", (NP, GH)), "vx": scratch("vx", (NP, HEADS * VW)),
        "res": scratch("res", (NP, D)), "agg1": scratch("agg1", (GH, NP, D)), "h1": scratch("h1", (NP, HID)),
        "tab2": scratch("tab2", (NP, TROW2)), "ald2": scratch("ald2", (NP, 1)), "x2": scratch("x2", (NP, D)),
    }
    dram["blocks"], dram["spans"] = scratch("blocks", (2, EP // 8)), scratch("spans", (P,))
    dram["ranges"] = nc.dram_tensor("ranges", (P, 2), I32).ap()
    for n in ("qt_h", "qt_l", "kt_h", "kt_l"):
        dram[n] = scratch(n, (NT, P, D))
    keep = {}
    with Pool(nc, "keep") as s:
        setup(nc, io, keep, s)
        with Pool(nc, "mix") as m:
            setup_mix(nc, io, keep, m)
            phase_a(nc, io, dram, keep)
            global_key_max(nc, keep)
            phase_b(nc, io, dram, keep)
            phase_c(nc, io, dram, keep)
        phase_ranges(nc, io, dram, keep, s)
        aggregate(nc, io, dram, keep, 1)
        aggregate_general(nc, io, dram, keep, 1)
        phase_f(nc, io, dram, keep)
        phase_g(nc, io, dram, keep)
        aggregate_one_head(nc, io, dram, keep)
        aggregate_general(nc, io, dram, keep, 2)
        phase_i(nc, io, dram, keep, out)




def kernel(x, src, dst, L0_gnn_W1, L0_gnn_att_src1, L0_gnn_att_dst1, L0_gnn_b1, L0_gnn_W2, L0_gnn_att_src2,
           L0_gnn_att_dst2, L0_gnn_b2, L0_mix_w_qkv, L0_mix_w_proj, L0_mix_b_proj, L0_mix_proj_mat, L0_ffn_Wr,
           L0_ffn_br, L0_ffn_W1, L0_ffn_b1, L0_ffn_W2, L0_ffn_b2, L0_ffn_ln_g, L0_ffn_ln_b):
    import numpy as np
    from concourse import bacc
    from concourse.bass_utils import run_bass_kernel_spmd

    arrays = host_arrays(x, src, dst, L0_gnn_W1, L0_gnn_att_src1, L0_gnn_att_dst1, L0_gnn_b1, L0_gnn_W2,
                         L0_gnn_att_src2, L0_gnn_att_dst2, L0_gnn_b2, L0_mix_w_qkv, L0_mix_w_proj, L0_mix_b_proj,
                         L0_mix_proj_mat, L0_ffn_Wr, L0_ffn_br, L0_ffn_W1, L0_ffn_b1, L0_ffn_W2, L0_ffn_b2,
                         L0_ffn_ln_g, L0_ffn_ln_b)
    nc = bacc.Bacc("TRN2", target_bir_lowering=False, num_devices=1)
    io = {n: nc.dram_tensor(f"in_{n}", a.shape, mybir.dt.from_np(a.dtype), kind="ExternalInput").ap()
          for n, a in arrays.items()}
    out = nc.dram_tensor("out", (N, D), F32, kind="ExternalOutput").ap()
    build(nc, io, out)
    r = run_bass_kernel_spmd(nc, [{f"in_{n}": a for n, a in arrays.items()}], core_ids=[0])
    return r.results[0]["out"]


def host_arrays(x, src, dst, W1, asrc1, adst1, b1, W2, asrc2, adst2, b2, w_qkv, w_proj, b_proj, proj_mat, Wr, br,
                eW1, eb1, eW2, eb2, ln_g, ln_b):
    import numpy as np

    def lay(a):
        return np.ascontiguousarray(a)

    xp = np.zeros((NP, D), np.asarray(x).dtype)
    xp[:N] = np.asarray(x)
    edges = np.zeros((2, EROOM), np.int32)
    edges[1] = 8192
    edges[0, :len(src)] = np.asarray(src)
    edges[1, :len(dst)] = np.asarray(dst)
    blocks = EP // 8
    return {
        "x": xp, "edges": edges, "W1": lay(W1), "asrc1": lay(asrc1).reshape(-1), "adst1": lay(adst1).reshape(-1),
        "b1": lay(b1), "W2": lay(W2), "asrc2": lay(asrc2).reshape(-1), "adst2": lay(adst2).reshape(-1), "b2": lay(b2),
        "wqkvT": lay(np.asarray(w_qkv).T), "wprojT": lay(np.asarray(w_proj).T), "bproj": lay(b_proj),
        "projT": lay(np.asarray(proj_mat).T), "Wr": lay(Wr), "br": lay(br),
        "eW1": lay(np.asarray(eW1).transpose(1, 0, 2).reshape(D, NEXP * DHID)), "eb1": lay(eb1).reshape(-1),
        "eW2": lay(np.asarray(eW2).reshape(NEXP * DHID, D)), "eb2": lay(eb2), "ln_g": lay(ln_g), "ln_b": lay(ln_b),
        "ident": np.eye(P, dtype=np.float32),
        "node_ids": np.arange(NP, dtype=np.float32),
        "steps": np.arange(P, dtype=np.float32).reshape(P, 1),
        "block_ramps": np.stack([np.arange(blocks, 0, -1), np.arange(1, blocks + 1)]).astype(np.float32),
        "head_pick": np.tile(np.kron(np.eye(GH), np.ones((TW, 1))), (1, 2)).astype(np.float32),
        "expert_ramp": np.arange(NEXP, 0, -1).astype(np.float32),
    }
```

```python
from contextlib import ExitStack

import concourse.bass as bass
from concourse import mybir

F32 = mybir.dt.float32
F32R = mybir.dt.float32r
I32 = mybir.dt.int32
ALU = mybir.AluOpType
ACT = mybir.ActivationFunctionType
AX = mybir.AxisListType
P = 128

N = 3125
NT = (N + P - 1) // P
NP = NT * P
LAST = N - (NT - 1) * P
D = 768
KC = D // P
HEADS = 12
DH = D // HEADS
M = 256
VW = DH + 1
MIX_EPS = 1e-4
LN_EPS = 1e-5
GH = 4
GC = 512
HID = GH * GC
SLOPE = 0.2
TW = 32
TROW1 = D + 1 + 2 * GH
TROW2 = D + 3
SLOTS = 5
CAP = SLOTS * P
BIG = 1.0e30
NEXP = 8
BLOCK = 16
EP = 53760
EROOM = EP + CAP
DHID = 192


def tile_pairs(eng, step, tiles=NT):
    pairs = tiles // 2
    step(0, 0, True, False)
    step(0, 1, True, False)
    with eng.Fori(1, pairs) as p:
        step(p, 0, False, False)
        step(p, 1, False, False)
    step(pairs, 0, False, True)


def loads_ahead(eng, load, store):
    pairs = NT // 2
    load(0, 0, True, False)
    load(0, 1, True, False)
    store(0, 0, True, False)
    load(1, 0, False, False)
    store(0, 1, True, False)
    load(1, 1, False, False)
    with eng.Fori(1, pairs - 1) as p:
        store(p, 0, False, False)
        load(p + 1, 0, False, False)
        store(p, 1, False, False)
        load(p + 1, 1, False, False)
    store(pairs - 1, 0, False, False)
    load(pairs, 0, False, True)
    store(pairs - 1, 1, False, False)
    store(pairs, 0, False, True)


def loads_first(eng, load, rest, start=lambda: None):
    pairs = NT // 2
    load(0, 0, True, False)
    load(0, 1, True, False)
    start()
    load(1, 0, False, False)
    rest(0, 0, True, False)
    load(1, 1, False, False)
    rest(0, 1, True, False)
    with eng.Fori(1, pairs - 1) as p:
        load(p + 1, 0, False, False)
        rest(p, 0, False, False)
        load(p + 1, 1, False, False)
        rest(p, 1, False, False)
    load(pairs, 0, False, True)
    rest(pairs - 1, 0, False, False)
    rest(pairs - 1, 1, False, False)
    rest(pairs, 0, False, True)


class Pool:

    def __init__(self, nc, tag):
        self.nc, self.tag, self.stack, self.sems, self.blk = nc, tag, ExitStack(), [], None

    def __enter__(self):
        return self

    def __exit__(self, *exc):
        if exc[0]:
            return
        if self.blk is not None:
            self.blk.close()
        if self.sems:
            nums = sorted(self.sems)
            starts = [n for n in nums if n - 1 not in nums]
            for first in starts:
                end = next(n for n in range(first, nums[-1] + 2) if n not in nums)
                self.nc.all_engine_barrier(sems_to_clear=range(first, end))
        self.stack.close()

    def sb(self, name, shape, dt=F32):
        return self.stack.enter_context(self.nc.sbuf_tensor(f"{self.tag}_{name}", shape, dt))

    def sb2(self, name, shape, dt=F32):
        return [self.sb(f"{name}{b}", shape, dt) for b in range(2)]

    def bank(self, name):
        return self.stack.enter_context(self.nc.psum_tensor(f"{self.tag}_{name}", [P, 512], F32))

    def sem(self, name):
        s = self.stack.enter_context(self.nc.semaphore(f"{self.tag}_{name}"))
        self.sems.append(s.num)
        return s

    def sem2(self, name):
        return [self.sem(f"{name}{b}") for b in range(2)]

    def block(self):
        self.blk = ExitStack()
        return self.blk.enter_context(self.nc.Block())


def product3(pe, out, x_hi, x_lo, w_hi, w_lo, last=True):
    n = len(x_hi)
    for k in range(n):
        pe.matmul(out, x_hi[k], w_hi[k], start=(k == 0), stop=False)
        pe.matmul(out, x_hi[k], w_lo[k], start=False, stop=False)
        mm = pe.matmul(out, x_lo[k], w_hi[k], start=False, stop=(last and k == n - 1))
    return mm


def group_heads(g):
    return 4 * (g // 2) + g % 2, 4 * (g // 2) + g % 2 + 2


def dash_pair(pe, banks, k_hi, k_lo, j, pj_h, pj_l, full):
    for i in range(2):
        for a, (x, w) in enumerate(((k_hi, pj_h), (k_hi, pj_l), (k_lo, pj_h))):
            for e in range(2):
                r = slice(e * DH, e * DH + DH)
                mm = pe.matmul(banks[e][:, M * i:M * i + M], x[r, j + i, :], w[r, :], start=(a == 0), stop=(a == 2))
                if i == 1 and a == 2:
                    mm.then_inc(full, 1)


def split_weights(nc, tag, jobs, width):
    S = 6
    with Pool(nc, tag) as s:
        stage = [s.sb(f"stage{b}", [P, width]) for b in range(S)]
        staged = [s.sem(f"staged{b}") for b in range(S)]
        hi_done, lo_done = s.sem("hi_done"), s.sem("lo_done")
        blk = s.block()

        @blk.sync
        def _(sp):
            for n, (src, hi, lo) in enumerate(jobs):
                if n >= S:
                    sp.wait_ge(lo_done, n - S + 1)
                sp.dma_start(stage[n % S][:, :src.shape[1]], src).then_inc(staged[n % S], 16)

        @blk.scalar
        def _(act):
            for n, (src, hi, lo) in enumerate(jobs):
                act.wait_ge(staged[n % S], 16 * (n // S + 1))
                act.activation(hi, stage[n % S][:, :src.shape[1]], ACT.Copy).then_inc(hi_done, 1)

        @blk.vector
        def _(dve):
            for n, (src, hi, lo) in enumerate(jobs):
                dve.wait_ge(hi_done, n + 1)
                dve.tensor_tensor(lo, stage[n % S][:, :src.shape[1]], hi.bitcast(F32),
                                  ALU.subtract).then_inc(lo_done, 1)


def layernorm_stats(dve, x, st, mv, stats_done, stats_seen, mean_done, t):
    for i in range(2):
        dve.bn_stats(st[:, i, :], x[:, i * (D // 2):(i + 1) * (D // 2)]).then_inc(stats_done, 1)
    dve.wait_ge(stats_done, t * 2 + 2)
    dve.sem_inc(stats_seen, 1)
    dve.bn_aggr(mv[:, :], st[:, :, :]).then_inc(mean_done, 1)


def layernorm_rstd(pool, mv, vps, rstd, ln_eps, minus_half, mean_done, vps_done, rstd_done, t):
    pool.wait_ge(mean_done, t + 1)
    pool.tensor_tensor(vps[:, :], mv[:, 1:2], ln_eps[:, :], ALU.add).then_inc(vps_done, 1)
    pool.wait_ge(vps_done, t + 1)
    pool.tensor_tensor(rstd[:, :], vps[:, :], minus_half[:, :], ALU.pow).then_inc(rstd_done, 1)


def joint_weights(nc, io, keep, w_hi, w_lo):
    with Pool(nc, "lw") as s:
        w1 = [s.sb(f"w1{b}", [P, HID]) for b in range(2)]
        att = s.sb("att", [P, 2, HID])
        junk = s.sb("junk", [P, GC])
        dots = s.sb("dots", [P, KC, 2 * GH])
        stage = s.sb2("stage", [P, 3 * D])
        att_in, w1_in, staged = s.sem("att_in"), s.sem2("w1_in"), s.sem2("staged")
        hi_done, lo_done = s.sem("hi_done"), s.sem("lo_done")
        dot_done, split_done = s.sem("dot_done"), s.sem("split_done")
        blk = s.block()

        @blk.sync
        def _(sp):
            sp.dma_start(att[:, 0, :], io["asrc1"].partition_broadcast(P)).then_inc(att_in, 16)
            sp.dma_start(att[:, 1, :], io["adst1"].partition_broadcast(P)).then_inc(att_in, 16)
            for k in range(KC):
                if k >= 2:
                    sp.wait_ge(dot_done, (k - 1) * 2 * GH)
                sp.dma_start(w1[k % 2][:, :], io["W1"][k * P:(k + 1) * P, :]).then_inc(w1_in[k % 2], 16)
                if k >= 2:
                    sp.wait_ge(lo_done, k - 1)
                sp.dma_start(stage[k % 2][:, :], io["wqkvT"][k * P:(k + 1) * P, :]).then_inc(staged[k % 2], 16)

        @blk.scalar
        def _(act):
            for k in range(KC):
                act.wait_ge(staged[k % 2], 16 * (k // 2 + 1))
                act.activation(w_hi[:, k, 0:3 * D], stage[k % 2][:, :], ACT.Copy).then_inc(hi_done, 1)

        @blk.vector
        def _(dve):
            dve.wait_ge(att_in, 32)
            n = 0
            for k in range(KC):
                dve.wait_ge(w1_in[k % 2], 16 * (k // 2 + 1))
                for side in range(2):
                    for h in range(GH):
                        if n:
                            dve.wait_ge(dot_done, n)
                        j = side * GH + h
                        dve.tensor_tensor_reduce(
                            junk[:, :], w1[k % 2][:, h * GC:(h + 1) * GC],
                            att[:, side, h * GC:(h + 1) * GC], 1.0, 0.0, ALU.mult, ALU.add,
                            dots[:, k, j:j + 1]).then_inc(dot_done, 1)
                        n += 1
                dve.wait_ge(hi_done, k + 1)
                dve.tensor_tensor(w_lo[:, k, 0:3 * D], stage[k % 2][:, :], w_hi[:, k, 0:3 * D].bitcast(F32),
                                  ALU.subtract).then_inc(lo_done, 1)
            dve.wait_ge(dot_done, n)
            a = 3 * D
            dve.tensor_copy(w_hi[:, :, a:a + 2 * GH], dots[:, :, :]).then_inc(split_done, 1)
            dve.wait_ge(split_done, 1)
            dve.tensor_tensor(w_lo[:, :, a:a + 2 * GH], dots[:, :, :],
                              w_hi[:, :, a:a + 2 * GH].bitcast(F32), ALU.subtract).then_inc(split_done, 1)


def phase_a(nc, io, dram, keep):
    WA = 3 * D + 2 * GH
    with Pool(nc, "a") as s:
        w_hi, w_lo = s.sb("w_hi", [P, KC, WA], F32R), s.sb("w_lo", [P, KC, WA], F32R)
        joint_weights(nc, io, keep, w_hi, w_lo)
        ident = keep["ident"]
        x = s.sb2("x", [P, D])
        xn = s.sb2("xn", [P, D])
        xt_h, xt_l = s.sb2("xt_h", [P, KC, P], F32R), s.sb2("xt_l", [P, KC, P], F32R)
        qk = s.sb2("qk", [P, 2 * D])
        sq = s.sb("sq", [P, 2 * D])
        dsum = s.sb("dsum", [P, 2 * HEADS])
        v = s.sb2("v", [P, HEADS * VW])
        al = s.sb2("al", [P, 1 + 2 * GH])
        qt_h, qt_l = s.sb2("qt_h", [P, 2 * KC, P], F32R), s.sb2("qt_l", [P, 2 * KC, P], F32R)
        st, mv = s.sb("st", [P, 2, 6]), s.sb("mv", [P, 2])
        vps, rstd = s.sb("vps", [P, 1]), s.sb("rstd", [P, 1])
        bank = [s.bank(f"bank{i}") for i in range(8)]

        x_in = s.sem2("x_in")
        stats_done, stats_seen, mean_done = s.sem("stats_done"), s.sem("stats_seen"), s.sem("mean_done")
        vps_done, rstd_done, xn_done = s.sem("vps_done"), s.sem("rstd_done"), s.sem("xn_done")
        xt_full, hi_done, lo_done = s.sem("xt_full"), s.sem("xt_hi_done"), s.sem("xt_lo_done")
        gemm_full = s.sem("gemm_full")
        qk_done, v_done = s.sem("qk_done"), s.sem("v_done")
        qt_full, qhi_done, qlo_done = s.sem("qt_full"), s.sem("qt_hi_done"), s.sem("qt_lo_done")
        dash_full, kmax_done = s.sem("dash_full"), s.sem("kmax_done")
        sq_done, dsum_done, diag_done = s.sem("sq_done"), s.sem("dsum_done"), s.sem("diag_done")
        ones_set, kmax_set = s.sem("ones_set"), s.sem("kmax_set")
        xn_out, v_out, q_out = s.sem2("xn_out"), s.sem2("v_out"), s.sem2("q_out")
        blk = s.block()
        CH = [(0, 512), (512, 512), (1024, 512), (1536, 512), (2048, WA - 2048)]
        pj_h, pj_l = keep["pj_h"], keep["pj_l"]

        @blk.sync
        def _(sp):
            def load(p, b, first, last):
                r = sp.snap((p * 2 + b) * P) if not first else b * P
                if not first:
                    sp.wait_ge(xn_done, p * 2 + b - 1)
                sp.dma_start(x[b][:, :], io["x"][bass.ds(r, P), :]).then_inc(x_in[b], 16)

            def store(p, b, first, last):
                t = p * 2 + b
                r = sp.snap(t * P) if not first else t * P
                t4 = sp.snap(t * 4) if not first else t * 4
                tt = sp.snap(t) if not first else t
                sp.wait_ge(xn_done, t + 1)
                sp.dma_start(dram["tab1"][bass.ds(r, P), 0:D], xn[b][:, :]).then_inc(xn_out[b], 16)
                sp.wait_ge(v_done, t * 4 + 4)
                sp.dma_start(dram["vx"][bass.ds(r, P), :], v[b][:, :]).then_inc(v_out[b], 16)
                sp.dma_start(dram["tab1"][bass.ds(r, P), D:TROW1], al[b][:, :]).then_inc(v_out[b], 16)
                sp.dma_start(dram["ald1"][bass.ds(r, P), :], al[b][:, 1 + GH:]).then_inc(v_out[b], 16)
                sp.wait_ge(qhi_done, t * 4 + 4)
                sp.wait_ge(qlo_done, t * 4 + 4)
                for i, (hi, lo) in enumerate((("qt_h", "qt_l"), ("kt_h", "kt_l"))):
                    sp.dma_start(dram[hi][bass.ds(tt, 1), :, :].rearrange("a p n -> (a p) n"),
                                 qt_h[b][:, i * KC:(i + 1) * KC, :].rearrange("p k n -> p (k n)").bitcast(F32)).then_inc(q_out[b], 16)
                    sp.dma_start(dram[lo][bass.ds(tt, 1), :, :].rearrange("a p n -> (a p) n"),
                                 qt_l[b][:, i * KC:(i + 1) * KC, :].rearrange("p k n -> p (k n)").bitcast(F32)).then_inc(q_out[b], 16)

            loads_first(sp, load, store)
            for b, n in ((0, NT - NT // 2), (1, NT // 2)):
                sp.wait_ge(xn_out[b], 16 * n)
                sp.wait_ge(v_out[b], 48 * n)
                sp.wait_ge(q_out[b], 64 * n)

        @blk.vector
        def _(dve):
            dve.memset(keep["kmx"][:, :], -BIG).then_inc(kmax_set, 1)
            dve.wait_ge(kmax_set, 1)

            def norm(t, b, first):
                dve.wait_ge(x_in[b], t * 8 + (16 - 8 * b))
                dve.wait_ge(rstd_done, t)
                layernorm_stats(dve, x[b], st, mv, stats_done, stats_seen, mean_done, t)
                dve.wait_ge(rstd_done, t + 1)
                if not first:
                    dve.wait_ge(xn_out[b], t * 8 - 8 * b)
                    dve.wait_ge(xt_full, t * 2 - 2)
                dve.tensor_scalar(xn[b][:, :], x[b][:, :], mv[:, 0:1], rstd[:, 0:1],
                                  ALU.subtract, ALU.mult).then_inc(xn_done, 1)

            def xt_low(t, b, first):
                for g in range(2):
                    dve.wait_ge(hi_done, t * 2 + g + 1)
                    if not first:
                        dve.wait_ge(gemm_full, t * 5 - 5)
                    o = xt_l[b][:, 3 * g:3 * g + 3, :].rearrange("p k n -> p (k n)")
                    dve.tensor_tensor(o, bank[g][:, 0:384],
                                      xt_h[b][:, 3 * g:3 * g + 3, :].rearrange("p k n -> p (k n)").bitcast(F32),
                                      ALU.subtract).then_inc(lo_done, 1)

            def diag(t, b):
                dve.wait_ge(sq_done, t + 1)
                dve.wait_ge(diag_done, t)
                dve.tensor_reduce(dsum[:, :], sq[:, :].rearrange("p (h d) -> p h d", d=DH), AX.X,
                                  ALU.add).then_inc(dsum_done, 1)
                dve.wait_ge(dsum_done, t + 1)
                dve.tensor_scalar(keep["diag"][:, bass.ds(t * 2 * HEADS, 2 * HEADS)].rearrange("p (g e i) -> p g e i", e=2, i=2),
                                  dsum[:, :].rearrange("p (g i e) -> p g e i", i=2, e=2),
                                  -0.5 * DH ** -0.5, None, ALU.mult).then_inc(diag_done, 1)

            def key_max(t, last):
                rows = LAST if last else P
                for g in range(6):
                    dve.wait_ge(dash_full, t * 6 + g + 1)
                    dve.tensor_reduce(keep["kmx"][0:rows, bass.ds(t * 6 + g, 1)],
                                      bank[2 + g % 5][0:rows, :], AX.X, ALU.max).then_inc(kmax_done, 1)

            def qt_low(t, b, first):
                if not first:
                    dve.wait_ge(q_out[b], t * 32 - 32 * b)
                    dve.wait_ge(dash_full, t * 6 - 6)
                for g in range(4):
                    dve.wait_ge(qhi_done, t * 4 + g + 1)
                    o = slice(3 * g, 3 * g + 3)
                    dve.tensor_tensor(qt_l[b][:, o, :].rearrange("p k n -> p (k n)"), bank[[7, 0, 1, 7][g]][:, 0:384],
                                      qt_h[b][:, o, :].rearrange("p k n -> p (k n)").bitcast(F32),
                                      ALU.subtract).then_inc(qlo_done, 1)

            norm(0, 0, True)
            xt_low(0, 0, True)

            def step(p, b, first, last):
                t = p * 2 + b
                if not last:
                    norm(t + 1, 1 - b, first and b == 0)
                    xt_low(t + 1, 1 - b, first and b == 0)
                if not (first and b == 0):
                    key_max(t - 1, False)
                qt_low(t, b, first)
                diag(t, b)
            tile_pairs(dve, step)
            key_max(NT - 1, True)

        @blk.gpsimd
        def _(pool):
            for b in range(2):
                ones = v[b][:, :].rearrange("p (h d) -> p h d", d=VW)[:, :, DH:VW]
                pool.memset(ones, 1.0).then_inc(ones_set, 1)
                pool.memset(al[b][:, 0:1], 1.0).then_inc(ones_set, 1)

            def rstd_of(t):
                layernorm_rstd(pool, mv, vps, rstd, keep["ln_eps"], keep["minus_half"], mean_done, vps_done, rstd_done, t)

            def squares(t, b):
                pool.wait_ge(dsum_done, t)
                pool.wait_ge(qk_done, t * 3 + 3)
                pool.tensor_tensor(sq[:, :], qk[b][:, :], qk[b][:, :], ALU.mult).then_inc(sq_done, 1)

            rstd_of(0)

            def step(p, b, first, last):
                t = p * 2 + b
                if not last:
                    rstd_of(t + 1)
                squares(t, b)
                if last:
                    ones = v[b][:, :].rearrange("p (h d) -> p h d", d=VW)[:, :, DH:VW]
                    pool.wait_ge(v_out[0], 48 * (NT // 2))
                    pool.memset(ones, 0.0).then_inc(ones_set, 1)
                    pool.wait_ge(ones_set, 5)
                    pool.memset(ones[0:LAST], 1.0).then_inc(ones_set, 1)
            tile_pairs(pool, step)

        @blk.scalar
        def _(act):
            def xt_high(t, b, first):
                for g in range(2):
                    act.wait_ge(xt_full, t * 2 + g + 1)
                    if not first:
                        act.wait_ge(gemm_full, t * 5 - 5)
                    act.activation(xt_h[b][:, 3 * g:3 * g + 3, :].rearrange("p k n -> p (k n)"),
                                   bank[g][:, 0:384], ACT.Copy).then_inc(hi_done, 1)

            def step(p, b, first, last):
                t = p * 2 + b
                if not last:
                    xt_high(t + 1, 1 - b, first and b == 0)
                if not first:
                    act.wait_ge(sq_done, t - 1)
                    act.wait_ge(qt_full, t * 4 - 4)
                for c in range(3):
                    act.wait_ge(gemm_full, t * 5 + c + 1)
                    act.activation(qk[b][:, 512 * c:512 * c + 512], bank[2 + c][:, :], ACT.Copy).then_inc(qk_done, 1)
                if first:
                    act.wait_ge(ones_set, 4)
                else:
                    act.wait_ge(v_out[b], t * 24 - 24 * b)
                if last:
                    act.wait_ge(ones_set, 6)
                vh = v[b][:, :].rearrange("p (h d) -> p h d", d=VW)[:, :, 0:DH]
                act.wait_ge(gemm_full, t * 5 + 4)
                act.activation(vh[:, 0:8, :], bank[5][:, :].rearrange("p (h d) -> p h d", d=DH), ACT.Copy).then_inc(v_done, 1)
                act.wait_ge(gemm_full, t * 5 + 5)
                act.activation(vh[:, 8:12, :], bank[6][:, 0:256].rearrange("p (h d) -> p h d", d=DH), ACT.Copy).then_inc(v_done, 1)
                act.activation(al[b][:, 1:1 + GH], bank[6][:, 256:256 + GH], ACT.Copy).then_inc(v_done, 1)
                act.activation(al[b][:, 1 + GH:], bank[6][:, 256 + GH:256 + 2 * GH], ACT.Copy).then_inc(v_done, 1)
                if not first:
                    act.wait_ge(q_out[b], t * 32 - 32 * b)
                    act.wait_ge(dash_full, t * 6 - 6)
                for g in range(4):
                    act.wait_ge(qt_full, t * 4 + g + 1)
                    act.activation(qt_h[b][:, 3 * g:3 * g + 3, :].rearrange("p k n -> p (k n)"),
                                   bank[[7, 0, 1, 7][g]][:, 0:384], ACT.Copy).then_inc(qhi_done, 1)

            xt_high(0, 0, True)
            tile_pairs(act, step)

        @blk.tensor
        def _(pe):
            def x_transposes(t, b, first):
                pe.wait_ge(xn_done, t + 1)
                for g in range(2):
                    if not first:
                        pe.wait_ge(qlo_done, t * 4 - 8 + g + 2)
                    for i in range(3):
                        k = 3 * g + i
                        mm = pe.transpose(bank[g][:, P * i:P * i + P], xn[b][:, k * P:(k + 1) * P], ident[:, :])
                    mm.then_inc(xt_full, 1)

            def products(t, b, first, chunks):
                if chunks[0] == 0:
                    pe.wait_ge(lo_done, t * 2 + 2)
                if chunks[0] == 0 and first and b == 1:
                    pe.wait_ge(qk_done, 3)
                    pe.wait_ge(v_done, 4)
                for c in chunks:
                    a, n = CH[c]
                    if not first:
                        pe.wait_ge(kmax_done, t * 6 - 12 + (6 if c == 0 else c + 1))
                    product3(pe, bank[2 + c][:, 0:n], [xt_h[b][:, k, :] for k in range(KC)],
                             [xt_l[b][:, k, :] for k in range(KC)],
                             [w_hi[:, k, a:a + n] for k in range(KC)],
                             [w_lo[:, k, a:a + n] for k in range(KC)]).then_inc(gemm_full, 1)

            def dash(t, b, gemm_tile):
                pe.wait_ge(qlo_done, t * 4 + 4)
                for g in range(6):
                    if g < 5 and gemm_tile is not None:
                        if g < 3:
                            pe.wait_ge(qk_done, gemm_tile * 3 + g + 1)
                        else:
                            pe.wait_ge(v_done, gemm_tile * 4 + (1 if g == 3 else 4))
                    elif g == 5:
                        pe.wait_ge(kmax_done, t * 6 + 1)
                    elif gemm_tile is None:
                        pe.wait_ge(kmax_done, t * 6 - 6 + (6 if g == 0 else g + 1))
                    if g % 2 == 1:
                        dash_pair(pe, (bank[1 + g], bank[2 + g % 5]), qt_h[b], qt_l[b], KC + g - 1, pj_h, pj_l, dash_full)

            def q_transposes(t, b, first, last):
                pe.wait_ge(qk_done, t * 3 + 3)
                for g in range(4):
                    if g == 0 and not (first and b == 0):
                        pe.wait_ge(qlo_done, t * 4)
                    if g in (1, 2) and not last:
                        pe.wait_ge(lo_done, t * 2 + 2 + g)
                    if g in (1, 2) and last:
                        pe.wait_ge(qlo_done, t * 4 - 2 + g - 1)
                    if g == 3:
                        pe.wait_ge(qlo_done, t * 4 + 1)
                    for i in range(3):
                        k = 3 * g + i
                        mm = pe.transpose(bank[[7, 0, 1, 7][g]][:, P * i:P * i + P], qk[b][:, k * P:(k + 1) * P],
                                          ident[:, :])
                    mm.then_inc(qt_full, 1)

            x_transposes(0, 0, True)

            def step(p, b, first, last):
                t = p * 2 + b
                products(t, b, first, (0, 1, 2))
                if not last:
                    x_transposes(t + 1, 1 - b, first and b == 0)
                products(t, b, first, (3, 4))
                if not (first and b == 0):
                    dash(t - 1, 1 - b, t)
                q_transposes(t, b, first, last)
            tile_pairs(pe, step)
            dash(NT - 1, 0, None)


def global_key_max(nc, keep):
    with Pool(nc, "gm") as s:
        col, row, one = s.sb("col", [P, 1]), s.sb("row", [1, 1]), s.sb("one", [1, P])
        pt, pb = s.bank("pt"), s.bank("pb")
        col_done, turned, row_done, spread = s.sem("col_done"), s.sem("turned"), s.sem("row_done"), s.sem("spread")
        one_set, neg_done, bias_done = s.sem("one_set"), s.sem("neg_done"), s.sem("bias_done")
        blk = s.block()

        @blk.vector
        def _(dve):
            dve.memset(one[:, :], -1.0).then_inc(one_set, 1)
            dve.tensor_reduce(col[:, :], keep["kmx"][:, :], AX.X, ALU.max).then_inc(col_done, 1)
            dve.wait_ge(turned, 1)
            dve.tensor_reduce(row[:, :], pt[0:1, 0:P], AX.X, ALU.max).then_inc(row_done, 1)
            dve.wait_ge(spread, 1)
            dve.tensor_copy(keep["negm"][:, :], pb[:, 0:1]).then_inc(neg_done, 1)
            dve.wait_ge(neg_done, 1)
            kd = keep["diag"][:, :].rearrange("p (t s h) -> p t s h", s=2, h=HEADS)[:, :, 1, :]
            dve.tensor_scalar(keep["kbias"][:, :].rearrange("p (t h) -> p t h", h=HEADS), kd,
                              keep["negm"][:, 0:1], None, ALU.add).then_inc(bias_done, 1)

        @blk.tensor
        def _(pe):
            pe.wait_ge(col_done, 1)
            pe.transpose(pt[0:1, 0:P], col[:, :], keep["ident"][:, :]).then_inc(turned, 1)
            pe.wait_ge(row_done, 1)
            pe.wait_ge(one_set, 1)
            pe.matmul(pb[:, 0:1], one[0:1, :], row[0:1, 0:1], start=True, stop=True).then_inc(spread, 1)


class EdgeRanges:

    NB = EP // BLOCK
    ROWS = 120

    def __init__(self, nc, io, dram, keep, t):
        self.io, self.dram, self.keep = io, dram, keep
        NB, ROWS = self.NB, self.ROWS
        self.d, self.q = t.sb("d", [ROWS, EP // ROWS], I32), t.sb("q", [ROWS, EP // ROWS], I32)
        self.blk_min, self.blk_max = t.sb("blk_min", [ROWS, NB // ROWS]), t.sb("blk_max", [ROWS, NB // ROWS])
        self.every_min, self.every_max = t.sb("every_min", [P, NB]), t.sb("every_max", [P, NB])
        self.ramps, self.hit = t.sb("ramps", [P, 2, NB]), t.sb("hit", [P, NB])
        self.step_no, self.ends, self.span = t.sb("step_no", [P, 1]), t.sb("ends", [P, 2]), t.sb("span", [P, 1])
        self.ints = t.sb("ints", [P, 2], I32)
        self.span_row, self.span_max = t.sb("span_row", [1, P]), t.sb("span_max", [1, 1])
        (self.d_in, self.c_in, self.blocks_out, self.blocks_in, self.ints_out, self.ints_in, self.q_done, self.blk_done,
         self.hit_done, self.end_done, self.int_done, self.long_done) = (t.sem(n) for n in (
             "d_in", "c_in", "blocks_out", "blocks_in", "ints_out", "ints_in", "q_done", "blk_done", "hit_done",
             "end_done", "int_done", "long_done"))

    def fetch(self, sp):
        sp.dma_start(self.d[:, :], self.io["edges"][1, 0:EP].rearrange("(p c) -> p c", p=self.ROWS)).then_inc(self.d_in, 16)

    def blocks(self, dve):
        dve.wait_ge(self.d_in, 16)
        dve.tensor_scalar(self.q[:, :], self.d[:, :], 5, None, ALU.logical_shift_right).then_inc(self.q_done, 1)
        dve.wait_ge(self.q_done, 1)
        qb = self.q[:, :].rearrange("p (b e) -> p b e", e=BLOCK)
        dve.tensor_reduce(self.blk_min[:, :], qb, AX.X, ALU.min).then_inc(self.blk_done, 1)
        dve.tensor_reduce(self.blk_max[:, :], qb, AX.X, ALU.max).then_inc(self.blk_done, 1)

    def spread(self, sp):
        sp.dma_start(self.ramps[:, :, :].rearrange("p s n -> p (s n)"),
                     self.io["block_ramps"].rearrange("s n -> (s n)").partition_broadcast(P)).then_inc(self.c_in, 16)
        sp.dma_start(self.step_no[:, :], self.io["steps"]).then_inc(self.c_in, 16)
        sp.wait_ge(self.blk_done, 2)
        for i, blk in enumerate((self.blk_min, self.blk_max)):
            sp.dma_start(self.dram["blocks"][i, :].rearrange("(p c) -> p c", p=self.ROWS), blk[:, :]).then_inc(self.blocks_out, 16)
        sp.wait_ge(self.blocks_out, 32)
        for i, every in enumerate((self.every_min, self.every_max)):
            sp.dma_start(every[:, :], self.dram["blocks"][i, :].partition_broadcast(P)).then_inc(self.blocks_in, 16)

    def end(self, dve, i):
        dve.wait_ge(self.c_in, 32)
        dve.wait_ge(self.blocks_in, 32)
        if i:
            dve.wait_ge(self.end_done, 1)
        dve.scalar_tensor_tensor(out=self.hit[:, :], in0=self.every_min[:, :], scalar=self.step_no[:, 0:1],
                                 in1=self.ramps[:, i, :], op0=ALU.is_le, op1=ALU.mult).then_inc(self.hit_done, 1)
        dve.wait_ge(self.hit_done, 2 * i + 1)
        dve.scalar_tensor_tensor(out=self.hit[:, :], in0=self.every_max[:, :], scalar=self.step_no[:, 0:1],
                                 in1=self.hit[:, :], op0=ALU.is_ge, op1=ALU.mult).then_inc(self.hit_done, 1)
        dve.wait_ge(self.hit_done, 2 * i + 2)
        dve.tensor_reduce(self.ends[:, i:i + 1], self.hit[:, :], AX.X, ALU.max).then_inc(self.end_done, 1)
        if i:
            dve.wait_ge(self.end_done, 2)
            dve.tensor_scalar(self.ints[:, 0:1], self.ends[:, 0:1], -float(BLOCK), float(BLOCK * self.NB), ALU.mult,
                              ALU.add).then_inc(self.int_done, 1)
            dve.tensor_scalar(self.ints[:, 1:2], self.ends[:, 1:2], float(BLOCK), None, ALU.mult).then_inc(self.int_done, 1)
            dve.tensor_tensor(self.span[:, :], self.ends[:, 0:1], self.ends[:, 1:2], ALU.add).then_inc(self.int_done, 1)

    def store_row(self, sp):
        sp.wait_ge(self.int_done, 3)
        sp.dma_start(self.dram["ranges"], self.ints[:, :]).then_inc(self.ints_out, 16)
        sp.dma_start(self.dram["spans"].rearrange("(p a) -> p a", a=1), self.span[:, :]).then_inc(self.ints_out, 16)
        sp.wait_ge(self.ints_out, 32)
        sp.dma_start(self.keep["ranges"][:, :], self.dram["ranges"].rearrange("(a p) c -> a (p c)", a=1)).then_inc(self.ints_in, 16)
        sp.dma_start(self.span_row[:, :], self.dram["spans"].rearrange("(a p) -> a p", a=1)).then_inc(self.ints_in, 16)
        sp.wait_ge(self.ints_in, 32)

    def longest(self, dve):
        dve.wait_ge(self.ints_in, 32)
        dve.tensor_reduce(self.span_max[:, :], self.span_row[:, :], AX.X, ALU.max).then_inc(self.long_done, 1)
        dve.wait_ge(self.long_done, 1)
        dve.tensor_scalar(self.keep["longest"][:, :], self.span_max[:, :], float(BLOCK), -float(BLOCK * self.NB), ALU.mult,
                          ALU.add).then_inc(self.long_done, 1)


def phase_b(nc, io, dram, keep):
    with Pool(nc, "b") as s:
        kt_h, kt_l = s.sb2("kt_h", [P, KC, P], F32R), s.sb2("kt_l", [P, KC, P], F32R)
        vx = s.sb2("vx", [P, HEADS * VW])
        kp = s.sb2("kp", [P, HEADS * M])
        zl, zr = s.sb("zl", [P, P]), s.sb("zr", [P, 512])
        dash = [s.bank(f"dash{i}") for i in range(4)]
        cacc = [s.bank(f"cacc{i}") for i in range(4)]
        kt_in, vx_in = s.sem2("kt_in"), s.sem2("vx_in")
        z_set, dash_full, exp_done, kp_done, ctx_done = (s.sem(n) for n in (
            "z_set", "dash_full", "exp_done", "kp_done", "ctx_done"))
        ctx_out = s.sem("ctx_out")
        blk = s.block()

        @blk.sync
        def _(sp):
            def step(p, b, first, last):
                t = p * 2 + b
                tt = sp.snap(t) if not first else t
                r = sp.snap(t * P) if not first else t * P
                if not first:
                    sp.wait_ge(dash_full, t * 6 - 6)
                sp.dma_start(kt_h[b][:, :, :].rearrange("p k n -> p (k n)").bitcast(F32),
                             dram["kt_h"][bass.ds(tt, 1), :, :].rearrange("a p n -> (a p) n")).then_inc(kt_in[b], 16)
                sp.dma_start(kt_l[b][:, :, :].rearrange("p k n -> p (k n)").bitcast(F32),
                             dram["kt_l"][bass.ds(tt, 1), :, :].rearrange("a p n -> (a p) n")).then_inc(kt_in[b], 16)
                if not first:
                    sp.wait_ge(ctx_done, t * 6 - 6)
                sp.dma_start(vx[b][:, :], dram["vx"][bass.ds(r, P), :]).then_inc(vx_in[b], 16)
            tile_pairs(sp, step)

        @blk.scalar
        def _(act):
            def step(p, b, first, last):
                t = p * 2 + b
                if not first:
                    act.wait_ge(ctx_done, t * 6 - 6)
                for g in range(6):
                    act.wait_ge(dash_full, t * 6 + g + 1)
                    for e in range(2):
                        h = 2 * g + e
                        act.activation(kp[b][:, h * M:(h + 1) * M], dash[(g + 2 * b) % 4][:, e * M:e * M + M],
                                       ACT.Exp, bias=keep["kbias"][:, bass.ds(t * HEADS + h, 1)]).then_inc(exp_done, 1)
            tile_pairs(act, step)

        @blk.vector
        def _(dve):
            dve.memset(zl[:, :], 0.0).then_inc(z_set, 1)
            dve.memset(zr[:, :], 0.0).then_inc(z_set, 1)

            def step(p, b, first, last):
                t = p * 2 + b
                for g in range(6):
                    dve.wait_ge(exp_done, t * 12 + 2 * g + 2)
                    kg = kp[b][:, 2 * g * M:2 * (g + 1) * M]
                    dve.tensor_scalar(kg, kg, MIX_EPS, None, ALU.add).then_inc(kp_done, 1)
            tile_pairs(dve, step)
            dve.wait_ge(ctx_done, NT * 6)
            for i in range(4):
                dve.tensor_copy(keep["ctx"][:, i * 6 * VW:(i + 1) * 6 * VW], cacc[i][:, 0:6 * VW]).then_inc(ctx_out, 1)

        @blk.tensor
        def _(pe):
            pe.wait_ge(z_set, 2)
            for i in range(4):
                pe.matmul(cacc[i][:, :], zl[:, :], zr[:, :], start=True, stop=True, skip_group_check=True)

            def dashes(t, b, g, first):
                if g == 0:
                    pe.wait_ge(kt_in[b], t * 16 + (32 - 16 * b))
                if not (first and g < 4):
                    pe.wait_ge(exp_done, t * 12 + 2 * g - 4)
                dash_pair(pe, [dash[(g + e + 2 * b) % 4] for e in range(2)], kt_h[b], kt_l[b], g,
                          keep["pj_h"], keep["pj_l"], dash_full)

            def contexts(t, b, g):
                if g == 0:
                    pe.wait_ge(vx_in[b], t * 8 + (16 - 8 * b))
                pe.wait_ge(kp_done, t * 6 + g + 1)
                for a, h in enumerate(group_heads(g)):
                    for m in range(2):
                        i = 2 * h + m
                        c = (2 * g + a) * M + m * P
                        mm = pe.matmul(cacc[i // 6][:, (i % 6) * VW:(i % 6 + 1) * VW], kp[b][:, c:c + P], vx[b][:, h * VW:(h + 1) * VW],
                                       start=False, stop=True, skip_group_check=True)
                mm.then_inc(ctx_done, 1)

            for g in (0, 2, 4):
                dashes(0, 0, g, True)

            def step(p, b, first, last):
                t = p * 2 + b
                for g in range(6):
                    contexts(t, b, g)
                    if not last and g % 2 == 0:
                        dashes(t + 1, 1 - b, g, False)
            tile_pairs(pe, step)


def setup(nc, io, keep, s):
    keep["ident"] = s.sb("ident", [P, P])
    keep["ranges"], keep["longest"] = s.sb("ranges", [1, 2 * P], I32), s.sb("longest", [1, 1], I32)
    keep["rows_in"] = [[s.stack.enter_context(nc.semaphore(f"rows_in{n}_{b}")) for b in range(4)] for n in range(2)]
    keep["rows_in_general"] = [s.stack.enter_context(nc.semaphore(f"rows_in_general{n}")) for n in range(2)]
    keep["minus_half"] = s.sb("minus_half", [P, 1])
    keep["ln_eps"] = s.sb("ln_eps", [P, 1])
    keep["minus_one"] = s.sb("minus_one", [P, 1])
    with Pool(nc, "st") as t:
        loaded, made = t.sem("loaded"), t.sem("made")
        blk = t.block()

        @blk.sync
        def _(sp):
            sp.dma_start(keep["ident"][:, :], io["ident"]).then_inc(loaded, 16)
            sp.wait_ge(loaded, 16)

        @blk.vector
        def _(dve):
            dve.memset(keep["minus_half"][:, :], -0.5).then_inc(made, 1)
            dve.memset(keep["ln_eps"][:, :], LN_EPS).then_inc(made, 1)
            dve.memset(keep["minus_one"][:, :], -1.0).then_inc(made, 1)


def setup_mix(nc, io, keep, s):
    keep["pj_h"], keep["pj_l"] = s.sb("pj_h", [P, M], F32R), s.sb("pj_l", [P, M], F32R)
    keep["kmx"] = s.sb("kmx", [P, NT * 6])
    keep["diag"] = s.sb("diag", [P, NT * 2 * HEADS])
    keep["negm"] = s.sb("negm", [P, 1])
    keep["kbias"] = s.sb("kbias", [P, NT * HEADS])
    keep["ctx"] = s.sb("ctx", [P, HEADS * 2 * VW])
    with Pool(nc, "sm") as t:
        raw, scaled = t.sb("raw", [P, M]), t.sb("scaled", [P, M])
        loaded, scale_done, hi_done, lo_done = (t.sem(n) for n in ("loaded", "scale_done", "hi_done", "lo_done"))
        blk = t.block()

        @blk.sync
        def _(sp):
            for e in range(2):
                sp.dma_start(raw[e * DH:(e + 1) * DH, :], io["projT"]).then_inc(loaded, 16)

        @blk.vector
        def _(dve):
            dve.wait_ge(loaded, 32)
            dve.tensor_scalar(scaled[:, :], raw[:, :], DH ** -0.25, None, ALU.mult).then_inc(scale_done, 1)
            dve.wait_ge(scale_done, 1)
            dve.tensor_copy(keep["pj_h"][:, :], scaled[:, :]).then_inc(hi_done, 1)
            dve.wait_ge(hi_done, 1)
            dve.tensor_tensor(keep["pj_l"][:, :], scaled[:, :], keep["pj_h"][:, :].bitcast(F32),
                              ALU.subtract).then_inc(lo_done, 1)


def phase_c(nc, io, dram, keep):
    with Pool(nc, "c") as s:
        ranges = EdgeRanges(nc, io, dram, keep, s)
        w_hi, w_lo = s.sb("w_hi", [P, KC, D], F32R), s.sb("w_lo", [P, KC, D], F32R)
        split_weights(nc, "cs", [(io["wprojT"][k * P:(k + 1) * P, :], w_hi[:, k, :], w_lo[:, k, :])
                                 for k in range(KC)], D)
        ident, ctx = keep["ident"], keep["ctx"]
        qt_h, qt_l = s.sb2("qt_h", [P, KC, P], F32R), s.sb2("qt_l", [P, KC, P], F32R)
        qp = s.sb2("qp", [P, HEADS * M])
        qpt = s.sb2("qpt", [P, 4 * P])
        mx, nb = s.sb("mx", [P, 2]), s.sb2("nb", [P, HEADS])
        rden = s.sb("rden", [P, HEADS])
        att = s.sb2("att", [P, D])
        at_h, at_l = s.sb("at_h", [P, KC, P], F32R), s.sb("at_l", [P, KC, P], F32R)
        x = s.sb2("x", [P, D])
        res = s.sb2("res", [P, D])
        bias = s.sb("bias", [P, D])
        eps = s.sb("eps", [P, 1])
        dash = [s.bank(f"dash{i}") for i in range(2)]
        turn = [s.bank(f"turn{i}") for i in range(2)]
        num = [s.bank(f"num{i}") for i in range(2)]
        proj = [s.bank(f"proj{i}") for i in range(2)]

        bias_in, q_in, x_in, res_out = s.sem("bias_in"), s.sem2("q_in"), s.sem2("x_in"), s.sem2("res_out")
        (eps_set, dash_full, mx_done, nb_done, exp_done, turn_full, qpa_done, qpd_done, num_full, rden_done,
         att_done, atr_full, ahi_done, alo_done, proj_full, xb_done, res_done) = (s.sem(n) for n in (
             "eps_set", "dash_full", "mx_done", "nb_done", "exp_done", "turn_full", "qpa_done", "qpd_done",
             "num_full", "rden_done", "att_done", "atr_full", "ahi_done", "alo_done", "proj_full", "xb_done",
             "res_done"))
        blk = s.block()

        @blk.sync
        def _(sp):
            sp.dma_start(bias[:, :], io["bproj"].partition_broadcast(P)).then_inc(bias_in, 16)
            ranges.fetch(sp)

            def load(p, b, first, last):
                t = p * 2 + b
                tt = sp.snap(t) if not first else t
                if not first:
                    sp.wait_ge(dash_full, t * 6 - 6)
                for i, (buf, src) in enumerate(((qt_h, "qt_h"), (qt_l, "qt_l"))):
                    sp.dma_start(buf[b][:, :, :].rearrange("p k n -> p (k n)").bitcast(F32),
                                 dram[src][bass.ds(tt, 1), :, :].rearrange("a p n -> (a p) n")).then_inc(q_in[b], 16)

            def load_x(p, b, first):
                t = p * 2 + b
                r = sp.snap(t * P) if not isinstance(p, int) else t * P
                if not first:
                    sp.wait_ge(res_done, t * 2 - 2)
                sp.dma_start(x[b][:, :], io["x"][bass.ds(r, P), :]).then_inc(x_in[b], 16)

            def store_res(p, b):
                t = p * 2 + b
                r = sp.snap(t * P) if not isinstance(p, int) else t * P
                sp.wait_ge(res_done, t * 2 + 2)
                sp.dma_start(dram["res"][bass.ds(r, P), :], res[b][:, :]).then_inc(res_out[b], 16)

            def rest(p, b, first, last):
                if not last:
                    load_x(p if b == 0 else p + 1, 1 - b, first and b == 0)
                if not (first and b == 0):
                    store_res(p if b == 1 else p - 1, 1 - b)

            def start():
                load_x(0, 0, True)
                ranges.spread(sp)

            loads_first(sp, load, rest, start)
            ranges.store_row(sp)
            store_res(NT // 2, 0)
            sp.wait_ge(res_out[0], 16 * (NT - NT // 2))
            sp.wait_ge(res_out[1], 16 * (NT // 2))

        @blk.gpsimd
        def _(pool):
            pool.memset(eps[:, :], MIX_EPS).then_inc(eps_set, 1)
            pool.wait_ge(bias_in, 16)

            def step(p, b, first, last):
                t = p * 2 + b
                pool.wait_ge(x_in[b], t * 8 + (16 - 8 * b))
                pool.tensor_tensor(x[b][:, :], x[b][:, :], bias[:, :], ALU.add).then_inc(xb_done, 1)
            tile_pairs(pool, step)

        @blk.scalar
        def _(act):
            def exps(t, b, g, first):
                act.wait_ge(nb_done, t * 6 + g + 1)
                if g == 0 and not first:
                    act.wait_ge(turn_full, t * 6 - 6)
                for h in (2 * g, 2 * g + 1):
                    act.activation(qp[b][:, h * M:(h + 1) * M], dash[g % 2][:, (h % 2) * M:(h % 2 + 1) * M], ACT.Exp,
                                   bias=nb[b][:, h:h + 1]).then_inc(exp_done, 1)

            def att_high(t):
                act.wait_ge(proj_full, t * 2)
                for g in range(2):
                    act.wait_ge(atr_full, t * 2 + g + 1)
                    act.activation(at_h[:, 3 * g:3 * g + 3, :].rearrange("p k n -> p (k n)"), proj[g][:, 0:384],
                                   ACT.Copy).then_inc(ahi_done, 1)

            act.wait_ge(eps_set, 1)
            for g in range(6):
                exps(0, 0, g, True)

            def step(p, b, first, last):
                t = p * 2 + b
                for g in range(6):
                    if not last and g > 0:
                        exps(t + 1, 1 - b, g, first and b == 0)
                    if g % 2 == 0:
                        act.wait_ge(turn_full, t * 6 + g + 1)
                        if not (first and b == 0 and g < 2):
                            act.wait_ge(num_full, t * 6 + g - 1)
                        act.activation(qpt[0][:, :], turn[0][:, :], ACT.Identity, bias=eps[:, 0:1]).then_inc(qpa_done, 1)
                    if not last and g == 0:
                        exps(t + 1, 1 - b, 0, first and b == 0)
                    if g == 1 and not (first and b == 0):
                        att_high(t - 1)
            tile_pairs(act, step)
            att_high(NT - 1)

        @blk.vector
        def _(dve):
            def maxima(t, b, g, first):
                dve.wait_ge(dash_full, t * 6 + g + 1)
                dve.wait_ge(nb_done, t * 6 + g)
                dve.tensor_reduce(mx[:, :], dash[g % 2][:, :].rearrange("p (e m) -> p e m", m=M), AX.X,
                                  ALU.max).then_inc(mx_done, 1)
                dve.wait_ge(mx_done, t * 6 + g + 1)
                if g == 0 and not first:
                    dve.wait_ge(exp_done, t * 12 - 12)
                dve.scalar_tensor_tensor(out=nb[b][:, 2 * g:2 * g + 2], in0=mx[:, :], scalar=-1.0,
                                         in1=keep["diag"][:, bass.ds(t * 2 * HEADS + 2 * g, 2)],
                                         op0=ALU.mult, op1=ALU.add).then_inc(nb_done, 1)

            def att_low(t):
                for g in range(2):
                    dve.wait_ge(ahi_done, t * 2 + g + 1)
                    dve.tensor_tensor(at_l[:, 3 * g:3 * g + 3, :].rearrange("p k n -> p (k n)"), proj[g][:, 0:384],
                                      at_h[:, 3 * g:3 * g + 3, :].rearrange("p k n -> p (k n)").bitcast(F32),
                                      ALU.subtract).then_inc(alo_done, 1)

            def residual(t, b, c, first):
                if c == 0:
                    dve.wait_ge(xb_done, t + 1)
                    if not first:
                        dve.wait_ge(res_out[b], t * 8 - 8 * b)
                dve.wait_ge(proj_full, t * 2 + c + 1)
                o = slice(384 * c, 384 * c + 384)
                dve.tensor_tensor(res[b][:, o], proj[c][:, 0:384], x[b][:, o], ALU.add).then_inc(res_done, 1)

            def divide(t, b, first):
                dve.wait_ge(num_full, t * 6 + 6)
                dve.wait_ge(att_done, t * 2)
                for i in range(2):
                    nv = num[i][:, 0:6 * VW].rearrange("p (h d) -> p h d", d=VW)
                    dve.reciprocal(rden[:, 6 * i:6 * i + 6].rearrange("p (h a) -> p h a", a=1), nv[:, :, DH:VW]).then_inc(rden_done, 1)
                dve.wait_ge(rden_done, t * 2 + 2)
                if not first:
                    dve.wait_ge(atr_full, t * 2 - 2)
                for i in range(2):
                    nv = num[i][:, 0:6 * VW].rearrange("p (h d) -> p h d", d=VW)
                    dve.tensor_tensor(att[b][:, 384 * i:384 * i + 384].rearrange("p (h d) -> p h d", d=DH), nv[:, :, 0:DH],
                                      rden[:, 6 * i:6 * i + 6].unsqueeze(2).to_broadcast([P, 6, DH]),
                                      ALU.mult).then_inc(att_done, 1)

            ranges.blocks(dve)
            for g in range(6):
                maxima(0, 0, g, True)

            def step(p, b, first, last):
                t = p * 2 + b
                for g in range(6):
                    if not last:
                        maxima(t + 1, 1 - b, g, first and b == 0)
                    if g % 2 == 1:
                        dve.wait_ge(turn_full, t * 6 + g + 1)
                        if not (first and b == 0 and g < 2):
                            dve.wait_ge(num_full, t * 6 + g - 1)
                        dve.tensor_scalar(qpt[1][:, :], turn[1][:, :], MIX_EPS, None, ALU.add).then_inc(qpd_done, 1)
                    if g == 1 and not (first and b == 0):
                        att_low(t - 1)
                    if g == 4 and not (first and b == 0):
                        residual(t - 1, 1 - b, 0, first)
                if not (first and b == 0):
                    residual(t - 1, 1 - b, 1, first)
                divide(t, b, first)
                if first and b == 1:
                    ranges.end(dve, 0)
                    ranges.end(dve, 1)
            tile_pairs(dve, step)
            att_low(NT - 1)
            for c in range(2):
                residual(NT - 1, 0, c, False)
            ranges.longest(dve)

        @blk.tensor
        def _(pe):
            def dashes(t, b, g):
                if g == 0:
                    pe.wait_ge(q_in[b], t * 16 + (32 - 16 * b))
                dash_pair(pe, dash, qt_h[b], qt_l[b], g, keep["pj_h"], keep["pj_l"], dash_full)

            def turns(t, b, g, first):
                pe.wait_ge(exp_done, t * 12 + 2 * g + 2)
                if not (first and b == 0 and g < 2):
                    pe.wait_ge((qpa_done, qpd_done)[g % 2], t * 3 + g // 2)
                for i in range(4):
                    mm = pe.transpose(turn[g % 2][:, i * P:(i + 1) * P],
                                      qp[b][:, 2 * g * M + i * P:2 * g * M + (i + 1) * P], ident[:, :])
                mm.then_inc(turn_full, 1)

            def heads_out(t, b, g):
                pe.wait_ge((qpa_done, qpd_done)[g % 2], t * 3 + g // 2 + 1)
                if g == 0:
                    pe.wait_ge(att_done, t * 2)
                for a, h in enumerate(group_heads(g)):
                    for m in range(2):
                        c = (h % 6) * VW
                        mm = pe.matmul(num[h // 6][:, c:c + VW], qpt[g % 2][:, (2 * a + m) * P:(2 * a + m + 1) * P],
                                       ctx[:, (2 * h + m) * VW:(2 * h + m + 1) * VW], start=(m == 0), stop=(m == 1),
                                       skip_group_check=True)
                mm.then_inc(num_full, 1)

            def att_turns(t, b):
                for g in range(2):
                    pe.wait_ge(att_done, t * 2 + 2)
                    pe.wait_ge(res_done, t * 2)
                    for i in range(3):
                        k = 3 * g + i
                        mm = pe.transpose(proj[g][:, i * P:(i + 1) * P], att[b][:, k * P:(k + 1) * P], ident[:, :])
                    mm.then_inc(atr_full, 1)

            def project(t, part):
                if part == 0:
                    pe.wait_ge(alo_done, t * 2 + 2)
                c = part // 2
                o = slice(384 * c, 384 * c + 384)
                for k in range(3 * (part % 2), 3 * (part % 2) + 3):
                    pe.matmul(proj[c][:, 0:384], at_h[:, k, :], w_hi[:, k, o], start=(k == 0), stop=False, skip_group_check=True)
                    pe.matmul(proj[c][:, 0:384], at_h[:, k, :], w_lo[:, k, o], start=False, stop=False, skip_group_check=True)
                    mm = pe.matmul(proj[c][:, 0:384], at_l[:, k, :], w_hi[:, k, o], start=False, stop=(k == KC - 1),
                                   skip_group_check=True)
                if part % 2 == 1:
                    mm.then_inc(proj_full, 1)

            for g in (0, 2, 4):
                if g:
                    pe.wait_ge(exp_done, 2 * g)
                dashes(0, 0, g)

            def step(p, b, first, last):
                t = p * 2 + b
                for g in range(6):
                    if not last and g % 2 == 0:
                        pe.wait_ge(exp_done, t * 12 + 2 * g + 12)
                        dashes(t + 1, 1 - b, g)
                    turns(t, b, g, first)
                    if g >= 1:
                        heads_out(t, b, g - 1)
                    if g == 1 and not (first and b == 0):
                        att_turns(t - 1, 1 - b)
                    if g >= 2 and not (first and b == 0):
                        project(t - 1, g - 2)
                heads_out(t, b, 5)
            tile_pairs(pe, step)
            att_turns(NT - 1, 0)
            for part in range(4):
                project(NT - 1, part)


def step_quads(eng, step, quads=NT):
    for b in range(4):
        step(0, b, True, False)
    with eng.Fori(1, quads - 1) as q:
        for b in range(4):
            step(q, b, False, False)
    for b in range(4):
        step(quads - 1, b, False, True)


def aggregate_four_heads(nc, io, dram, keep):
    H, HD, TROW = GH, GH * TW, TROW1
    tab, ald_d = dram["tab1"], dram["ald1"]
    HALF = ((0, 384), (384, D + 1 - 384))
    with Pool(nc, "e") as s:
        ids = s.sb("ids", [P, NP])
        pick = s.sb("pick", [P, 2 * GH])
        ones = s.sb("ones", [P, P])
        e = [s.sb(f"e{b}", [P, 2, SLOTS], I32) for b in range(4)]
        rows = [s.sb(f"rows{b}", [P, SLOTS, TROW]) for b in range(4)]
        ald = [s.sb(f"ald{b}", [P, HD]) for b in range(4)]
        own = [s.sb(f"own{b}", [HD, TROW]) for b in range(4)]
        mask, pen = s.sb("mask", [P, SLOTS, TW]), s.sb("pen", [P, SLOTS, TW])
        z = s.sb("z", [P, SLOTS, HD])
        zmax = s.sb("zmax", [P, HD])
        mcol, zs, zself, m2, dself = (s.sb(n, [HD, 1]) for n in ("mcol", "zs", "zself", "m2", "dself"))
        junk = s.sb("junk", [HD, 2 * GH])
        dg = s.sb("dg", [HD, HD])
        wt = s.sb2("wt", [P, SLOTS, HD])
        wself = [s.sb(f"wself{b}", [HD, 1]) for b in range(4)]
        acc = s.sb("acc", [HD, D + 1])
        den, rden = s.sb("den", [HD, 1]), s.sb("rden", [HD, 1])
        outb = s.sb2("outb", [HD, D])
        zt, mrow = s.bank("zt"), s.bank("mrow")
        num = [[s.bank(f"num{b}{i}") for i in range(2)] for b in range(2)]
        const_in = s.sem("const_in")
        e_in, ald_in, own_in = ([s.sem(f"{n}{b}") for b in range(4)] for n in ("e_in", "ald_in", "own_in"))
        rows_in = keep["rows_in"][0]
        stored = s.sem2("stored")
        (load_go, ones_set, gather_go, mask_done, pen_done, z1_done, z2_done, z3_done, zmax_done, zt_full, mcol_done, zs_done,
         zself_done, m2_done, dg_done, dself_done, mrow_full, shift_done, wself_done, exp_done, num_full, acc_done,
         den_done, rden_done, out_done) = (s.sem(n) for n in (
             "load_go", "ones_set", "gather_go", "mask_done", "pen_done", "z1_done", "z2_done", "z3_done", "zmax_done", "zt_full",
             "mcol_done", "zs_done", "zself_done", "m2_done", "dg_done", "dself_done", "mrow_full", "shift_done",
             "wself_done", "exp_done", "num_full", "acc_done", "den_done", "rden_done", "out_done"))
        blk = s.block()

        def fits(eng):
            return eng.value_load(keep["longest"][0:1, 0:1], min_val=0, max_val=2 * EP) <= CAP

        @blk.sync
        def _(sp):
            with sp.If(fits(sp)):
                sp.dma_start(ids[:, :], io["node_ids"].partition_broadcast(P)).then_inc(const_in, 16)
                sp.dma_start(pick[:, :], io["head_pick"]).then_inc(const_in, 16)

                def edges(q, b, first):
                    T = q * 4 + b
                    lo = sp.value_load(keep["ranges"][0:1, bass.ds(T * 2, 1)], min_val=0, max_val=EP)
                    if not first:
                        sp.wait_ge(num_full, T * 2 - 6)
                        sp.sem_inc(load_go, 1)
                    sp.dma_start(e[b][:, :, :], io["edges"][:, bass.ds(lo, CAP)].rearrange("s (p c) -> p s c", c=SLOTS)).then_inc(e_in[b], 16)

                def own_rows(q, b):
                    T = q * 4 + b
                    n0 = sp.snap(T * TW) if not isinstance(q, int) else T * TW
                    if not isinstance(q, int) or q:
                        sp.wait_ge(acc_done, T * 2 - 6)
                        sp.sem_inc(load_go, 1)
                    sp.dma_start(ald[b][:, :], ald_d[bass.ds(n0, TW), :].rearrange("d h -> (d h)").partition_broadcast(P)).then_inc(ald_in[b], 16)
                    for h in range(H):
                        sp.dma_start(own[b][h * TW:(h + 1) * TW, :], tab[bass.ds(n0, TW), :]).then_inc(own_in[b], 16)

                def step(q, b, first, last):
                    edges(q, b, first)
                    if not (first and b == 0):
                        own_rows(*((q, b - 1) if b > 0 else (q - 1, 3)))
                    if last and b == 3:
                        own_rows(q, b)
                step_quads(sp, step)

        @blk.gpsimd
        def _(pool):
            with pool.If(fits(pool)):
                pool.memset(ones[:, :], 1.0).then_inc(ones_set, 1)

                def step(q, b, first, last):
                    T = q * 4 + b
                    pool.wait_ge(e_in[b], q * 16 + 16)
                    pool.sem_inc(gather_go, 1)
                    if not first:
                        pool.wait_ge(num_full, T * 2 - 6)
                        pool.sem_inc(gather_go, 1)
                    for c in range(SLOTS):
                        pool.indirect_dma_start(rows[b][:, c, :], None, tab,
                                                bass.IndirectOffsetOnAxis(ap=e[b][:, 0, c:c + 1], axis=0)).then_inc(rows_in[b], 16)
                step_quads(pool, step)

        @blk.vector
        def _(dve):
            with dve.If(fits(dve)):
                dve.wait_ge(const_in, 32)

                def match(q, b):
                    T = q * 4 + b
                    dve.wait_ge(e_in[b], q * 16 + 16)
                    dve.tensor_tensor(mask[:, :, :], e[b][:, 1, :].unsqueeze(2).to_broadcast([P, SLOTS, TW]),
                                      ids[:, bass.ds(T * TW, TW)].unsqueeze(1).to_broadcast([P, SLOTS, TW]),
                                      ALU.is_equal).then_inc(mask_done, 1)

                def penalty(q, b):
                    T = q * 4 + b
                    dve.wait_ge(mask_done, T + 1)
                    dve.wait_ge(z1_done, T)
                    dve.tensor_scalar(pen[:, :, :], mask[:, :, :], BIG, -BIG, ALU.mult, ALU.add).then_inc(pen_done, 1)

                def logits(q, b):
                    T = q * 4 + b
                    dve.wait_ge(rows_in[b], q * (16 * SLOTS) + 16 * SLOTS)
                    dve.wait_ge(ald_in[b], q * 16 + 16)
                    dve.wait_ge(pen_done, T + 1)
                    dve.wait_ge(shift_done, T)
                    z4 = z[:, :, :].rearrange("p c (h d) -> p c h d", h=H)
                    dve.tensor_tensor(z4, rows[b][:, :, D + 1:D + 1 + H].unsqueeze(3).to_broadcast([P, SLOTS, H, TW]),
                                      pen[:, :, :].unsqueeze(2).to_broadcast([P, SLOTS, H, TW]), ALU.add).then_inc(z1_done, 1)
                    dve.wait_ge(z1_done, T + 1)
                    dve.tensor_tensor(z4, z4, ald[b][:, :].rearrange("p (d h) -> p h d", h=H).unsqueeze(1)
                                      .to_broadcast([P, SLOTS, H, TW]), ALU.add).then_inc(z2_done, 1)
                    dve.wait_ge(z2_done, T + 1)
                    zf = z[:, :, :].rearrange("p c n -> p (c n)")
                    dve.scalar_tensor_tensor(out=zf, in0=zf, scalar=SLOPE, in1=zf, op0=ALU.mult, op1=ALU.max).then_inc(z3_done, 1)
                    dve.wait_ge(z3_done, T + 1)
                    dve.wait_ge(zt_full, T)
                    dve.tensor_reduce(zmax[:, :], z[:, :, :].rearrange("p c n -> p n c"), AX.X, ALU.max).then_inc(zmax_done, 1)

                def maxima(q, b, last):
                    q1, b1 = (q, b + 1) if b < 3 else (q + 1, 0)
                    T = q * 4 + b
                    dve.wait_ge(own_in[b], q * (16 * H) + 16 * H)
                    dve.wait_ge(zself_done, T)
                    dve.tensor_tensor_reduce(junk[:, :], own[b][:, D + 1:D + 1 + 2 * H], pick[:, :], 1.0, 0.0, ALU.mult,
                                             ALU.add, zs[:, :]).then_inc(zs_done, 1)
                    dve.wait_ge(zs_done, T + 1)
                    dve.wait_ge(dself_done, T)
                    dve.scalar_tensor_tensor(out=zself[:, :], in0=zs[:, :], scalar=SLOPE, in1=zs[:, :], op0=ALU.mult,
                                             op1=ALU.max).then_inc(zself_done, 1)
                    if not last:
                        match(q1, b1)
                    dve.wait_ge(zt_full, T + 1)
                    dve.tensor_reduce(mcol[:, :], zt[0:HD, 0:P], AX.X, ALU.max).then_inc(mcol_done, 1)
                    dve.wait_ge(mcol_done, T + 1)
                    dve.wait_ge(zself_done, T + 1)
                    dve.wait_ge(dg_done, T)
                    dve.tensor_tensor(m2[:, :], mcol[:, :], zself[:, :], ALU.max).then_inc(m2_done, 1)
                    dve.wait_ge(m2_done, T + 1)
                    dve.wait_ge(mrow_full, T)
                    dve.tensor_scalar(dg[:, :], keep["ident"][0:HD, 0:HD], m2[:, 0:1], None, ALU.mult).then_inc(dg_done, 1)
                    dve.wait_ge(wself_done, T)
                    dve.tensor_tensor(dself[:, :], zself[:, :], m2[:, :], ALU.subtract).then_inc(dself_done, 1)
                    if not last:
                        penalty(q1, b1)

                def shift(q, b, first):
                    T = q * 4 + b
                    dve.wait_ge(mrow_full, T + 1)
                    if not first or b >= 2:
                        dve.wait_ge(num_full, T * 2 - 2)
                    dve.tensor_tensor(wt[b % 2][:, :, :], z[:, :, :], mrow[:, 0:HD].unsqueeze(1).to_broadcast([P, SLOTS, HD]),
                                      ALU.subtract).then_inc(shift_done, 1)

                def sums(q, b):
                    T = q * 4 + b
                    dve.wait_ge(wself_done, T + 1)
                    dve.wait_ge(out_done, T)
                    dve.wait_ge(num_full, T * 2 + 2)
                    for i, (a, n) in reversed(list(enumerate(HALF))):
                        dve.scalar_tensor_tensor(out=acc[:, a:a + n], in0=own[b][:, a:a + n], scalar=wself[b][:, 0:1],
                                                 in1=num[b % 2][i][0:HD, 0:n], op0=ALU.mult, op1=ALU.add).then_inc(acc_done, 1)
                    dve.wait_ge(acc_done, T * 2 + 1)
                    dve.tensor_scalar(den[:, :], acc[:, D:D + 1], 1e-16, None, ALU.add).then_inc(den_done, 1)
                    dve.wait_ge(den_done, T + 1)
                    dve.reciprocal(rden[:, :], den[:, :]).then_inc(rden_done, 1)

                match(0, 0)
                penalty(0, 0)
                logits(0, 0)
                maxima(0, 0, False)
                shift(0, 0, True)

                def step(q, b, first, last):
                    q1, b1 = (q, b + 1) if b < 3 else (q + 1, 0)
                    if not (last and b == 3):
                        logits(q1, b1)
                        maxima(q1, b1, last and b == 2)
                    if not (last and b == 3):
                        shift(q1, b1, first and b < 3)
                    if not (first and b == 0):
                        sums(*((q, b - 1) if b > 0 else (q - 1, 3)))
                step_quads(dve, step)
                sums(NT - 1, 3)

        @blk.scalar
        def _(act):
            with act.If(fits(act)):
                def exps(q, b):
                    T = q * 4 + b
                    act.wait_ge(dself_done, T + 1)
                    if not isinstance(q, int) or q:
                        act.wait_ge(acc_done, T * 2 - 6)
                    act.activation(wself[b][:, :], dself[:, :], ACT.Exp).then_inc(wself_done, 1)
                    act.wait_ge(shift_done, T + 1)
                    for c in range(SLOTS):
                        act.activation(wt[b % 2][:, c, :], wt[b % 2][:, c, :], ACT.Exp).then_inc(exp_done, 1)

                exps(0, 0)

                def result(q, b):
                    T = q * 4 + b
                    n0 = act.snap(T * TW) if not isinstance(q, int) else T * TW
                    act.wait_ge(acc_done, T * 2 + 2)
                    act.wait_ge(rden_done, T + 1)
                    if not isinstance(q, int) or q or b >= 2:
                        act.wait_ge(stored[b % 2], q * (64 * 2) + 64 * (b // 2))
                    act.activation(outb[b % 2][:, :], acc[:, 0:D], ACT.Copy, scale=rden[:, 0:1]).then_inc(out_done, 1)
                    act.wait_ge(out_done, T + 1)
                    for h in range(H):
                        act.dma_start(dram["agg1"][h, bass.ds(n0, TW), :], outb[b % 2][h * TW:(h + 1) * TW, :]).then_inc(stored[b % 2], 16)

                def step(q, b, first, last):
                    q1, b1 = (q, b + 1) if b < 3 else (q + 1, 0)
                    if not (last and b == 3):
                        exps(q1, b1)
                    if not (first and b == 0):
                        result(*((q, b - 1) if b > 0 else (q - 1, 3)))
                step_quads(act, step)
                result(NT - 1, 3)
                for b in range(2):
                    act.wait_ge(stored[b], 16 * H * 2 * NT)

        @blk.tensor
        def _(pe):
            with pe.If(fits(pe)):
                def turn(q, b):
                    T = q * 4 + b
                    pe.wait_ge(zmax_done, T + 1)
                    pe.wait_ge(mcol_done, T)
                    pe.transpose(zt[0:HD, 0:P], zmax[:, :], keep["ident"][:, :]).then_inc(zt_full, 1)

                def spread(q, b):
                    T = q * 4 + b
                    pe.wait_ge(dg_done, T + 1)
                    pe.wait_ge(shift_done, T)
                    pe.matmul(mrow[:, 0:HD], ones[0:HD, :], dg[:, :], start=True, stop=True).then_inc(mrow_full, 1)

                def sum_slot(q, b, c, first, between):
                    T = q * 4 + b
                    pe.wait_ge(exp_done, T * SLOTS + c + 1)
                    if c == 0 and (not first or b >= 2):
                        pe.wait_ge(acc_done, T * 2 - 2)
                    for i, (a, n) in enumerate(HALF):
                        mm = pe.matmul(num[b % 2][i][0:HD, 0:n], wt[b % 2][:, c, :], rows[b][:, c, a:a + n], start=(c == 0),
                                       stop=(c == SLOTS - 1))
                        if c == SLOTS - 1:
                            mm.then_inc(num_full, 1)
                        if i == 0:
                            between()

                pe.wait_ge(ones_set, 1)
                turn(0, 0)
                spread(0, 0)

                def step(q, b, first, last):
                    q1, b1 = (q, b + 1) if b < 3 else (q + 1, 0)
                    for c in range(SLOTS):
                        work = {2: turn, 3: spread}.get(c) if not (last and b == 3) else None
                        sum_slot(q, b, c, first, lambda: work(q1, b1) if work else None)
                step_quads(pe, step)


def phase_f(nc, io, dram, keep):
    with Pool(nc, "f") as s:
        w_hi, w_lo = s.sb("w_hi", [P, KC, HID], F32R), s.sb("w_lo", [P, KC, HID], F32R)
        split_weights(nc, "fs", [(io["W1"][k * P:(k + 1) * P, :], w_hi[:, k, :], w_lo[:, k, :]) for k in range(KC)], HID)
        ident = keep["ident"]
        NK = GH * KC
        a_in = s.sb2("a_in", [P, GH, D])
        a_h, a_l = s.sb2("a_h", [P, NK, P], F32R), s.sb2("a_l", [P, NK, P], F32R)
        b1p = s.sb("b1p", [P, HID])
        r1 = s.sb("r1", [P, HID])
        e = s.sb2("e", [P, HID])
        turn = [s.bank(f"turn{i}") for i in range(4)]
        prod = [s.bank(f"prod{i}") for i in range(GH)]
        b_in, in_sem, out_sem = s.sem("b_in"), s.sem2("in"), s.sem2("out")
        bias_done, turn_full, hi_done, lo_done, prod_full, r1_done, exp_done, elu_done = (s.sem(n) for n in (
            "bias_done", "turn_full", "hi_done", "lo_done", "prod_full", "r1_done", "exp_done", "elu_done"))
        blk = s.block()

        @blk.sync
        def _(sp):
            sp.dma_start(b1p[:, :], io["b1"].partition_broadcast(P)).then_inc(b_in, 16)

            def load(p, b, first, last):
                t = p * 2 + b
                r = sp.snap(t * P) if not first else t * P
                if not first:
                    sp.wait_ge(turn_full, t * 8 - 8)
                sp.dma_start(a_in[b][:, :, :], dram["agg1"][:, bass.ds(r, P), :].rearrange("h p n -> p h n")).then_inc(in_sem[b], 16)

            def store(p, b, first, last):
                t = p * 2 + b
                r = sp.snap(t * P) if not first else t * P
                sp.wait_ge(elu_done, t * 4 + 4)
                sp.dma_start(dram["h1"][bass.ds(r, P), :], e[b][:, :]).then_inc(out_sem[b], 16)
            loads_first(sp, load, store)
            sp.wait_ge(out_sem[0], 16 * (NT - NT // 2))
            sp.wait_ge(out_sem[1], 16 * (NT // 2))

        @blk.scalar
        def _(act):
            def high(t, b, g, first):
                act.wait_ge(turn_full, t * 8 + g + 1)
                if g == 0 and not first:
                    act.wait_ge(prod_full, t * 4 - 4)
                act.activation(a_h[b][:, 3 * g:3 * g + 3, :].rearrange("p k n -> p (k n)"), turn[g % 4][:, 0:384],
                               ACT.Copy).then_inc(hi_done, 1)

            for g in range(8):
                high(0, 0, g, True)

            def step(p, b, first, last):
                t = p * 2 + b
                for h in range(GH):
                    if not last:
                        high(t + 1, 1 - b, 2 * h, first and b == 0)
                        high(t + 1, 1 - b, 2 * h + 1, first and b == 0)
                    act.wait_ge(r1_done, t * 4 + h + 1)
                    if h == 0 and not first:
                        act.wait_ge(out_sem[b], t * 8 - 8 * b)
                    c = slice(h * GC, (h + 1) * GC)
                    act.activation(e[b][:, c], r1[:, c], ACT.Exp, bias=keep["minus_one"][:, 0:1]).then_inc(exp_done, 1)
            tile_pairs(act, step)

        @blk.vector
        def _(dve):
            def low(t, b, g):
                dve.wait_ge(hi_done, t * 8 + g + 1)
                o = a_h[b][:, 3 * g:3 * g + 3, :].rearrange("p k n -> p (k n)")
                dve.tensor_tensor(a_l[b][:, 3 * g:3 * g + 3, :].rearrange("p k n -> p (k n)"), turn[g % 4][:, 0:384],
                                  o.bitcast(F32), ALU.subtract).then_inc(lo_done, 1)

            def elu(t, b, h):
                c = slice(h * GC, (h + 1) * GC)
                dve.wait_ge(exp_done, t * 4 + h + 1)
                dve.scalar_tensor_tensor(out=e[b][:, c], in0=e[b][:, c], scalar=1.0, in1=r1[:, c], op0=ALU.min,
                                         op1=ALU.max).then_inc(elu_done, 1)

            dve.wait_ge(b_in, 16)
            dve.tensor_scalar(b1p[:, :], b1p[:, :], 1.0, None, ALU.add).then_inc(bias_done, 1)
            dve.wait_ge(bias_done, 1)
            for g in range(8):
                low(0, 0, g)

            def step(p, b, first, last):
                t = p * 2 + b
                for h in range(GH):
                    c = slice(h * GC, (h + 1) * GC)
                    if not last:
                        low(t + 1, 1 - b, 2 * h)
                    dve.wait_ge(prod_full, t * 4 + h + 1)
                    if not (first and b == 0):
                        dve.wait_ge(elu_done, t * 4 + h - 3)
                    dve.tensor_tensor(r1[:, c], prod[h][:, :], b1p[:, c], ALU.add).then_inc(r1_done, 1)
                    if not last:
                        low(t + 1, 1 - b, 2 * h + 1)
                    if h:
                        elu(t, b, h - 1)
                elu(t, b, GH - 1)
            tile_pairs(dve, step)

        @blk.tensor
        def _(pe):
            def turns(t, b, g, first):
                if g == 0:
                    pe.wait_ge(in_sem[b], t * 8 + (16 - 8 * b))
                if not (first and g < 4):
                    pe.wait_ge(lo_done, t * 8 + g - 3)
                for i in range(3):
                    k = 3 * g + i
                    mm = pe.transpose(turn[g % 4][:, i * P:(i + 1) * P],
                                      a_in[b][:, k // KC, (k % KC) * P:(k % KC + 1) * P], ident[:, :])
                mm.then_inc(turn_full, 1)

            for g in range(8):
                turns(0, 0, g, True)

            def step(p, b, first, last):
                t = p * 2 + b
                for h in range(GH):
                    pe.wait_ge(lo_done, t * 8 + 2 * h + 2)
                    if not (first and b == 0):
                        pe.wait_ge(r1_done, t * 4 + h - 3)
                    ks = range(KC)
                    product3(pe, prod[h][:, :], [a_h[b][:, h * KC + k, :] for k in ks], [a_l[b][:, h * KC + k, :] for k in ks],
                             [w_hi[:, k, h * GC:(h + 1) * GC] for k in ks],
                             [w_lo[:, k, h * GC:(h + 1) * GC] for k in ks]).then_inc(prod_full, 1)
                    if not last:
                        turns(t + 1, 1 - b, 2 * h, False)
                        turns(t + 1, 1 - b, 2 * h + 1, False)
            tile_pairs(pe, step)


def phase_g(nc, io, dram, keep):
    NK = HID // P
    with Pool(nc, "g") as s:
        w_hi, w_lo = s.sb("w_hi", [P, NK, D], F32R), s.sb("w_lo", [P, NK, D], F32R)
        split_weights(nc, "gs", [(io["W2"][k * P:(k + 1) * P, :], w_hi[:, k, :], w_lo[:, k, :]) for k in range(NK)], D)
        h = s.sb2("h", [P, HID])
        h_h, h_l = s.sb2("h_h", [P, NK, P], F32R), s.sb2("h_l", [P, NK, P], F32R)
        row = s.sb2("row", [P, TROW2])
        a2 = s.sb("a2", [P, 2, D])
        junk = s.sb("junk", [P, D])
        turn = [s.bank(f"turn{i}") for i in range(4)]
        prod = [s.bank(f"prod{i}") for i in range(2)]
        a_in, in_sem, out_sem = s.sem("a_in"), s.sem2("in"), s.sem2("out")
        ones_set, turn_full, hi_done, lo_done, prod_full, row_done, dot_done = (s.sem(n) for n in (
            "ones_set", "turn_full", "hi_done", "lo_done", "prod_full", "row_done", "dot_done"))
        blk = s.block()

        @blk.sync
        def _(sp):
            for i, n in enumerate(("asrc2", "adst2")):
                sp.dma_start(a2[:, i, :], io[n].partition_broadcast(P)).then_inc(a_in, 16)

            def load(p, b, first, last):
                t = p * 2 + b
                r = sp.snap(t * P) if not first else t * P
                if not first:
                    sp.wait_ge(turn_full, t * 4 - 4)
                sp.dma_start(h[b][:, :], dram["h1"][bass.ds(r, P), :]).then_inc(in_sem[b], 16)

            def store(p, b, first, last):
                t = p * 2 + b
                r = sp.snap(t * P) if not first else t * P
                sp.wait_ge(dot_done, t * 2 + 2)
                sp.dma_start(dram["tab2"][bass.ds(r, P), :], row[b][:, :]).then_inc(out_sem[b], 16)
                sp.dma_start(dram["ald2"][bass.ds(r, P), :], row[b][:, D + 2:D + 3]).then_inc(out_sem[b], 16)
            loads_first(sp, load, store)
            sp.wait_ge(out_sem[0], 32 * (NT - NT // 2))
            sp.wait_ge(out_sem[1], 32 * (NT // 2))

        @blk.gpsimd
        def _(pool):
            for b in range(2):
                pool.memset(row[b][:, D:D + 1], 1.0).then_inc(ones_set, 1)

        @blk.scalar
        def _(act):
            def high(t, b, g, first):
                act.wait_ge(turn_full, t * 4 + g + 1)
                if g == 0 and not first:
                    act.wait_ge(prod_full, t * 2 - 2)
                act.activation(h_h[b][:, 4 * g:4 * g + 4, :].rearrange("p k n -> p (k n)"), turn[g][:, :], ACT.Identity,
                               bias=keep["minus_one"][:, 0:1]).then_inc(hi_done, 1)

            for g in range(4):
                high(0, 0, g, True)

            def step(p, b, first, last):
                t = p * 2 + b
                for c in range(2):
                    if not last:
                        high(t + 1, 1 - b, 2 * c, first and b == 0)
                        high(t + 1, 1 - b, 2 * c + 1, first and b == 0)
                    if c == 0 and not first:
                        act.wait_ge(out_sem[b], t * 16 - 16 * b)
                    act.wait_ge(prod_full, t * 2 + c + 1)
                    act.activation(row[b][:, 384 * c:384 * c + 384], prod[c][:, 0:384], ACT.Copy).then_inc(row_done, 1)
            tile_pairs(act, step)

        @blk.vector
        def _(dve):
            def low(t, b, g):
                dve.wait_ge(hi_done, t * 4 + g + 1)
                o = h_h[b][:, 4 * g:4 * g + 4, :].rearrange("p k n -> p (k n)")
                dve.scalar_tensor_tensor(out=h_l[b][:, 4 * g:4 * g + 4, :].rearrange("p k n -> p (k n)"), in0=turn[g][:, :],
                                         scalar=-1.0, in1=o.bitcast(F32), op0=ALU.add, op1=ALU.subtract).then_inc(lo_done, 1)

            dve.wait_ge(a_in, 32)
            dve.wait_ge(ones_set, 2)
            for g in range(4):
                low(0, 0, g)

            def step(p, b, first, last):
                t = p * 2 + b
                if not last:
                    for g in range(4):
                        low(t + 1, 1 - b, g)
                dve.wait_ge(row_done, t * 2 + 2)
                for i in range(2):
                    dve.wait_ge(dot_done, t * 2 + i)
                    dve.tensor_tensor_reduce(junk[:, :], row[b][:, 0:D], a2[:, i, :], 1.0, 0.0, ALU.mult, ALU.add,
                                             row[b][:, D + 1 + i:D + 2 + i]).then_inc(dot_done, 1)
            tile_pairs(dve, step)

        @blk.tensor
        def _(pe):
            def turns(t, b, g, first):
                if g == 0:
                    pe.wait_ge(in_sem[b], t * 8 + (16 - 8 * b))
                if not first:
                    pe.wait_ge(lo_done, t * 4 + g - 3)
                for i in range(4):
                    k = 4 * g + i
                    mm = pe.transpose(turn[g][:, i * P:(i + 1) * P], h[b][:, k * P:(k + 1) * P], keep["ident"][:, :])
                mm.then_inc(turn_full, 1)

            for g in range(4):
                turns(0, 0, g, True)

            def step(p, b, first, last):
                t = p * 2 + b
                pe.wait_ge(lo_done, t * 4 + 4)
                for c in range(2):
                    if not (first and b == 0):
                        pe.wait_ge(row_done, t * 2 + c - 1)
                    ks, o = range(NK), slice(384 * c, 384 * c + 384)
                    product3(pe, prod[c][:, 0:384], [h_h[b][:, k, :] for k in ks], [h_l[b][:, k, :] for k in ks],
                             [w_hi[:, k, o] for k in ks], [w_lo[:, k, o] for k in ks]).then_inc(prod_full, 1)
                    if c == 0 and not last:
                        for g in range(4):
                            turns(t + 1, 1 - b, g, False)
            tile_pairs(pe, step)


def aggregate_general(nc, io, dram, keep, layer):
    H = GH if layer == 1 else 1
    HD = H * TW
    TROW = TROW1 if layer == 1 else TROW2
    tab, ald_d = dram[f"tab{layer}"], dram[f"ald{layer}"]
    HALF = ((0, 384), (384, D + 1 - 384))
    KD = 14
    with Pool(nc, f"x{layer}") as s:
        ids, pick, ones = s.sb("ids", [P, NP]), s.sb("pick", [P, 2 * GH]), s.sb("ones", [P, P])
        e, rows = s.sb("e", [P, 2, SLOTS], I32), s.sb("rows", [P, SLOTS, TROW])
        ald, own = s.sb("ald", [P, HD]), s.sb("own", [HD, TROW])
        mask, pen = s.sb("mask", [P, SLOTS, TW]), s.sb("pen", [P, SLOTS, TW])
        z, zmax, wt = s.sb("z", [P, SLOTS, HD]), s.sb("zmax", [P, HD]), s.sb("wt", [P, SLOTS, HD])
        mcol, zs, mrun, m2, shrink, scale, den, rden = (s.sb(n, [HD, 1]) for n in (
            "mcol", "zs", "mrun", "m2", "shrink", "scale", "den", "rden"))
        junk, dg = s.sb("junk", [HD, 2 * GH]), s.sb("dg", [HD, HD])
        acc, outb = s.sb("acc", [HD, D + 1]), s.sb("outb", [HD, D])
        res, bias = s.sb("res", [TW, D]), s.sb("bias", [TW, D])
        zt, mrow = s.bank("zt"), s.bank("mrow")
        num = [s.bank(f"num{i}") for i in range(2)]
        rows_in = keep["rows_in_general"][layer - 1]
        (const_in, step_in, e_in, stored, ones_set, gather_go, load_go, state_done, state_step, group_step, zt_full,
         mrow_full, exp_done, num_full, end_step) = (s.sem(n) for n in (
             "const_in", "step_in", "e_in", "stored", "ones_set", "gather_go", "load_go", "state_done", "state_step",
             "group_step", "zt_full", "mrow_full", "exp_done", "num_full", "end_step"))
        JS, JE = 4, 4
        IN = 16 * (H + 1 + (layer == 2))
        blk = s.block()

        def too_long(eng):
            return eng.value_load(keep["longest"][0:1, 0:1], min_val=0, max_val=2 * EP) > CAP

        def groups(eng, before, group, after):
            done = eng.alloc_register(f"x{layer}_done")
            eng.reg_mov(done, 0)
            with eng.Fori(0, NP // TW) as T:
                before(T)
                lo = eng.value_load(keep["ranges"][0:1, bass.ds(T * 2, 1)], min_val=0, max_val=EP)
                hi = eng.value_load(keep["ranges"][0:1, bass.ds(T * 2 + 1, 1)], min_val=0, max_val=EP)
                with eng.Fori(lo, hi, CAP) as at:
                    n = eng.snap(done, min_val=0, max_val=NP // TW * (EP // CAP + 1))
                    group(at, n, T)
                    eng.reg_add(done, done, 1)
                after(T, eng.snap(done, min_val=0, max_val=NP // TW * (EP // CAP + 1)))

        @blk.sync
        def _(sp):
            with sp.If(too_long(sp)):
                sp.dma_start(ids[:, :], io["node_ids"].partition_broadcast(P)).then_inc(const_in, 16)
                sp.dma_start(pick[:, :], io["head_pick"]).then_inc(const_in, 16)
                sp.dma_start(bias[:, :], io["b2"].partition_broadcast(TW)).then_inc(const_in, 16)

                def before(T):
                    n0 = sp.snap(T * TW)
                    sp.wait_ge(end_step, T * JE + 1)
                    sp.sem_inc(load_go, 1)
                    sp.dma_start(ald[:, :], ald_d[bass.ds(n0, TW), :].rearrange("d h -> (d h)").partition_broadcast(P)).then_inc(step_in, 16)
                    for h in range(H):
                        sp.dma_start(own[h * TW:(h + 1) * TW, :], tab[bass.ds(n0, TW), :]).then_inc(step_in, 16)
                    if layer == 2:
                        sp.dma_start(res[:, :], dram["res"][bass.ds(n0, TW), :]).then_inc(step_in, 16)

                def group(at, n, T):
                    sp.wait_ge(group_step, n * KD + 1)
                    sp.sem_inc(load_go, 1)
                    sp.dma_start(e[:, :, :], io["edges"][:, bass.ds(at, CAP)].rearrange("s (p c) -> p s c", c=SLOTS)).then_inc(e_in, 16)

                def after(T, n):
                    n0 = sp.snap(T * TW)
                    sp.wait_ge(end_step, T * JE + JE + 1)
                    sp.sem_inc(load_go, 1)
                    for h in range(H):
                        dst_ = dram["agg1"][h, bass.ds(n0, TW), :] if layer == 1 else dram["x2"][bass.ds(n0, TW), :]
                        sp.dma_start(dst_, outb[h * TW:(h + 1) * TW, :]).then_inc(stored, 16)
                    sp.wait_ge(stored, T * (16 * H) + 16 * H)
                    sp.sem_inc(load_go, 1)
                groups(sp, before, group, after)

        @blk.gpsimd
        def _(pool):
            with pool.If(too_long(pool)):
                pool.memset(ones[:, :], 1.0).then_inc(ones_set, 1)

                def group(at, n, T):
                    pool.wait_ge(e_in, n * 16 + 16)
                    pool.sem_inc(gather_go, 1)
                    for c in range(SLOTS):
                        pool.indirect_dma_start(rows[:, c, :], None, tab,
                                                bass.IndirectOffsetOnAxis(ap=e[:, 0, c:c + 1], axis=0)).then_inc(rows_in, 16)
                groups(pool, lambda T: None, group, lambda T, n: None)

        @blk.vector
        def _(dve):
            with dve.If(too_long(dve)):
                dve.wait_ge(const_in, 48)
                dve.sem_inc(group_step, 1)
                dve.sem_inc(end_step, 1)

                def before(T):
                    dve.wait_ge(step_in, T * IN + IN)
                    if layer == 1:
                        dve.tensor_tensor_reduce(junk[:, :], own[:, D + 1:D + 1 + 2 * H], pick[:, :], 1.0, 0.0, ALU.mult,
                                                 ALU.add, zs[:, :]).then_inc(state_step, 1)
                    else:
                        dve.tensor_tensor(zs[:, :], own[:, D + 1:D + 2], own[:, D + 2:D + 3], ALU.add).then_inc(state_step, 1)
                    dve.wait_ge(state_step, T * JS + 1)
                    dve.scalar_tensor_tensor(out=mrun[:, :], in0=zs[:, :], scalar=SLOPE, in1=zs[:, :], op0=ALU.mult,
                                             op1=ALU.max).then_inc(state_step, 1)
                    dve.tensor_copy(acc[:, :], own[:, 0:D + 1]).then_inc(state_step, 1)
                    if layer == 2:
                        dve.tensor_tensor(res[:, :], res[:, :], bias[:, :], ALU.add).then_inc(state_step, 1)
                    else:
                        dve.sem_inc(state_step, 1)
                    dve.wait_ge(state_step, T * JS + JS)

                def group(at, n, T):
                    k = [0]

                    def chain(ins):
                        ins.then_inc(group_step, 1)
                        k[0] += 1
                        dve.wait_ge(group_step, n * KD + k[0] + 1)

                    dve.wait_ge(rows_in, n * (16 * SLOTS) + 16 * SLOTS)
                    chain(dve.tensor_tensor(mask[:, :, :], e[:, 1, :].unsqueeze(2).to_broadcast([P, SLOTS, TW]),
                                            ids[:, bass.ds(T * TW, TW)].unsqueeze(1).to_broadcast([P, SLOTS, TW]), ALU.is_equal))
                    chain(dve.tensor_scalar(pen[:, :, :], mask[:, :, :], BIG, -BIG, ALU.mult, ALU.add))
                    z4 = z[:, :, :].rearrange("p c (h d) -> p c h d", h=H)
                    chain(dve.tensor_tensor(z4, rows[:, :, D + 1:D + 1 + H].unsqueeze(3).to_broadcast([P, SLOTS, H, TW]),
                                            pen[:, :, :].unsqueeze(2).to_broadcast([P, SLOTS, H, TW]), ALU.add))
                    chain(dve.tensor_tensor(z4, z4, ald[:, :].rearrange("p (d h) -> p h d", h=H).unsqueeze(1)
                                            .to_broadcast([P, SLOTS, H, TW]), ALU.add))
                    zf = z[:, :, :].rearrange("p c n -> p (c n)")
                    chain(dve.scalar_tensor_tensor(out=zf, in0=zf, scalar=SLOPE, in1=zf, op0=ALU.mult, op1=ALU.max))
                    chain(dve.tensor_reduce(zmax[:, :], z[:, :, :].rearrange("p c n -> p n c"), AX.X, ALU.max))
                    dve.wait_ge(zt_full, n + 1)
                    chain(dve.tensor_reduce(mcol[:, :], zt[0:HD, 0:P], AX.X, ALU.max))
                    chain(dve.tensor_tensor(m2[:, :], mcol[:, :], mrun[:, :], ALU.max))
                    chain(dve.tensor_scalar(dg[:, :], keep["ident"][0:HD, 0:HD], m2[:, 0:1], None, ALU.mult))
                    chain(dve.tensor_tensor(shrink[:, :], mrun[:, :], m2[:, :], ALU.subtract))
                    chain(dve.tensor_copy(mrun[:, :], m2[:, :]))
                    dve.wait_ge(mrow_full, n + 1)
                    chain(dve.tensor_tensor(wt[:, :, :], z[:, :, :], mrow[:, 0:HD].unsqueeze(1).to_broadcast([P, SLOTS, HD]),
                                            ALU.subtract))
                    dve.wait_ge(exp_done, n * 2 + 2)
                    for i, (a, w) in enumerate(HALF):
                        dve.wait_ge(num_full, n * 2 + i + 1)
                        chain(dve.scalar_tensor_tensor(out=acc[:, a:a + w], in0=acc[:, a:a + w], scalar=scale[:, 0:1],
                                                       in1=num[i][0:HD, 0:w], op0=ALU.mult, op1=ALU.add))

                def after(T, n):
                    dve.tensor_scalar(den[:, :], acc[:, D:D + 1], 1e-16, None, ALU.add).then_inc(end_step, 1)
                    dve.wait_ge(end_step, T * JE + 2)
                    dve.reciprocal(rden[:, :], den[:, :]).then_inc(end_step, 1)
                    dve.wait_ge(end_step, T * JE + 3)
                    dve.tensor_scalar(outb[:, :], acc[:, 0:D], rden[:, 0:1], None, ALU.mult).then_inc(end_step, 1)
                    dve.wait_ge(end_step, T * JE + 4)
                    if layer == 2:
                        dve.tensor_tensor(outb[:, :], outb[:, :], res[:, :], ALU.add).then_inc(end_step, 1)
                    else:
                        dve.tensor_copy(mcol[:, :], den[:, :]).then_inc(end_step, 1)
                groups(dve, before, group, after)

        @blk.scalar
        def _(act):
            with act.If(too_long(act)):
                def group(at, n, T):
                    act.wait_ge(group_step, n * KD + 13)
                    act.activation(scale[:, :], shrink[:, :], ACT.Exp).then_inc(exp_done, 1)
                    act.activation(wt[:, :, :].rearrange("p c n -> p (c n)"), wt[:, :, :].rearrange("p c n -> p (c n)"),
                                   ACT.Exp).then_inc(exp_done, 1)
                groups(act, lambda T: None, group, lambda T, n: None)

        @blk.tensor
        def _(pe):
            with pe.If(too_long(pe)):
                pe.wait_ge(ones_set, 1)

                def group(at, n, T):
                    pe.wait_ge(group_step, n * KD + 7)
                    pe.transpose(zt[0:HD, 0:P], zmax[:, :], keep["ident"][:, :]).then_inc(zt_full, 1)
                    pe.wait_ge(group_step, n * KD + 10)
                    pe.matmul(mrow[:, 0:HD], ones[0:HD, :], dg[:, :], start=True, stop=True).then_inc(mrow_full, 1)
                    pe.wait_ge(exp_done, n * 2 + 2)
                    for c in range(SLOTS):
                        for i, (a, w) in enumerate(HALF):
                            mm = pe.matmul(num[i][0:HD, 0:w], wt[:, c, :], rows[:, c, a:a + w], start=(c == 0),
                                           stop=(c == SLOTS - 1))
                            if c == SLOTS - 1:
                                mm.then_inc(num_full, 1)
                groups(pe, lambda T: None, group, lambda T, n: None)


def aggregate_one_head(nc, io, dram, keep):
    GR = P // TW
    S = GR * SLOTS
    HALF = ((0, 384), (384, D + 1 - 384))
    tab = dram["tab2"]
    with Pool(nc, "h") as s:
        ids, ones = s.sb("ids", [P, NP]), s.sb("ones", [P, P])
        e, rows = s.sb2("e", [P, 2, S], I32), s.sb2("rows", [P, S, TROW2])
        ald, own, resb = s.sb2("ald", [P, P]), s.sb2("own", [P, TROW2]), s.sb2("resb", [P, D])
        bias, other, z = s.sb("bias", [P, D]), s.sb("other", [P, S, TW]), s.sb("z", [P, S, TW])
        zmax, dg = s.sb("zmax", [P, P]), s.sb("dg", [P, P])
        mcol, zs, zself, m2, dself, den, rden = (s.sb(n, [P, 1]) for n in ("mcol", "zs", "zself", "m2", "dself", "den", "rden"))
        wt, wself = s.sb2("wt", [P, S, TW]), s.sb2("wself", [P, 1])
        acc, outb = s.sb("acc", [P, D + 1]), s.sb2("outb", [P, D])
        zt, mrow = s.bank("zt"), s.bank("mrow")
        num = [[s.bank(f"num{b}{i}") for i in range(2)] for b in range(2)]
        const_in = s.sem("const_in")
        e_in, ald_in, own_in, res_in, stored = (s.sem2(n) for n in ("e_in", "ald_in", "own_in", "res_in", "stored"))
        rows_in = keep["rows_in"][1]
        (ones_set, gather_go, other_done, z1_done, z2_done, z3_done, zmax_done, zt_full, mcol_done, zs_done,
         zself_done, m2_done, dg_done, dself_done, mrow_full, shift_done, wself_done, exp_done, num_full, acc_done,
         den_done, rden_done, out_done, resb_done) = (s.sem(n) for n in (
             "ones_set", "gather_go", "other_done", "z1_done", "z2_done", "z3_done", "zmax_done", "zt_full",
             "mcol_done", "zs_done", "zself_done", "m2_done", "dg_done", "dself_done", "mrow_full", "shift_done",
             "wself_done", "exp_done", "num_full", "acc_done", "den_done", "rden_done", "out_done", "resb_done"))
        blk = s.block()

        def fits(eng):
            return eng.value_load(keep["longest"][0:1, 0:1], min_val=0, max_val=2 * EP) <= CAP

        @blk.sync
        def _(sp):
            with sp.If(fits(sp)):
                sp.dma_start(ids[:, :], io["node_ids"].partition_broadcast(P)).then_inc(const_in, 16)
                sp.dma_start(bias[:, :], io["b2"].partition_broadcast(P)).then_inc(const_in, 16)

                def load(p, b, first, last):
                    t = p * 2 + b
                    r = sp.snap(t * P) if not first else t * P
                    for k in range(GR):
                        lo = sp.value_load(keep["ranges"][0:1, bass.ds(t * (2 * GR) + 2 * k, 1)], min_val=0, max_val=EP)
                        sp.dma_start(e[b][:, :, k * SLOTS:(k + 1) * SLOTS],
                                     io["edges"][:, bass.ds(lo, CAP)].rearrange("s (p c) -> p s c", c=SLOTS)).then_inc(e_in[b], 16)
                    sp.dma_start(ald[b][:, :], dram["ald2"][bass.ds(r, P), :].rearrange("d h -> (d h)").partition_broadcast(P)).then_inc(ald_in[b], 16)
                    sp.dma_start(own[b][:, :], tab[bass.ds(r, P), :]).then_inc(own_in[b], 16)
                    sp.dma_start(resb[b][:, :], dram["res"][bass.ds(r, P), :]).then_inc(res_in[b], 16)

                def store(p, b, first, last):
                    t = p * 2 + b
                    r = sp.snap(t * P) if not first else t * P
                    sp.wait_ge(out_done, t + 1)
                    sp.dma_start(dram["x2"][bass.ds(r, P), :], outb[b][:, :]).then_inc(stored[b], 16)
                loads_ahead(sp, load, store)
                sp.wait_ge(stored[0], 16 * (NT - NT // 2))
                sp.wait_ge(stored[1], 16 * (NT // 2))

        @blk.gpsimd
        def _(pool):
            with pool.If(fits(pool)):
                pool.memset(ones[:, :], 1.0).then_inc(ones_set, 1)

                def step(p, b, first, last):
                    pool.wait_ge(e_in[b], p * (16 * GR) + 16 * GR)
                    pool.sem_inc(gather_go, 1)
                    for c in range(S):
                        pool.indirect_dma_start(rows[b][:, c, :], None, tab,
                                                bass.IndirectOffsetOnAxis(ap=e[b][:, 0, c:c + 1], axis=0)).then_inc(rows_in[b], 16)
                tile_pairs(pool, step)

        @blk.vector
        def _(dve):
            with dve.If(fits(dve)):
                dve.wait_ge(const_in, 32)

                def split4(ap):
                    return ap.rearrange("p (k c) d -> p k c d", k=GR)

                def weights(p, b, first):
                    t = p * 2 + b
                    dve.wait_ge(e_in[b], p * (16 * GR) + 16 * GR)
                    dve.wait_ge(z1_done, t)
                    dve.tensor_tensor(split4(other[:, :, :]),
                                      e[b][:, 1, :].rearrange("p (k c) -> p k c", k=GR).unsqueeze(3).to_broadcast([P, GR, SLOTS, TW]),
                                      ids[:, bass.ds(t * P, P)].rearrange("p (k d) -> p k d", k=GR).unsqueeze(2)
                                      .to_broadcast([P, GR, SLOTS, TW]), ALU.not_equal).then_inc(other_done, 1)
                    dve.wait_ge(own_in[b], p * 16 + 16)
                    dve.wait_ge(zself_done, t)
                    dve.tensor_tensor(zs[:, :], own[b][:, D + 1:D + 2], own[b][:, D + 2:D + 3], ALU.add).then_inc(zs_done, 1)
                    dve.wait_ge(zs_done, t + 1)
                    dve.wait_ge(dself_done, t)
                    dve.scalar_tensor_tensor(out=zself[:, :], in0=zs[:, :], scalar=SLOPE, in1=zs[:, :], op0=ALU.mult,
                                             op1=ALU.max).then_inc(zself_done, 1)
                    dve.wait_ge(rows_in[b], p * (16 * S) + 16 * S)
                    dve.wait_ge(ald_in[b], p * 16 + 16)
                    dve.wait_ge(other_done, t + 1)
                    dve.wait_ge(shift_done, t)
                    dve.scalar_tensor_tensor(out=z[:, :, :], in0=other[:, :, :], scalar=-BIG,
                                             in1=rows[b][:, :, D + 1:D + 2].to_broadcast([P, S, TW]), op0=ALU.mult,
                                             op1=ALU.add).then_inc(z1_done, 1)
                    dve.wait_ge(z1_done, t + 1)
                    dve.tensor_tensor(split4(z[:, :, :]), split4(z[:, :, :]),
                                      ald[b][:, :].rearrange("p (k d) -> p k d", k=GR).unsqueeze(2)
                                      .to_broadcast([P, GR, SLOTS, TW]), ALU.add).then_inc(z2_done, 1)
                    dve.wait_ge(z2_done, t + 1)
                    zf = z[:, :, :].rearrange("p c n -> p (c n)")
                    dve.scalar_tensor_tensor(out=zf, in0=zf, scalar=SLOPE, in1=zf, op0=ALU.mult, op1=ALU.max).then_inc(z3_done, 1)
                    dve.wait_ge(z3_done, t + 1)
                    dve.wait_ge(zt_full, t)
                    dve.tensor_reduce(zmax[:, :].rearrange("p (k d) -> p k d", k=GR),
                                      split4(z[:, :, :]).rearrange("p k c d -> p k d c"), AX.X, ALU.max).then_inc(zmax_done, 1)
                    dve.wait_ge(zt_full, t + 1)
                    dve.tensor_reduce(mcol[:, :], zt[:, 0:P], AX.X, ALU.max).then_inc(mcol_done, 1)
                    dve.wait_ge(mcol_done, t + 1)
                    dve.wait_ge(zself_done, t + 1)
                    dve.wait_ge(dg_done, t)
                    dve.tensor_tensor(m2[:, :], mcol[:, :], zself[:, :], ALU.max).then_inc(m2_done, 1)
                    dve.wait_ge(m2_done, t + 1)
                    dve.wait_ge(mrow_full, t)
                    dve.tensor_scalar(dg[:, :], keep["ident"][:, :], m2[:, 0:1], None, ALU.mult).then_inc(dg_done, 1)
                    dve.wait_ge(wself_done, t)
                    dve.tensor_tensor(dself[:, :], zself[:, :], m2[:, :], ALU.subtract).then_inc(dself_done, 1)
                    dve.wait_ge(mrow_full, t + 1)
                    if not first:
                        dve.wait_ge(num_full, t * 2 - 2)
                    dve.tensor_tensor(split4(wt[b][:, :, :]), split4(z[:, :, :]),
                                      mrow[:, 0:P].rearrange("p (k d) -> p k d", k=GR).unsqueeze(2)
                                      .to_broadcast([P, GR, SLOTS, TW]), ALU.subtract).then_inc(shift_done, 1)

                def sums(p, b, first):
                    t = p * 2 + b
                    dve.wait_ge(res_in[b], p * 16 + 16)
                    dve.tensor_tensor(resb[b][:, :], resb[b][:, :], bias[:, :], ALU.add).then_inc(resb_done, 1)
                    dve.wait_ge(wself_done, t + 1)
                    dve.wait_ge(out_done, t)
                    for i, (a, n) in enumerate(HALF):
                        dve.wait_ge(num_full, t * 2 + i + 1)
                        dve.scalar_tensor_tensor(out=acc[:, a:a + n], in0=own[b][:, a:a + n], scalar=wself[b][:, 0:1],
                                                 in1=num[b][i][:, 0:n], op0=ALU.mult, op1=ALU.add).then_inc(acc_done, 1)
                    dve.wait_ge(acc_done, t * 2 + 2)
                    dve.tensor_scalar(den[:, :], acc[:, D:D + 1], 1e-16, None, ALU.add).then_inc(den_done, 1)
                    dve.wait_ge(den_done, t + 1)
                    dve.reciprocal(rden[:, :], den[:, :]).then_inc(rden_done, 1)
                    dve.wait_ge(rden_done, t + 1)
                    dve.wait_ge(resb_done, t + 1)
                    if not first:
                        dve.wait_ge(stored[b], p * 16)
                    dve.scalar_tensor_tensor(out=outb[b][:, :], in0=acc[:, 0:D], scalar=rden[:, 0:1], in1=resb[b][:, :],
                                             op0=ALU.mult, op1=ALU.add).then_inc(out_done, 1)

                def step(p, b, first, last):
                    weights(p, b, first)
                    sums(p, b, first)
                tile_pairs(dve, step)

        @blk.scalar
        def _(act):
            with act.If(fits(act)):
                def step(p, b, first, last):
                    t = p * 2 + b
                    act.wait_ge(dself_done, t + 1)
                    if not first:
                        act.wait_ge(acc_done, t * 2 - 2)
                    act.activation(wself[b][:, :], dself[:, :], ACT.Exp).then_inc(wself_done, 1)
                    act.wait_ge(shift_done, t + 1)
                    wf = wt[b][:, :, :].rearrange("p c n -> p (c n)")
                    act.activation(wf, wf, ACT.Exp).then_inc(exp_done, 1)
                tile_pairs(act, step)

        @blk.tensor
        def _(pe):
            with pe.If(fits(pe)):
                pe.wait_ge(ones_set, 1)

                def step(p, b, first, last):
                    t = p * 2 + b
                    pe.wait_ge(zmax_done, t + 1)
                    pe.transpose(zt[:, 0:P], zmax[:, :], keep["ident"][:, :]).then_inc(zt_full, 1)
                    pe.wait_ge(dg_done, t + 1)
                    pe.matmul(mrow[:, 0:P], ones[:, :], dg[:, :], start=True, stop=True).then_inc(mrow_full, 1)
                    pe.wait_ge(exp_done, t + 1)
                    if not first:
                        pe.wait_ge(acc_done, t * 2 - 2)
                    for i, (a, n) in enumerate(HALF):
                        for c in range(SLOTS):
                            for k in range(GR):
                                mm = pe.matmul(num[b][i][k * TW:(k + 1) * TW, 0:n], wt[b][:, k * SLOTS + c, :],
                                               rows[b][:, k * SLOTS + c, a:a + n], start=(c == 0), stop=(c == SLOTS - 1),
                                               tile_position=(0, k * TW), skip_group_check=True)
                        mm.then_inc(num_full, 1)
                tile_pairs(pe, step)


def phase_i(nc, io, dram, keep, out):
    EH = NEXP * DHID
    NK = EH // P
    with Pool(nc, "i") as s:
        u_hi, u_lo = s.sb("u_hi", [P, KC, EH], F32R), s.sb("u_lo", [P, KC, EH], F32R)
        w_hi, w_lo = s.sb("w_hi", [P, NK, D], F32R), s.sb("w_lo", [P, NK, D], F32R)
        r_hi, r_lo = s.sb("r_hi", [P, KC, NEXP], F32R), s.sb("r_lo", [P, KC, NEXP], F32R)
        split_weights(nc, "is", [(io["eW1"][k * P:(k + 1) * P, :], u_hi[:, k, :], u_lo[:, k, :]) for k in range(KC)]
                      + [(io["eW2"][k * P:(k + 1) * P, :], w_hi[:, k, :], w_lo[:, k, :]) for k in range(NK)]
                      + [(io["Wr"][k * P:(k + 1) * P, :], r_hi[:, k, :], r_lo[:, k, :]) for k in range(KC)], EH)
        ident = keep["ident"]
        x, xs = s.sb2("x", [P, D]), s.sb2("xs", [P, D])
        xn = s.sb("xn", [P, D])
        xt_h, xt_l = s.sb2("xt_h", [P, KC, P], F32R), s.sb2("xt_l", [P, KC, P], F32R)
        hid = s.sb("hid", [P, EH])
        ht_h, ht_l = s.sb("ht_h", [P, NK, P], F32R), s.sb("ht_l", [P, NK, P], F32R)
        y = xn
        b1, b2 = s.sb("b1", [P, EH]), s.sb("b2", [NEXP, D])
        gain, shift = s.sb("gain", [P, D]), s.sb("shift", [P, D])
        br, ramp = s.sb("br", [P, NEXP]), s.sb("ramp", [P, NEXP])
        st, mv, vps, rstd = s.sb("st", [P, 2, 6]), s.sb("mv", [P, 2]), s.sb("vps", [P, 1]), s.sb("rstd", [P, 1])
        yst, ymv, yvps, yrstd = s.sb("yst", [P, 2, 6]), s.sb("ymv", [P, 2]), s.sb("yvps", [P, 1]), s.sb("yrstd", [P, 1])
        lg, hot = s.sb("lg", [P, NEXP]), s.sb("hot", [P, 2, NEXP])
        score, rest, ex, ew = (s.sb(n, [P, NEXP]) for n in ("score", "rest", "ex", "ew"))
        top, best, negm, den, rden = (s.sb(n, [P, 1]) for n in ("top", "best", "negm", "den", "rden"))
        ewt = s.sb("ewt", [NEXP, P])
        turn = [s.bank(f"turn{i}") for i in range(2)]
        log_b, ewt_b = s.bank("log_b"), s.bank("ewt_b")
        up = [s.bank(f"up{i}") for i in range(2)]
        down = [s.bank(f"down{i}") for i in range(2)]
        c_in, x_in, out_sem = s.sem("c_in"), s.sem2("x_in"), s.sem2("out")
        (stats_done, stats_seen, mean_done, vps_done, rstd_done, xn_done, turn_full, hi_done, lo_done, log_full, route_step, ew_steps,
         exp_done, ew_done, ewt_full, ewt_done, up_full, biased, gelu_done, scaled, ht_full, hth_done, htl_done, down_full,
         y_done, ystats_done, ystats_seen, ymean_done, yvps_done, yrstd_done, gain_done, sum_done, xs_done) = (
            s.sem(n) for n in (
                "stats_done", "stats_seen", "mean_done", "vps_done", "rstd_done", "xn_done", "turn_full", "hi_done",
                "lo_done", "log_full", "route_step", "ew_steps", "exp_done", "ew_done", "ewt_full", "ewt_done", "up_full", "biased",
                "gelu_done", "scaled", "ht_full", "hth_done", "htl_done", "down_full", "y_done", "ystats_done",
                "ystats_seen", "ymean_done", "yvps_done", "yrstd_done", "gain_done", "sum_done", "xs_done"))
        blk = s.block()
        RSTEPS = 11

        @blk.sync
        def _(sp):
            for dst_, src_ in ((b1, "eb1"), (gain, "ln_g"), (shift, "ln_b"), (br, "br"), (ramp, "expert_ramp")):
                sp.dma_start(dst_[:, :], io[src_].partition_broadcast(P)).then_inc(c_in, 16)
            sp.dma_start(b2[:, :], io["eb2"]).then_inc(c_in, 16)

            def load(p, b, first, last):
                t = p * 2 + b
                r = sp.snap(t * P) if not first else t * P
                rows = LAST if last else P
                if not first:
                    sp.wait_ge(xs_done, t - 1)
                    sp.wait_ge(xn_done, t - 1)
                sp.dma_start(x[b][0:rows, :], dram["x2"][bass.ds(r, rows), :]).then_inc(x_in[b], 16)

            def store(p, b, first, last):
                t = p * 2 + b
                r = sp.snap(t * P) if not first else t * P
                rows = LAST if last else P
                sp.wait_ge(sum_done, t + 1)
                sp.dma_start(out[bass.ds(r, rows), :], xs[b][0:rows, :]).then_inc(out_sem[b], 16)
            loads_first(sp, load, store)
            sp.wait_ge(out_sem[0], 16 * (NT - NT // 2))
            sp.wait_ge(out_sem[1], 16 * (NT // 2))

        @blk.gpsimd
        def _(pool):
            pool.wait_ge(c_in, 16 * 6)

            def shifted(t, b, first):
                layernorm_rstd(pool, mv, vps, rstd, keep["ln_eps"], keep["minus_half"], mean_done, vps_done, rstd_done, t)
                if not first:
                    pool.wait_ge(out_sem[b], t * 8 - 8 * b)
                pool.tensor_tensor(xs[b][:, :], x[b][:, :], shift[:, :], ALU.add).then_inc(xs_done, 1)

            shifted(0, 0, True)

            def step(p, b, first, last):
                t = p * 2 + b
                if not last:
                    shifted(t + 1, 1 - b, first and b == 0)
                layernorm_rstd(pool, ymv, yvps, yrstd, keep["ln_eps"], keep["minus_half"], ymean_done, yvps_done, yrstd_done, t)
            tile_pairs(pool, step)

        @blk.scalar
        def _(act):
            def high(t, b, g, first):
                act.wait_ge(turn_full, t * 2 + g + 1)
                if g == 0 and not first:
                    act.wait_ge(up_full, t * 4 - 4)
                act.activation(xt_h[b][:, 3 * g:3 * g + 3, :].rearrange("p k n -> p (k n)"), turn[g][:, 0:384],
                               ACT.Copy).then_inc(hi_done, 1)

            high(0, 0, 0, True)
            high(0, 0, 1, True)

            def step(p, b, first, last):
                t = p * 2 + b
                act.wait_ge(route_step, t * RSTEPS + 3)
                act.activation(ex[:, :], lg[:, :], ACT.Exp, bias=negm[:, 0:1]).then_inc(exp_done, 1)
                if not last:
                    high(t + 1, 1 - b, 0, first and b == 0)
                    high(t + 1, 1 - b, 1, first and b == 0)

                def gelu(c):
                    act.wait_ge(biased, t * 4 + c + 1)
                    act.activation(hid[:, 384 * c:384 * c + 384], hid[:, 384 * c:384 * c + 384],
                                   ACT.Gelu_apprx_tanh).then_inc(gelu_done, 1)

                def hidden_high(g):
                    act.wait_ge(ht_full, t * 4 + g + 1)
                    act.activation(ht_h[:, 3 * g:3 * g + 3, :].rearrange("p k n -> p (k n)"), turn[g % 2][:, 0:384],
                                   ACT.Copy).then_inc(hth_done, 1)

                for c in range(3):
                    gelu(c)
                act.wait_ge(down_full, t * 2)
                hidden_high(0)
                hidden_high(1)
                gelu(3)
                hidden_high(2)
                hidden_high(3)
                act.wait_ge(sum_done, t)
                act.wait_ge(turn_full, t * 2 + (2 if last else 4))
                for c in range(2):
                    act.wait_ge(down_full, t * 2 + c + 1)
                    act.activation(y[:, 384 * c:384 * c + 384], down[c][:, 0:384], ACT.Copy).then_inc(y_done, 1)
            tile_pairs(act, step)

        @blk.vector
        def _(dve):
            dve.wait_ge(c_in, 16 * 6)

            def norm_stats(t, b):
                dve.wait_ge(x_in[b], t * 8 + (16 - 8 * b))
                dve.wait_ge(rstd_done, t)
                layernorm_stats(dve, x[b], st, mv, stats_done, stats_seen, mean_done, t)

            def normalise(t, b):
                dve.wait_ge(rstd_done, t + 1)
                dve.wait_ge(turn_full, t * 2)
                if not (isinstance(t, int) and t < 2):
                    dve.wait_ge(sum_done, t - 1)
                dve.tensor_scalar(xn[:, :], x[b][:, :], mv[:, 0:1], rstd[:, 0:1], ALU.subtract, ALU.mult).then_inc(xn_done, 1)

            def low(t, b):
                for g in range(2):
                    dve.wait_ge(hi_done, t * 2 + g + 1)
                    o = xt_h[b][:, 3 * g:3 * g + 3, :].rearrange("p k n -> p (k n)")
                    dve.tensor_tensor(xt_l[b][:, 3 * g:3 * g + 3, :].rearrange("p k n -> p (k n)"), turn[g][:, 0:384],
                                      o.bitcast(F32), ALU.subtract).then_inc(lo_done, 1)

            def route(t):
                n = [t * RSTEPS]

                def chain(ins):
                    ins.then_inc(route_step, 1)
                    n[0] = n[0] + 1
                    dve.wait_ge(route_step, n[0])

                dve.wait_ge(log_full, t + 1)
                dve.wait_ge(ew_done, t)
                chain(dve.tensor_tensor(lg[:, :], log_b[:, 0:NEXP], br[:, :], ALU.add))
                for i, src_ in enumerate((lg, rest)):
                    chain(dve.tensor_reduce(top[:, :], src_[:, :], AX.X, ALU.max))
                    if i == 0:
                        chain(dve.tensor_scalar(negm[:, :], top[:, :], -1.0, None, ALU.mult))
                    chain(dve.scalar_tensor_tensor(out=score[:, :], in0=src_[:, :], scalar=top[:, 0:1], in1=ramp[:, :],
                                                   op0=ALU.is_equal, op1=ALU.mult))
                    chain(dve.tensor_reduce(best[:, :], score[:, :], AX.X, ALU.max))
                    chain(dve.tensor_scalar(hot[:, i, :], score[:, :], best[:, 0:1], None, ALU.is_equal))
                    if i == 0:
                        chain(dve.scalar_tensor_tensor(out=rest[:, :], in0=hot[:, 0, :], scalar=-BIG, in1=lg[:, :],
                                                       op0=ALU.mult, op1=ALU.add))

            def route_end(t):
                dve.wait_ge(exp_done, t + 1)
                dve.tensor_tensor(hot[:, 0, :], hot[:, 0, :], hot[:, 1, :], ALU.add).then_inc(ew_steps, 1)
                dve.wait_ge(ew_steps, t * 4 + 1)
                dve.tensor_tensor(ex[:, :], ex[:, :], hot[:, 0, :], ALU.mult).then_inc(ew_steps, 1)
                dve.wait_ge(ew_steps, t * 4 + 2)
                dve.tensor_reduce(den[:, :], ex[:, :], AX.X, ALU.add).then_inc(ew_steps, 1)
                dve.wait_ge(ew_steps, t * 4 + 3)
                dve.reciprocal(rden[:, :], den[:, :]).then_inc(ew_steps, 1)
                dve.wait_ge(ew_steps, t * 4 + 4)
                dve.wait_ge(scaled, t * 4)
                dve.wait_ge(ewt_full, t)
                dve.tensor_scalar(ew[:, :], ex[:, :], rden[:, 0:1], None, ALU.mult).then_inc(ew_done, 1)

            def route_turned(t):
                dve.wait_ge(ewt_full, t + 1)
                dve.wait_ge(down_full, t * 2)
                dve.tensor_copy(ewt[:, :], ewt_b[0:NEXP, 0:P]).then_inc(ewt_done, 1)

            def add_bias(t, c):
                dve.wait_ge(up_full, t * 4 + c + 1)
                if c == 0:
                    dve.wait_ge(ht_full, t * 4)
                o = slice(384 * c, 384 * c + 384)
                dve.tensor_tensor(hid[:, o], up[c % 2][:, 0:384], b1[:, o], ALU.add).then_inc(biased, 1)

            def scale(t, c):
                dve.wait_ge(gelu_done, t * 4 + c + 1)
                dve.wait_ge(ew_done, t + 1)
                v = hid[:, 384 * c:384 * c + 384].rearrange("p (e j) -> p e j", j=DHID)
                dve.tensor_tensor(v, v, ew[:, 2 * c:2 * c + 2].unsqueeze(2).to_broadcast([P, 2, DHID]), ALU.mult).then_inc(scaled, 1)

            def hid_low(t, g):
                dve.wait_ge(hth_done, t * 4 + g + 1)
                o = ht_h[:, 3 * g:3 * g + 3, :].rearrange("p k n -> p (k n)")
                dve.tensor_tensor(ht_l[:, 3 * g:3 * g + 3, :].rearrange("p k n -> p (k n)"), turn[g % 2][:, 0:384],
                                  o.bitcast(F32), ALU.subtract).then_inc(htl_done, 1)

            def finish(t, b):
                dve.wait_ge(y_done, t * 2 + 2)
                dve.wait_ge(yrstd_done, t)
                layernorm_stats(dve, y, yst, ymv, ystats_done, ystats_seen, ymean_done, t)
                dve.wait_ge(ymean_done, t + 1)
                dve.scalar_tensor_tensor(out=y[:, :], in0=y[:, :], scalar=ymv[:, 0:1], in1=gain[:, :], op0=ALU.subtract,
                                         op1=ALU.mult).then_inc(gain_done, 1)
                dve.wait_ge(gain_done, t + 1)
                dve.wait_ge(yrstd_done, t + 1)
                dve.wait_ge(xs_done, t + 1)
                dve.scalar_tensor_tensor(out=xs[b][:, :], in0=y[:, :], scalar=yrstd[:, 0:1], in1=xs[b][:, :], op0=ALU.mult,
                                         op1=ALU.add).then_inc(sum_done, 1)

            norm_stats(0, 0)
            normalise(0, 0)
            low(0, 0)

            def step(p, b, first, last):
                t = p * 2 + b
                if not last:
                    norm_stats(t + 1, 1 - b)
                add_bias(t, 0)
                if not last:
                    normalise(t + 1, 1 - b)
                add_bias(t, 1)
                route(t)
                if not last:
                    low(t + 1, 1 - b)
                route_end(t)
                scale(t, 0)
                scale(t, 1)
                add_bias(t, 2)
                scale(t, 2)
                add_bias(t, 3)
                route_turned(t)
                hid_low(t, 0)
                hid_low(t, 1)
                scale(t, 3)
                hid_low(t, 2)
                hid_low(t, 3)
                finish(t, b)
            tile_pairs(dve, step)

        @blk.tensor
        def _(pe):
            def x_turns(t):
                pe.wait_ge(xn_done, t + 1)
                for g in range(2):
                    if not (isinstance(t, int) and t < 2):
                        pe.wait_ge(htl_done, t * 4 - 5 + g)
                    for i in range(3):
                        k = 3 * g + i
                        mm = pe.transpose(turn[g][:, i * P:(i + 1) * P], xn[:, k * P:(k + 1) * P], ident[:, :])
                    mm.then_inc(turn_full, 1)

            ks = range(KC)

            def logits(t, b):
                pe.wait_ge(lo_done, t * 2 + 2)
                pe.wait_ge(route_step, t * RSTEPS)
                product3(pe, log_b[:, 0:NEXP], [xt_h[b][:, k, :] for k in ks], [xt_l[b][:, k, :] for k in ks],
                         [r_hi[:, k, :] for k in ks], [r_lo[:, k, :] for k in ks]).then_inc(log_full, 1)

            x_turns(0)
            logits(0, 0)

            def step(p, b, first, last):
                t = p * 2 + b
                xh, xl = [xt_h[b][:, k, :] for k in ks], [xt_l[b][:, k, :] for k in ks]
                def up_product(c):
                    if not (first and b == 0 and c < 2):
                        pe.wait_ge(biased, t * 4 + c - 1)
                    o = slice(384 * c, 384 * c + 384)
                    product3(pe, up[c % 2][:, 0:384], xh, xl, [u_hi[:, k, o] for k in ks], [u_lo[:, k, o] for k in ks]).then_inc(up_full, 1)

                def hidden_turns(g):
                    pe.wait_ge(scaled, t * 4 + g + 1)
                    if g >= 2:
                        pe.wait_ge(htl_done, t * 4 + g - 1)
                    elif not last:
                        pe.wait_ge(lo_done, t * 2 + g + 3)
                    elif g < 2:
                        pe.wait_ge(lo_done, t * 2 + g + 1)
                    for i in range(3):
                        k = 3 * g + i
                        mm = pe.transpose(turn[g % 2][:, i * P:(i + 1) * P], hid[:, k * P:(k + 1) * P], ident[:, :])
                    mm.then_inc(ht_full, 1)

                def down_product(c, g):
                    if c == 0:
                        pe.wait_ge(htl_done, t * 4 + g + 1)
                    if g == 0 and not (first and b == 0):
                        pe.wait_ge(y_done, t * 2 + c - 1)
                    o = slice(384 * c, 384 * c + 384)
                    for k in range(3 * g, 3 * g + 3):
                        pe.matmul(down[c][:, 0:384], ht_h[:, k, :], w_hi[:, k, o], start=(k == 0), stop=False, skip_group_check=True)
                        pe.matmul(down[c][:, 0:384], ht_h[:, k, :], w_lo[:, k, o], start=False, stop=False, skip_group_check=True)
                        pe.matmul(down[c][:, 0:384], ht_l[:, k, :], w_hi[:, k, o], start=False, stop=False, skip_group_check=True)
                    if g == 3:
                        pe.wait_ge(ewt_done, t + 1)
                        pe.matmul(down[c][:, 0:384], ewt[:, :], b2[:, o], start=False, stop=True,
                                  skip_group_check=True).then_inc(down_full, 1)

                up_product(0)
                up_product(1)
                up_product(2)
                if not last:
                    x_turns(t + 1)
                up_product(3)
                pe.wait_ge(ew_done, t + 1)
                pe.wait_ge(ewt_done, t)
                pe.transpose(ewt_b[0:NEXP, 0:P], ew[:, :], ident[:, :]).then_inc(ewt_full, 1)
                hidden_turns(0)
                hidden_turns(1)
                if not last:
                    logits(t + 1, 1 - b)
                down_product(0, 0)
                hidden_turns(2)
                down_product(0, 1)
                hidden_turns(3)
                down_product(0, 2)
                down_product(0, 3)
                for g in range(4):
                    down_product(1, g)
            tile_pairs(pe, step)


def build(nc, io, out):
    def scratch(name, shape):
        return nc.dram_tensor(name, shape, F32).ap()

    dram = {
        "tab1": scratch("tab1", (NP, TROW1)), "ald1": scratch("ald1", (NP, GH)), "vx": scratch("vx", (NP, HEADS * VW)),
        "res": scratch("res", (NP, D)), "agg1": scratch("agg1", (GH, NP, D)), "h1": scratch("h1", (NP, HID)),
        "tab2": scratch("tab2", (NP, TROW2)), "ald2": scratch("ald2", (NP, 1)), "x2": scratch("x2", (NP, D)),
    }
    dram["blocks"], dram["spans"] = scratch("blocks", (2, EP // BLOCK)), scratch("spans", (P,))
    dram["ranges"] = nc.dram_tensor("ranges", (P, 2), I32).ap()
    for n in ("qt_h", "qt_l", "kt_h", "kt_l"):
        dram[n] = scratch(n, (NT, P, D))
    keep = {}
    with Pool(nc, "keep") as s:
        setup(nc, io, keep, s)
        with Pool(nc, "mix") as m:
            setup_mix(nc, io, keep, m)
            phase_a(nc, io, dram, keep)
            global_key_max(nc, keep)
            phase_b(nc, io, dram, keep)
            phase_c(nc, io, dram, keep)
        aggregate_four_heads(nc, io, dram, keep)
        aggregate_general(nc, io, dram, keep, 1)
        phase_f(nc, io, dram, keep)
        phase_g(nc, io, dram, keep)
        aggregate_one_head(nc, io, dram, keep)
        aggregate_general(nc, io, dram, keep, 2)
        phase_i(nc, io, dram, keep, out)




def kernel(x, src, dst, L0_gnn_W1, L0_gnn_att_src1, L0_gnn_att_dst1, L0_gnn_b1, L0_gnn_W2, L0_gnn_att_src2,
           L0_gnn_att_dst2, L0_gnn_b2, L0_mix_w_qkv, L0_mix_w_proj, L0_mix_b_proj, L0_mix_proj_mat, L0_ffn_Wr,
           L0_ffn_br, L0_ffn_W1, L0_ffn_b1, L0_ffn_W2, L0_ffn_b2, L0_ffn_ln_g, L0_ffn_ln_b):
    import numpy as np
    from concourse import bacc
    from concourse.bass_utils import run_bass_kernel_spmd

    arrays = host_arrays(x, src, dst, L0_gnn_W1, L0_gnn_att_src1, L0_gnn_att_dst1, L0_gnn_b1, L0_gnn_W2,
                         L0_gnn_att_src2, L0_gnn_att_dst2, L0_gnn_b2, L0_mix_w_qkv, L0_mix_w_proj, L0_mix_b_proj,
                         L0_mix_proj_mat, L0_ffn_Wr, L0_ffn_br, L0_ffn_W1, L0_ffn_b1, L0_ffn_W2, L0_ffn_b2,
                         L0_ffn_ln_g, L0_ffn_ln_b)
    nc = bacc.Bacc("TRN2", target_bir_lowering=False, num_devices=1)
    io = {n: nc.dram_tensor(f"in_{n}", a.shape, mybir.dt.from_np(a.dtype), kind="ExternalInput").ap()
          for n, a in arrays.items()}
    out = nc.dram_tensor("out", (N, D), F32, kind="ExternalOutput").ap()
    build(nc, io, out)
    r = run_bass_kernel_spmd(nc, [{f"in_{n}": a for n, a in arrays.items()}], core_ids=[0])
    return r.results[0]["out"]


def host_arrays(x, src, dst, W1, asrc1, adst1, b1, W2, asrc2, adst2, b2, w_qkv, w_proj, b_proj, proj_mat, Wr, br,
                eW1, eb1, eW2, eb2, ln_g, ln_b):
    import numpy as np

    def lay(a):
        return np.ascontiguousarray(a)

    xp = np.zeros((NP, D), np.asarray(x).dtype)
    xp[:N] = np.asarray(x)
    edges = np.zeros((2, EROOM), np.int32)
    edges[1] = 8192
    edges[0, :len(src)] = np.asarray(src)
    edges[1, :len(dst)] = np.asarray(dst)
    blocks = EP // BLOCK
    return {
        "x": xp, "edges": edges, "W1": lay(W1), "asrc1": lay(asrc1).reshape(-1), "adst1": lay(adst1).reshape(-1),
        "b1": lay(b1), "W2": lay(W2), "asrc2": lay(asrc2).reshape(-1), "adst2": lay(adst2).reshape(-1), "b2": lay(b2),
        "wqkvT": lay(np.asarray(w_qkv).T), "wprojT": lay(np.asarray(w_proj).T), "bproj": lay(b_proj),
        "projT": lay(np.asarray(proj_mat).T), "Wr": lay(Wr), "br": lay(br),
        "eW1": lay(np.asarray(eW1).transpose(1, 0, 2).reshape(D, NEXP * DHID)), "eb1": lay(eb1).reshape(-1),
        "eW2": lay(np.asarray(eW2).reshape(NEXP * DHID, D)), "eb2": lay(eb2), "ln_g": lay(ln_g), "ln_b": lay(ln_b),
        "ident": np.eye(P, dtype=np.float32),
        "node_ids": np.arange(NP, dtype=np.float32),
        "steps": np.arange(P, dtype=np.float32).reshape(P, 1),
        "block_ramps": np.stack([np.arange(blocks, 0, -1), np.arange(1, blocks + 1)]).astype(np.float32),
        "head_pick": np.tile(np.kron(np.eye(GH), np.ones((TW, 1))), (1, 2)).astype(np.float32),
        "expert_ramp": np.arange(NEXP, 0, -1).astype(np.float32),
    }
```
